# Optimizing a Trainium2 kernel written in Bass

```python
import numpy as np
import jax
import jax.numpy as jnp

def _softmax(x, axis=-1):
    return jax.nn.softmax(x, axis=axis)

def _gelu(x):
    return jax.nn.gelu(x, approximate=True)

def _silu(x):
    return jax.nn.silu(x)

def _sigmoid(x):
    return jax.nn.sigmoid(x)

def _layernorm(x, axis=-1, eps=1e-05):
    m = jnp.mean(x, axis=axis, keepdims=True)
    v = jnp.var(x, axis=axis, keepdims=True)
    return (x - m) / jnp.sqrt(v + eps)

def _scatter_add(tgt, idx, src, axis=0):
    return tgt.at[idx].add(src)

def _segment_sum(src, seg, n):
    return jax.ops.segment_sum(src, seg, n)
kernel_name = 'mk_lm_tower_d2_tok_ids256_r4_27cbf0'

def setup_inputs(seed: int=0):
    np.random.seed(seed)
    _w = jnp.asarray

    def _rec_inputs():
        import jax
        import jax.numpy as jnp
        _rk = jax.random.key(seed)
        x = jax.random.randint(jax.random.fold_in(_rk, 1), (64, 256), 0, 64, jnp.int32)
        return x
    x = _rec_inputs()

    def _L0_tok_setup():
        import jax, jax.numpy as jnp
        import numpy as np
        PRIME = 31
        VOCAB = 125000
        NGRAM_SIZES = (2, 3, 4)

        def _ngram_hash(byte_ids, n):
            T = byte_ids.shape[1]
            powers = PRIME ** jnp.arange(n - 1, -1, -1, dtype=jnp.int64) % VOCAB
            windows = jnp.stack([byte_ids[:, i:T - n + 1 + i] for i in range(n)], axis=-1)
            return (windows.astype(jnp.int64) * powers).sum(axis=-1) % VOCAB
        key = jax.random.key(seed)
        k0, k1, k2, k3 = jax.random.split(key, 4)
        byte_ids = jax.random.randint(k0, (8, 1024), 0, 64, dtype=jnp.int64)
        emb_2 = jax.random.normal(k1, (VOCAB, 64), dtype=jnp.float32)
        emb_3 = jax.random.normal(k2, (VOCAB, 64), dtype=jnp.float32)
        emb_4 = jax.random.normal(k3, (VOCAB, 64), dtype=jnp.float32)
        return {'byte_ids': byte_ids, 'emb_2': emb_2, 'emb_3': emb_3, 'emb_4': emb_4}
    _L0_tok_all = _L0_tok_setup()
    _L0_tok_in = {k: v for k, v in _L0_tok_all.items() if k in ('emb_2', 'emb_3', 'emb_4')}
    del _L0_tok_all

    def _L0_attn_setup():
        import jax, jax.numpy as jnp
        import numpy as np
        import math
        N_SEQ, L_RES, D_MODEL = (128, 96, 64)
        N_HEAD, C_HEAD = (8, 32)
        EPS = 1e-05
        key = jax.random.key(seed)
        ks = jax.random.split(key, 8)
        s = 1.0 / math.sqrt(D_MODEL)
        return {'m': jax.random.normal(ks[0], (N_SEQ, L_RES, D_MODEL), jnp.float32), 'gamma': jnp.ones((D_MODEL,), jnp.float32), 'beta': jnp.zeros((D_MODEL,), jnp.float32), 'Wq': jax.random.normal(ks[1], (D_MODEL, N_HEAD * C_HEAD), jnp.float32) * s, 'Wk': jax.random.normal(ks[2], (D_MODEL, N_HEAD * C_HEAD), jnp.float32) * s, 'Wv': jax.random.normal(ks[3], (D_MODEL, N_HEAD * C_HEAD), jnp.float32) * s, 'Wg': jax.random.normal(ks[4], (D_MODEL, N_HEAD * C_HEAD), jnp.float32) * s, 'bg': jnp.zeros((N_HEAD * C_HEAD,), jnp.float32), 'Wo': jax.random.normal(ks[5], (N_HEAD * C_HEAD, D_MODEL), jnp.float32) * s, 'bo': jnp.zeros((D_MODEL,), jnp.float32)}
    _L0_attn_all = _L0_attn_setup()
    _L0_attn_in = {k: v for k, v in _L0_attn_all.items() if k in ('gamma', 'beta', 'Wq', 'Wk', 'Wv', 'Wg', 'bg', 'Wo', 'bo')}
    del _L0_attn_all

    def _L0_ffn_setup():
        import jax, jax.numpy as jnp
        import numpy as np
        B, T, C = (64, 96, 64)
        NH, NKV = (4, 2)
        HD = C // NH
        NREP = NH // NKV
        NE, TOPK = (8, 2)
        HID = int(8 / 3 * C)
        EPS_RMS = 1e-06

        def _rope_tables(t_len):
            inv_freq = 1.0 / 10000.0 ** (np.arange(0, HD, 2, dtype=np.float32) / HD)
            t = np.arange(t_len, dtype=np.float32)
            freqs = np.outer(t, inv_freq)
            emb = np.concatenate([freqs, freqs], axis=-1)
            return (jnp.asarray(np.cos(emb)), jnp.asarray(np.sin(emb)))

        def _rotate_half(x):
            h = x.shape[-1] // 2
            return jnp.concatenate([-x[..., h:], x[..., :h]], axis=-1)

        def _rmsnorm(v, w):
            return v * jax.lax.rsqrt(jnp.mean(v * v, axis=-1, keepdims=True) + EPS_RMS) * w
        key = jax.random.key(seed)
        ks = jax.random.split(key, 10)
        s = lambda k, shape: jax.random.normal(k, shape, jnp.float32) * 0.02
        return {'x': jax.random.normal(ks[0], (B, T, C), jnp.float32), 'ln1_w': jnp.ones((C,), jnp.float32), 'ln2_w': jnp.ones((C,), jnp.float32), 'wq': s(ks[1], (NH * HD, C)), 'wk': s(ks[2], (NKV * HD, C)), 'wv': s(ks[3], (NKV * HD, C)), 'wo': s(ks[4], (C, C)), 'router_w': s(ks[5], (NE, C)), 'w1': s(ks[6], (NE, HID, C)), 'w2': s(ks[7], (NE, C, HID)), 'w3': s(ks[8], (NE, HID, C))}
    _L0_ffn_all = _L0_ffn_setup()
    _L0_ffn_in = {k: v for k, v in _L0_ffn_all.items() if k in ('ln1_w', 'ln2_w', 'wq', 'wk', 'wv', 'wo', 'router_w', 'w1', 'w2', 'w3')}
    del _L0_ffn_all

    def _L1_attn_setup():
        import jax, jax.numpy as jnp
        import numpy as np
        D_MODEL = 64
        D_INNER = 128
        N_STATE = 64
        DT_RANK = 16
        K = 4
        B, L = (2, 256)

        def _selective_scan(u, delta, A, Bm, Cm, Dv):
            dA = jnp.einsum('bld,dn->bldn', delta, A)
            dB_u = jnp.einsum('bld,bld,bln->bldn', delta, u, Bm)
            shifted = jnp.concatenate([dA[:, 1:], jnp.zeros_like(dA[:, :1])], axis=1)
            e = jnp.exp(jnp.flip(jnp.cumsum(jnp.flip(shifted, axis=1), axis=1), axis=1))
            x = jnp.cumsum(dB_u * e, axis=1) / (e + 1e-12)
            y = jnp.einsum('bldn,bln->bld', x, Cm)
            return y + u * Dv
        key = jax.random.key(seed)
        ks = jax.random.split(key, 6)
        s = 0.02
        return {'x': jax.random.normal(ks[0], (B, L, D_MODEL), jnp.float32), 'W_in': jax.random.normal(ks[1], (D_MODEL, 2 * D_INNER), jnp.float32) * s, 'conv_k': jax.random.normal(ks[2], (K, D_INNER), jnp.float32) * s, 'conv_b': jnp.zeros((D_INNER,), jnp.float32), 'W_x': jax.random.normal(ks[3], (D_INNER, DT_RANK + 2 * N_STATE), jnp.float32) * s, 'W_dt': jax.random.normal(ks[4], (DT_RANK, D_INNER), jnp.float32) * s, 'b_dt': jnp.zeros((D_INNER,), jnp.float32), 'A_log': jnp.log(jnp.tile(jnp.arange(1, N_STATE + 1, dtype=jnp.float32)[None, :], (D_INNER, 1))), 'D_param': jnp.ones((D_INNER,), jnp.float32), 'W_out': jax.random.normal(ks[5], (D_INNER, D_MODEL), jnp.float32) * s}
    _L1_attn_all = _L1_attn_setup()
    _L1_attn_in = {k: v for k, v in _L1_attn_all.items() if k in ('W_in', 'conv_k', 'conv_b', 'W_x', 'W_dt', 'b_dt', 'A_log', 'D_param', 'W_out')}
    del _L1_attn_all

    def _L1_ffn_setup():
        import jax, jax.numpy as jnp
        import numpy as np
        D_IN, D_HID, D_OUT = (64, 128, 64)
        N_EXPERTS, TOP_K = (64, 2)
        B, S = (8, 1024)
        key = jax.random.key(seed)
        ks = jax.random.split(key, 8)
        scale_in = 1.0 / np.sqrt(D_IN)
        scale_hid = 1.0 / np.sqrt(D_HID)
        return {'x': jax.random.normal(ks[0], (B, S, D_IN), dtype=jnp.float32), 'Wr': jax.random.uniform(ks[1], (D_IN, N_EXPERTS), jnp.float32, -scale_in, scale_in), 'br': jax.random.uniform(ks[2], (N_EXPERTS,), jnp.float32, -scale_in, scale_in), 'W1': jax.random.uniform(ks[3], (N_EXPERTS, D_IN, D_HID), jnp.float32, -scale_in, scale_in), 'b1': jax.random.uniform(ks[4], (N_EXPERTS, D_HID), jnp.float32, -scale_in, scale_in), 'W2': jax.random.uniform(ks[5], (N_EXPERTS, D_HID, D_OUT), jnp.float32, -scale_hid, scale_hid), 'b2': jax.random.uniform(ks[6], (N_EXPERTS, D_OUT), jnp.float32, -scale_hid, scale_hid)}
    _L1_ffn_all = _L1_ffn_setup()
    _L1_ffn_in = {k: v for k, v in _L1_ffn_all.items() if k in ('Wr', 'br', 'W1', 'b1', 'W2', 'b2')}
    del _L1_ffn_all
    return {'x': x, 'L0_tok_emb_2': _L0_tok_in['emb_2'], 'L0_tok_emb_3': _L0_tok_in['emb_3'], 'L0_tok_emb_4': _L0_tok_in['emb_4'], 'L0_attn_gamma': _L0_attn_in['gamma'], 'L0_attn_beta': _L0_attn_in['beta'], 'L0_attn_Wq': _L0_attn_in['Wq'], 'L0_attn_Wk': _L0_attn_in['Wk'], 'L0_attn_Wv': _L0_attn_in['Wv'], 'L0_attn_Wg': _L0_attn_in['Wg'], 'L0_attn_bg': _L0_attn_in['bg'], 'L0_attn_Wo': _L0_attn_in['Wo'], 'L0_attn_bo': _L0_attn_in['bo'], 'L0_ffn_ln1_w': _L0_ffn_in['ln1_w'], 'L0_ffn_ln2_w': _L0_ffn_in['ln2_w'], 'L0_ffn_wq': _L0_ffn_in['wq'], 'L0_ffn_wk': _L0_ffn_in['wk'], 'L0_ffn_wv': _L0_ffn_in['wv'], 'L0_ffn_wo': _L0_ffn_in['wo'], 'L0_ffn_router_w': _L0_ffn_in['router_w'], 'L0_ffn_w1': _L0_ffn_in['w1'], 'L0_ffn_w2': _L0_ffn_in['w2'], 'L0_ffn_w3': _L0_ffn_in['w3'], 'L1_attn_W_in': _L1_attn_in['W_in'], 'L1_attn_conv_k': _L1_attn_in['conv_k'], 'L1_attn_conv_b': _L1_attn_in['conv_b'], 'L1_attn_W_x': _L1_attn_in['W_x'], 'L1_attn_W_dt': _L1_attn_in['W_dt'], 'L1_attn_b_dt': _L1_attn_in['b_dt'], 'L1_attn_A_log': _L1_attn_in['A_log'], 'L1_attn_D_param': _L1_attn_in['D_param'], 'L1_attn_W_out': _L1_attn_in['W_out'], 'L1_ffn_Wr': _L1_ffn_in['Wr'], 'L1_ffn_br': _L1_ffn_in['br'], 'L1_ffn_W1': _L1_ffn_in['W1'], 'L1_ffn_b1': _L1_ffn_in['b1'], 'L1_ffn_W2': _L1_ffn_in['W2'], 'L1_ffn_b2': _L1_ffn_in['b2']}

def reference(x, L0_tok_emb_2, L0_tok_emb_3, L0_tok_emb_4, L0_attn_gamma, L0_attn_beta, L0_attn_Wq, L0_attn_Wk, L0_attn_Wv, L0_attn_Wg, L0_attn_bg, L0_attn_Wo, L0_attn_bo, L0_ffn_ln1_w, L0_ffn_ln2_w, L0_ffn_wq, L0_ffn_wk, L0_ffn_wv, L0_ffn_wo, L0_ffn_router_w, L0_ffn_w1, L0_ffn_w2, L0_ffn_w3, L1_attn_W_in, L1_attn_conv_k, L1_attn_conv_b, L1_attn_W_x, L1_attn_W_dt, L1_attn_b_dt, L1_attn_A_log, L1_attn_D_param, L1_attn_W_out, L1_ffn_Wr, L1_ffn_br, L1_ffn_W1, L1_ffn_b1, L1_ffn_W2, L1_ffn_b2):
    import jax
    import jax.numpy as jnp

    def _L0_tok_ref(byte_ids, emb_2, emb_3, emb_4):
        import jax, jax.numpy as jnp
        import numpy as np
        PRIME = 31
        VOCAB = 125000
        NGRAM_SIZES = (2, 3, 4)

        def _ngram_hash(byte_ids, n):
            T = byte_ids.shape[1]
            powers = PRIME ** jnp.arange(n - 1, -1, -1, dtype=jnp.int64) % VOCAB
            windows = jnp.stack([byte_ids[:, i:T - n + 1 + i] for i in range(n)], axis=-1)
            return (windows.astype(jnp.int64) * powers).sum(axis=-1) % VOCAB
        tables = {2: emb_2, 3: emb_3, 4: emb_4}
        B, T = byte_ids.shape
        D = emb_2.shape[1]
        out = jnp.zeros((B, T, D), dtype=emb_2.dtype)
        for n in NGRAM_SIZES:
            idx = _ngram_hash(byte_ids, n)
            gathered = tables[n][idx]
            out = out + jnp.pad(gathered, ((0, 0), (n - 1, 0), (0, 0)))
        return out / (len(NGRAM_SIZES) + 1)

    def _L0_attn_ref(m, gamma, beta, Wq, Wk, Wv, Wg, bg, Wo, bo):
        import jax, jax.numpy as jnp
        import numpy as np
        import math
        N_SEQ, L_RES, D_MODEL = (128, 96, 64)
        N_HEAD, C_HEAD = (8, 32)
        EPS = 1e-05
        N, L, D = m.shape
        H, C = (N_HEAD, C_HEAD)
        mu = jnp.mean(m, axis=-1, keepdims=True)
        var = jnp.mean(jnp.square(m - mu), axis=-1, keepdims=True)
        mn = (m - mu) * jax.lax.rsqrt(var + EPS) * gamma + beta
        q = (mn @ Wq).reshape(N, L, H, C)
        k = (mn @ Wk).reshape(N, L, H, C)
        v = (mn @ Wv).reshape(N, L, H, C)
        g = jax.nn.sigmoid(mn @ Wg + bg).reshape(N, L, H, C)
        scale = 1.0 / math.sqrt(C) / math.sqrt(L)
        att = jnp.einsum('slhc,tlhc->sth', q, k) * scale
        att = jax.nn.softmax(att, axis=1)
        o = jnp.einsum('sth,tlhc->slhc', att, v) * g
        return o.reshape(N, L, H * C) @ Wo + bo

    def _L0_ffn_ref(x, ln1_w, ln2_w, wq, wk, wv, wo, router_w, w1, w2, w3):
        import jax, jax.numpy as jnp
        import numpy as np
        B, T, C = (64, 96, 64)
        NH, NKV = (4, 2)
        HD = C // NH
        NREP = NH // NKV
        NE, TOPK = (8, 2)
        HID = int(8 / 3 * C)
        EPS_RMS = 1e-06

        def _rope_tables(t_len):
            inv_freq = 1.0 / 10000.0 ** (np.arange(0, HD, 2, dtype=np.float32) / HD)
            t = np.arange(t_len, dtype=np.float32)
            freqs = np.outer(t, inv_freq)
            emb = np.concatenate([freqs, freqs], axis=-1)
            return (jnp.asarray(np.cos(emb)), jnp.asarray(np.sin(emb)))

        def _rotate_half(x):
            h = x.shape[-1] // 2
            return jnp.concatenate([-x[..., h:], x[..., :h]], axis=-1)

        def _rmsnorm(v, w):
            return v * jax.lax.rsqrt(jnp.mean(v * v, axis=-1, keepdims=True) + EPS_RMS) * w
        Bx, Tx, Cx = x.shape
        h = _rmsnorm(x, ln1_w)
        q = (h @ wq.T).reshape(Bx, Tx, NH, HD).transpose(0, 2, 1, 3)
        k = (h @ wk.T).reshape(Bx, Tx, NKV, HD).transpose(0, 2, 1, 3)
        v = (h @ wv.T).reshape(Bx, Tx, NKV, HD).transpose(0, 2, 1, 3)
        cos, sin = _rope_tables(Tx)
        cos, sin = (cos[None, None], sin[None, None])
        q = q * cos + _rotate_half(q) * sin
        k = k * cos + _rotate_half(k) * sin
        k = jnp.repeat(k, NREP, axis=1)
        v = jnp.repeat(v, NREP, axis=1)
        scores = jnp.einsum('bhtd,bhsd->bhts', q, k) / jnp.sqrt(jnp.float32(HD))
        causal = jnp.tril(jnp.ones((Tx, Tx), dtype=bool))
        scores = jnp.where(causal[None, None], scores, jnp.float32(-1e+30))
        att = jax.nn.softmax(scores, axis=-1)
        y = jnp.einsum('bhts,bhsd->bhtd', att, v).transpose(0, 2, 1, 3).reshape(Bx, Tx, Cx)
        x = x + y @ wo.T
        flat = _rmsnorm(x, ln2_w).reshape(-1, Cx)
        probs = jax.nn.softmax(flat @ router_w.T, axis=-1)
        tp, ti = jax.lax.top_k(probs, TOPK)
        tp = tp / (jnp.sum(tp, axis=-1, keepdims=True) + 1e-09)
        weights = jnp.sum(tp[..., None] * jax.nn.one_hot(ti, NE, dtype=flat.dtype), axis=1)
        out = jnp.zeros_like(flat)
        for e in range(NE):
            hh = jax.nn.silu(flat @ w1[e].T) * (flat @ w3[e].T)
            out = out + weights[:, e:e + 1] * (hh @ w2[e].T)
        return x + out.reshape(Bx, Tx, Cx)

    def _L1_attn_ref(x, W_in, conv_k, conv_b, W_x, W_dt, b_dt, A_log, D_param, W_out):
        import jax, jax.numpy as jnp
        import numpy as np
        D_MODEL = 64
        D_INNER = 128
        N_STATE = 64
        DT_RANK = 16
        K = 4
        B, L = (2, 256)

        def _selective_scan(u, delta, A, Bm, Cm, Dv):
            dA = jnp.einsum('bld,dn->bldn', delta, A)
            dB_u = jnp.einsum('bld,bld,bln->bldn', delta, u, Bm)
            shifted = jnp.concatenate([dA[:, 1:], jnp.zeros_like(dA[:, :1])], axis=1)
            e = jnp.exp(jnp.flip(jnp.cumsum(jnp.flip(shifted, axis=1), axis=1), axis=1))
            x = jnp.cumsum(dB_u * e, axis=1) / (e + 1e-12)
            y = jnp.einsum('bldn,bln->bld', x, Cm)
            return y + u * Dv
        x_and_res = x @ W_in
        x_int, res = jnp.split(x_and_res, 2, axis=-1)
        xp = jnp.pad(x_int, ((0, 0), (K - 1, 0), (0, 0)))
        xc = jax.lax.conv_general_dilated(xp, conv_k[:, None, :], window_strides=(1,), padding='VALID', dimension_numbers=('NWC', 'WIO', 'NWC'), feature_group_count=D_INNER) + conv_b
        xc = jax.nn.swish(xc)
        x_dbl = xc @ W_x
        dl, Bm, Cm = jnp.split(x_dbl, [DT_RANK, DT_RANK + N_STATE], axis=-1)
        delta = jax.nn.softplus(dl @ W_dt + b_dt)
        A = -jnp.exp(A_log)
        y = _selective_scan(xc, delta, A, Bm, Cm, D_param)
        y = y * jax.nn.swish(res)
        return y @ W_out

    def _L1_ffn_ref(x, Wr, br, W1, b1, W2, b2):
        import jax, jax.numpy as jnp
        import numpy as np
        D_IN, D_HID, D_OUT = (64, 128, 64)
        N_EXPERTS, TOP_K = (64, 2)
        B, S = (8, 1024)
        Bx, Sx, D = x.shape
        xf = x.reshape(-1, D)
        T = xf.shape[0]
        E = Wr.shape[1]
        logits = xf @ Wr + br
        topk_logits, topk_idx = jax.lax.top_k(logits, TOP_K)
        gates = jax.nn.softmax(topk_logits, axis=1)
        combine = jnp.zeros((T, E), xf.dtype).at[jnp.arange(T)[:, None], topk_idx].add(gates)
        out = jnp.zeros((T, W2.shape[-1]), xf.dtype)
        for e in range(E):
            h = jax.nn.relu(xf @ W1[e] + b1[e])
            y = h @ W2[e] + b2[e]
            out = out + combine[:, e:e + 1] * y
        return out.reshape(Bx, Sx, -1)
    h = _L0_tok_ref(x, L0_tok_emb_2, L0_tok_emb_3, L0_tok_emb_4)
    h = h + _L0_attn_ref(_layernorm(h, axis=-1), L0_attn_gamma, L0_attn_beta, L0_attn_Wq, L0_attn_Wk, L0_attn_Wv, L0_attn_Wg, L0_attn_bg, L0_attn_Wo, L0_attn_bo)
    h = h + _L0_ffn_ref(_layernorm(h, axis=-1), L0_ffn_ln1_w, L0_ffn_ln2_w, L0_ffn_wq, L0_ffn_wk, L0_ffn_wv, L0_ffn_wo, L0_ffn_router_w, L0_ffn_w1, L0_ffn_w2, L0_ffn_w3)
    h = h + _L1_attn_ref(_layernorm(h, axis=-1), L1_attn_W_in, L1_attn_conv_k, L1_attn_conv_b, L1_attn_W_x, L1_attn_W_dt, L1_attn_b_dt, L1_attn_A_log, L1_attn_D_param, L1_attn_W_out)
    h = h + _L1_ffn_ref(_layernorm(h, axis=-1), L1_ffn_Wr, L1_ffn_br, L1_ffn_W1, L1_ffn_b1, L1_ffn_W2, L1_ffn_b2)
    return h

_drawn_inputs = setup_inputs


def setup_inputs(seed=0):
    import zlib

    import numpy as np

    out = dict(_drawn_inputs(seed))
    spreads = {'L0_attn_gamma': (1.0, 0.2),
     'L0_attn_beta': (0.0, 0.1),
     'L0_attn_bg': (0.0, 0.1),
     'L0_attn_bo': (0.0, 0.1),
     'L0_ffn_ln1_w': (1.0, 0.6),
     'L0_ffn_ln2_w': (1.0, 0.6),
     'L1_attn_conv_b': (0.0, 0.8),
     'L1_attn_b_dt': (0.0, 0.8),
     'L1_attn_D_param': (1.0, 0.6)}
    factors = {'L0_ffn_wq': 8.0,
     'L0_ffn_wk': 8.0,
     'L0_ffn_wv': 5.562,
     'L0_ffn_wo': 6.034,
     'L0_ffn_router_w': 8.0,
     'L0_ffn_w1': 8.0,
     'L0_ffn_w2': 8.0,
     'L0_ffn_w3': 8.0,
     'L1_attn_W_in': 8.0,
     'L1_attn_conv_k': 8.0,
     'L1_attn_W_x': 8.0,
     'L1_attn_W_dt': 8.0,
     'L1_attn_A_log': 8.0,
     'L1_attn_W_out': 8.0,
     'L1_ffn_b1': 16.518,
     'L1_ffn_br': 4.132,
     'L1_ffn_b2': 8.0}
    for name, (base, spread) in spreads.items():
        noise = np.random.default_rng([zlib.crc32(name.encode()), seed]).standard_normal(out[name].shape)
        drawn = base * np.exp(spread * noise) if base else spread * noise
        out[name] = jnp.asarray(drawn.astype(out[name].dtype))
    for name, factor in factors.items():
        out[name] = (out[name] * factor).astype(out[name].dtype)
    return out
```

```python
from contextlib import ExitStack

import concourse.bass as bass
from concourse import mybir

F32 = mybir.dt.float32
BF16 = mybir.dt.bfloat16
I32 = mybir.dt.int32
U32 = mybir.dt.uint32
ALU = mybir.AluOpType
ACT = mybir.ActivationFunctionType
AX_X = mybir.AxisListType.X

P = 128
SEQ, LEN, D = 64, 256, 64
TILES = SEQ * LEN // P
VOCAB, PRIME = 125000, 31
LN_EPS, RMS_EPS = 1e-5, 1e-6


class Kit:

    def __init__(self, nc, ctx):
        self.nc, self.ctx = nc, ctx
        self.held = ctx.enter_context(nc.semaphore("held"))
        self.used = []

    def sb(self, ctx, name, shape, dt=F32):
        return ctx.enter_context(self.nc.sbuf_tensor(name, shape, dt))

    def ps(self, ctx, name, shape, dt=F32):
        return ctx.enter_context(self.nc.psum_tensor(name, shape, dt))

    def sem(self, ctx, name):
        handle = ctx.enter_context(self.nc.semaphore(name))
        self.used.append(handle)
        return handle

    def block(self, ctx):
        ctx.callback(self.clear)
        return ctx.enter_context(self.nc.Block())

    def clear(self):
        done, self.used = self.used, []
        with self.nc.Block() as block:
            @block.sync
            def _(sp):
                for handle in done:
                    sp.sem_clear(handle)

    def hold(self, eng, sem, value):
        eng.wait_ge(sem, value)
        eng.sem_inc(self.held, 1)


def bcast(ap, n):
    return ap.unsqueeze(2).to_broadcast([ap.shape[0], ap.shape[1], n])


def embed_and_logits(nc, kit, a, H, YT, LOGITS):
    G = 8
    STEPS = TILES // G
    with ExitStack() as c:
        sb = lambda n, s, d=F32: kit.sb(c, n, s, d)
        sem = lambda n: kit.sem(c, n)
        tok_i = sb("tok_i", [P, 4 + LEN], I32)
        tok = sb("tok", [P, 4 + LEN])
        hs = sb("hs", [P, 3, TILES])
        quo = sb("quo", [P, 3, TILES])
        quo_i = sb("quo_i", [P, 3, TILES], I32)
        rows = sb("rows", [P, 3, TILES], U32)
        rows_now = sb("rows_now", [P, 2, 3, G], U32)
        gath = sb("gath", [P, 2, 3, G, D])
        h_now = sb("h_now", [P, G, D])
        cen = sb("cen", [P, G, D])
        sq = sb("sq", [P, G, D])
        ys = sb("ys", [P, G, D])
        st = sb("st", [P, 4, G])
        eps2 = sb("eps2", [P, 1])
        ident = sb("ident1", [P, P])
        wqk = sb("wqk", [P, 8, P])
        gb = sb("gb", [P, 2])
        yt = sb("yt_now", [P, 4, P])
        qk = sb("qk", [P, 2, 2, 4 * P])
        zer = sb("zer", [P, 256])
        ps_t = kit.ps(c, "ps_t", [P, 4, P])
        ps_qk = kit.ps(c, "ps_qk", [P, 2, 2, 4 * P])
        ps_att = kit.ps(c, "ps_att", [P, 4, SEQ])
        tok_in, w_in, rows_ready, cleared = sem("tok_in"), sem("w_in"), sem("rows_ready"), sem("cleared")
        picked = [sem("picked0"), sem("picked1")]
        gath_free, ssum, root, ys_ready, t_done = sem("gath_free"), sem("ssum"), sem("root"), sem("ys_ready"), sem("t_done")
        yt_ready, proj, q_out, k_out, att_done = sem("yt_ready"), sem("proj"), sem("q_out"), sem("k_out"), sem("att_done")
        zero_ready = sem("zero_ready")
        block = kit.block(c)

        @block.sync
        def _(sp):
            sp.wait_ge(zero_ready, 1)
            sp.dma_start(tok_i[0:64, 4:260], a["x"]).then_inc(tok_in, 16)
            sp.dma_start(tok_i[64:128, 3:259], a["x"]).then_inc(tok_in, 16)
            sp.dma_start(ident[:], a["ident"]).then_inc(w_in, 16)
            sp.dma_start(wqk[:], a["attn_wqk"]).then_inc(w_in, 16)
            sp.dma_start(gb[:], a["attn_gb"]).then_inc(w_in, 16)

        @block.gpsimd
        def _(pool):
            pool.wait_ge(rows_ready, 1)
            pool.wait_ge(cleared, 2)
            with pool.Fori(0, STEPS // 2) as i:
                for b in range(2):
                    step = i * 2 + b
                    kit.hold(pool, gath_free, step + 1)
                    pool.tensor_copy(rows_now[:, b], rows[:, :, bass.ds(step * G, G)])
                    pool.drain()
                    for t in range(G):
                        for n in range(3):
                            pool.indirect_dma_start(
                                gath[:, b, n, t, :], None, a[f"emb{n + 2}"],
                                bass.IndirectOffsetOnAxis(ap=rows_now[:, b, n, t:t + 1], axis=0),
                                bounds_check=VOCAB - 1, oob_is_err=False).then_inc(picked[b], 16)

        @block.vector
        def _(dve):
            dve.memset(tok_i[:], 0).then_inc(zero_ready, 1)
            dve.memset(gath[:, 0], 0.0).then_inc(cleared, 1)
            dve.memset(gath[:, 1], 0.0).then_inc(cleared, 1)
            dve.memset(zer[:], 0.0).then_inc(cleared, 1)
            dve.memset(eps2[:], LN_EPS * LN_EPS).then_inc(cleared, 1)
            dve.sem_inc(gath_free, 2)
            dve.wait_ge(tok_in, 32)
            dve.tensor_copy(tok[:], tok_i[:])
            dve.drain()
            tv = tok[:].rearrange("p (l two) -> p l two", two=2)

            def back(k):
                o = 4 - k
                return tok[:, o:o + 2 * TILES - 1:2] if o + 2 * TILES - 1 <= 260 else tok[:, o:260:2]
            dve.scalar_tensor_tensor(hs[:, 0], back(1), float(PRIME), back(0), ALU.mult, ALU.add)
            dve.drain()
            dve.scalar_tensor_tensor(hs[:, 1], back(2), float(PRIME ** 2 % VOCAB), hs[:, 0], ALU.mult, ALU.add)
            dve.drain()
            dve.scalar_tensor_tensor(hs[:, 2], back(3), float(PRIME ** 3 % VOCAB), hs[:, 1], ALU.mult, ALU.add)
            dve.drain()
            dve.tensor_scalar(quo[:], hs[:], 1.0 / VOCAB, None, ALU.mult)
            dve.drain()
            dve.tensor_copy(quo_i[:], quo[:])
            dve.drain()
            dve.tensor_copy(quo[:], quo_i[:])
            dve.drain()
            dve.scalar_tensor_tensor(hs[:], quo[:], -float(VOCAB), hs[:], ALU.mult, ALU.add)
            dve.drain()
            for cmp, shift in ((ALU.is_lt, float(VOCAB)), (ALU.is_ge, -float(VOCAB))):
                edge = 0.0 if cmp == ALU.is_lt else float(VOCAB)
                dve.tensor_scalar(quo[:], hs[:], edge, shift, cmp, ALU.mult)
                dve.drain()
                dve.tensor_tensor(hs[:], hs[:], quo[:], ALU.add)
                dve.drain()
            dve.memset(hs[0:64, 0, 0:1], 2.0 ** 20)
            dve.memset(hs[:, 1:3, 0:1], 2.0 ** 20)
            dve.memset(hs[0:64, 2, 1:2], 2.0 ** 20)
            dve.drain()
            dve.tensor_copy(rows[:], hs[:]).then_inc(rows_ready, 1)
            with dve.Fori(0, STEPS // 2) as i:
                for b in range(2):
                    step = i * 2 + b
                    kit.hold(dve, picked[b], 16 * 3 * G * i + 16 * 3 * G)
                    dve.tensor_tensor(sq[:], gath[:, b, 0], gath[:, b, 1], ALU.add)
                    dve.drain()
                    dve.tensor_tensor(cen[:], sq[:], gath[:, b, 2], ALU.add).then_inc(gath_free, 1)
                    dve.drain()
                    dve.tensor_scalar(h_now[:], cen[:], 0.25, None, ALU.mult)
                    dve.drain()
                    dve.tensor_copy(H[:, bass.ds(step * G, G), :], h_now[:])
                    dve.tensor_reduce(st[:, 0], h_now[:], AX_X, ALU.add)
                    dve.drain()
                    dve.tensor_scalar(st[:, 1], st[:, 0], 1.0 / D, None, ALU.mult)
                    dve.drain()
                    dve.tensor_tensor(cen[:], h_now[:], bcast(st[:, 1], D), ALU.subtract)
                    dve.drain()
                    dve.tensor_tensor(sq[:], cen[:], cen[:], ALU.mult)
                    dve.drain()
                    dve.tensor_reduce(st[:, 2], sq[:], AX_X, ALU.add).then_inc(ssum, 1)
                    dve.wait_ge(root, step + 1)
                    dve.reciprocal(st[:, 3], st[:, 1])
                    dve.drain()
                    dve.tensor_tensor(ys[:], cen[:], bcast(st[:, 3], D), ALU.mult).then_inc(ys_ready, 1)
                    for p in range(4):
                        kit.hold(dve, proj, step * 4 + p + 1)
                        dve.tensor_copy(qk[:, p % 2, 1, :], ps_qk[:, p % 2, 1, :]).then_inc(k_out, 1)
            dve.wait_ge(att_done, 1)
            dve.tensor_copy(LOGITS[:], ps_att[:])

        @block.scalar
        def _(act):
            act.wait_ge(w_in, 48)
            act.wait_ge(cleared, 4)
            with act.Fori(0, STEPS) as i:
                kit.hold(act, ssum, i + 1)
                act.activation(st[:, 1], st[:, 2], ACT.Sqrt, bias=eps2[:], scale=(1 + LN_EPS) / D).then_inc(root, 1)
                kit.hold(act, t_done, i + 1)
                act.activation(yt[:], ps_t[:], ACT.Identity, bias=gb[:, 1:2], scale=gb[:, 0:1]).then_inc(yt_ready, 1)
                act.activation(YT[:, bass.ds(i * 4, 4), :], ps_t[:], ACT.Identity, bias=gb[:, 1:2], scale=gb[:, 0:1]).then_inc(yt_ready, 1)
                for p in range(4):
                    kit.hold(act, proj, i * 4 + p + 1)
                    act.activation(qk[:, p % 2, 0, :], ps_qk[:, p % 2, 0, :], ACT.Copy).then_inc(q_out, 1)

        @block.tensor
        def _(pe):
            pe.wait_ge(w_in, 48)
            pe.wait_ge(cleared, 4)
            pe.matmul(ps_att[:].rearrange("p a t -> p (a t)"), zer[:, 0:P], zer[:], start=True, stop=False, skip_group_check=True)

            def project(p, b):
                pe.matmul(ps_qk[:, b, 0, :], wqk[:, p, :], yt[:].rearrange("p a t -> p (a t)"), start=True, stop=True)
                pe.matmul(ps_qk[:, b, 1, :], wqk[:, 4 + p, :], yt[:].rearrange("p a t -> p (a t)"), start=True, stop=True).then_inc(proj, 1)

            def logits(p, i):
                kit.hold(pe, q_out, i * 4 + p + 1)
                kit.hold(pe, k_out, i * 4 + p + 1)
                for h in range(2):
                    r = slice(64 * h, 64 * h + 64)
                    for s in range(8):
                        mm = pe.matmul(ps_att[r, p, :], qk[r, p % 2, 0, 64 * s:64 * s + 64], qk[r, p % 2, 1, 64 * s:64 * s + 64],
                                       start=False, stop=False, skip_group_check=True)
                return mm

            with pe.Fori(0, STEPS) as i:
                kit.hold(pe, ys_ready, i + 1)
                for t in range(4):
                    tr = pe.transpose(ps_t[:, t, :], ys[:, 2 * t:2 * t + 2, :].rearrange("p a d -> p (a d)"), ident[:])
                tr.then_inc(t_done, 1)
                kit.hold(pe, yt_ready, 2 * i + 2)
                project(0, 0)
                project(1, 1)
                logits(0, i)
                project(2, 0)
                logits(1, i)
                project(3, 1)
                logits(2, i)
                logits(3, i)
            pe.matmul(ps_att[:].rearrange("p a t -> p (a t)"), zer[:, 0:P], zer[:], start=False, stop=True,
                      skip_group_check=True).then_inc(att_done, 1)


def row_softmax(nc, kit, a, LOGITS, MIX):
    scale = 1.0 / (32 ** 0.5) / (LEN ** 0.5)
    with ExitStack() as c:
        sb = lambda n, s, d=F32: kit.sb(c, n, s, d)
        sem = lambda n: kit.sem(c, n)
        ident = sb("ident2", [P, P])
        prob = sb("prob", [P, 4, SEQ])
        twice = sb("twice", [P, 4, 2, SEQ])
        st = sb("st2", [P, 3, 4])
        ps_t = kit.ps(c, "ps_t2", [P, 4, P])
        w_in, lmax, expd, twice_ready, t_done = sem("w_in2"), sem("lmax"), sem("expd"), sem("twice_ready"), sem("t_done2")
        block = kit.block(c)

        @block.sync
        def _(sp):
            sp.dma_start(ident[:], a["ident"]).then_inc(w_in, 16)

        @block.vector
        def _(dve):
            dve.memset(MIX[:], 0.0)
            dve.tensor_reduce(st[:, 0], LOGITS[:], AX_X, ALU.max)
            dve.drain()
            dve.tensor_tensor(prob[:], LOGITS[:], bcast(st[:, 0], SEQ), ALU.subtract).then_inc(lmax, 1)
            dve.wait_ge(expd, 1)
            dve.tensor_reduce(st[:, 1], prob[:], AX_X, ALU.add)
            dve.drain()
            dve.reciprocal(st[:, 2], st[:, 1])
            dve.drain()
            for k in range(2):
                w = dve.tensor_tensor(twice[:, :, k, :], prob[:], bcast(st[:, 2], SEQ), ALU.mult)
            w.then_inc(twice_ready, 1)
            dve.wait_ge(t_done, 1)
            for k in range(2):
                r = slice(64 * k, 64 * k + 64)
                dve.tensor_copy(MIX[r, :, r].rearrange("t (p h) s -> t p h s", h=2), ps_t[r, :, :].rearrange("t p (h s) -> t p h s", h=2))

        @block.scalar
        def _(act):
            act.wait_ge(lmax, 1)
            act.activation(prob[:], prob[:], ACT.Exp, scale=scale).then_inc(expd, 1)

        @block.tensor
        def _(pe):
            pe.wait_ge(w_in, 16)
            pe.wait_ge(twice_ready, 1)
            for p in range(4):
                tr = pe.transpose(ps_t[:, p, :], twice[:, p, :, :].rearrange("p k s -> p (k s)"), ident[:])
            tr.then_inc(t_done, 1)


def row_attention_out(nc, kit, a, H, YT, MIX, h1):
    N = TILES // 2
    with ExitStack() as c:
        sb = lambda n, s, d=F32: kit.sb(c, n, s, d)
        sem = lambda n: kit.sem(c, n)
        ident = sb("ident3", [P, P])
        wvg = sb("wvg", [P, 2, 512])
        wo = sb("wo", [P, 2, D])
        bg = sb("bg", [P, 256])
        bo = sb("bo", [P, D])
        yt = sb("yt3", [P, 2, P])
        v = sb("v", [P, 2, 2, 256])
        gz = sb("gz", [P, 2, 2, 256])
        og = sb("og", [P, 2, 2, 256])
        ogt = sb("ogt", [P, 2, 2, 2, P])
        res = sb("res3", [P, 4, D])
        ps_vg = kit.ps(c, "ps_vg", [P, 2, 2, 2, 256])
        ps_o = kit.ps(c, "ps_o", [P, 2, 8, 2, 32])
        ps_t = kit.ps(c, "ps_t3", [P, 2, 2, P])
        ps_h = kit.ps(c, "ps_h", [P, 4, D])
        w_in, yt_ready, vg_done, v_out, gz_out, sig = (sem(n) for n in ("w_in3", "yt_ready3", "vg_done", "v_out", "gz_out", "sig"))
        o_done, og_out, t_done, ogt_out, h_done, h_out, stored = (sem(n) for n in ("o_done", "og_out", "t_done3", "ogt_out", "h_done", "h_out", "stored3"))
        block = kit.block(c)

        @block.sync
        def _(sp):
            for dst, src in ((ident[:], a["ident"]), (wvg[:], a["attn_wvg"]), (wo[:], a["attn_wo"]),
                             (bg[:], a["attn_bg"].to_broadcast([P, 256])), (bo[:], a["attn_bo"].to_broadcast([P, D]))):
                sp.dma_start(dst, src).then_inc(w_in, 16)
            sp.wait_ge(h_out, N)
            for l2 in range(2):
                sp.dma_start(h1.rearrange("s (lp l2) d -> l2 s lp d", l2=2)[l2], H[64 * l2:64 * l2 + 64, :, :]).then_inc(stored, 16)
            sp.wait_ge(stored, 32)

        @block.gpsimd
        def _(pool):
            with pool.Fori(0, N // 2) as i:
                for b in range(2):
                    kit.hold(pool, vg_done, i * 2 + b + 1)
                    pool.tensor_copy(yt[:, b, :], YT[:, bass.ds(i * 2 + b, 1), :].rearrange("p a t -> p (a t)")).then_inc(yt_ready, 1)

        @block.scalar
        def _(act):
            with act.Fori(0, N // 2) as i:
                for b in range(2):
                    kit.hold(act, vg_done, i * 2 + b + 3)
                    act.activation(v[:, b], ps_vg[:, b, 0], ACT.Copy).then_inc(v_out, 1)
                    kit.hold(act, gz_out, i * 2 + b + 1)
                    act.activation(gz[:, b], gz[:, b], ACT.Sigmoid).then_inc(sig, 1)
                for b in range(2):
                    kit.hold(act, t_done, i * 2 + b + 1)
                    act.activation(ogt[:, b].rearrange("p l k t -> p (l k t)"), ps_t[:].rearrange("p l k t -> p (l k t)"), ACT.Copy).then_inc(ogt_out, 1)

        @block.vector
        def _(dve):
            dve.sem_inc(vg_done, 2)
            dve.wait_ge(w_in, 80)
            with dve.Fori(0, N // 2) as i:
                for b in range(2):
                    kit.hold(dve, vg_done, i * 2 + b + 3)
                    dve.tensor_tensor(gz[:, b], ps_vg[:, b, 1], bg[:].unsqueeze(1).to_broadcast([P, 2, 256]), ALU.add).then_inc(gz_out, 1)
                for b in range(2):
                    kit.hold(dve, sig, i * 2 + b + 1)
                    kit.hold(dve, o_done, i * 2 + b + 1)
                    dve.tensor_tensor(og[:, b].rearrange("p l (h c) -> p h l c", h=8), ps_o[:, b], gz[:, b].rearrange("p l (h c) -> p h l c", h=8), ALU.mult).then_inc(og_out, 1)
                kit.hold(dve, h_done, i * 2 + 2)
                dve.tensor_tensor(res[:], ps_h[:], bo[:].unsqueeze(1).to_broadcast([P, 4, D]), ALU.add)
                dve.drain()
                hh = H[:, bass.ds(i * 4, 4), :]
                dve.tensor_tensor(hh, hh, res[:], ALU.add).then_inc(h_out, 2)

        @block.tensor
        def _(pe):
            pe.wait_ge(w_in, 80)
            with pe.Fori(0, N // 2) as i:
                for b in range(2):
                    kit.hold(pe, yt_ready, i * 2 + b + 1)
                    for j in range(2):
                        for k in range(2):
                            mm = pe.matmul(ps_vg[:, b, k, j, :], yt[:, b, :], wvg[:, j, 256 * k:256 * k + 256], start=True, stop=True)
                    mm.then_inc(vg_done, 1)
                for b in range(2):
                    kit.hold(pe, v_out, i * 2 + b + 1)
                    for h in range(8):
                        mm = pe.matmul(ps_o[:, b, h], MIX[:, h, :], v[:, b, :, 32 * h:32 * h + 32], start=True, stop=True)
                    mm.then_inc(o_done, 1)
                for b in range(2):
                    kit.hold(pe, og_out, i * 2 + b + 1)
                    if b == 1:
                        kit.hold(pe, ogt_out, i * 2 + 1)
                    for l in range(2):
                        for k in range(2):
                            mm = pe.transpose(ps_t[:, l, k, :], og[:, b, l, 128 * k:128 * k + 128], ident[:])
                    mm.then_inc(t_done, 1)
                for b in range(2):
                    kit.hold(pe, ogt_out, i * 2 + b + 1)
                    for l in range(2):
                        for k in range(2):
                            mm = pe.matmul(ps_h[:, 2 * b + l, :], ogt[:, b, l, k, :], wo[:, k, :], start=(k == 0), stop=(k == 1))
                    mm.then_inc(h_done, 1)


NEG = -1e30


def norm_statistics(dve, src, cen, sq, st):
    dve.tensor_reduce(st[:, 0], src, AX_X, ALU.add)
    dve.drain()
    dve.tensor_scalar(st[:, 1], st[:, 0], 1.0 / D, None, ALU.mult)
    dve.drain()
    dve.tensor_tensor(cen, src, bcast(st[:, 1], D), ALU.subtract)
    dve.drain()
    dve.tensor_tensor(sq, cen, cen, ALU.mult)
    dve.drain()
    dve.tensor_reduce(st[:, 2], sq, AX_X, ALU.add)
    dve.drain()


def causal_attention(nc, kit, a, h1, H, X2):
    with ExitStack() as c:
        sb = lambda n, s, d=F32: kit.sb(c, n, s, d)
        sem = lambda n: kit.sem(c, n)
        ident = sb("ident4", [P, P])
        identb = sb("identb4", [P, P], BF16)
        maskf = sb("maskf", [P, P])
        mask = sb("mask", [P, P], BF16)
        wqkv = sb("wqkv", [64, 4 * P + 32])
        wo = sb("wo4", [64, D])
        ln1 = sb("ln1", [64, 1])
        rope = sb("rope", [P, 2, LEN])
        cen = sb("cen4", [P, 2, D])
        sq = sb("sq4", [P, 2, D])
        u = sb("u4", [P, 2, D])
        st = sb("st4", [P, 3, 2])
        var = sb("var4", [P, 2, 2])
        half = sb("half4", [P, 2, 2])
        rs = sb("rs4", [P, 2, 2])
        ht = sb("ht", [64, LEN])
        q = sb("q4", [P, LEN])
        k = sb("k4", [P, LEN])
        t1 = sb("t14", [P, LEN])
        t2 = sb("t24", [P, LEN])
        v = sb("v4", [P, 2, 32])
        mx = sb("mx4", [P, 2, 4])
        nm = sb("nm4", [P, 2, 4])
        sums = sb("sums4", [P, 2, 4])
        rsum = sb("rsum4", [P, 2, 4])
        E = sb("E4", [P, 4, 3 * P])
        ET = sb("ET4", [P, 3, 4, P])
        y = sb("y4", [P, 2, D])
        yt = sb("yt4", [64, LEN])
        ps_s = kit.ps(c, "ps_s", [P, 4, 512])
        ps_t = kit.ps(c, "ps_t4", [P, 2, 4, P])
        ps_a = kit.ps(c, "ps_a4", [P, 512])
        ps_b = kit.ps(c, "ps_b4", [P, 512])
        names = ("w_in var_ready rs_ready u_ready ht_done ht_out proj q_out k_out v_done v_out scores nm_ready "
                 "exps t_done t_outa t_outd y_done y_out yt_done yt_out o_done o_out mask_ready").split()
        s = {n: sem(n + "_4") for n in names}
        block = kit.block(c)
        SCALE = 16 ** -0.5

        @block.sync
        def _(sp):
            for dst, src in ((ident[:], a["ident"]), (maskf[:], a["causal"]), (wqkv[:], a["ffn_wqkv"]), (wo[:], a["ffn_wo"]),
                             (ln1[:], a["ffn_ln1"]), (rope[:], a["rope"])):
                sp.dma_start(dst, src).then_inc(s["w_in"], 16)
            sp.dma_start(H[:], h1.rearrange("s (two p) d -> p (s two) d", p=P)).then_inc(s["w_in"], 16)

        @block.gpsimd
        def _(pool):
            pool.memset(half[:], -0.5)
            pool.drain()

            def first(n):
                kit.hold(pool, s["var_ready"], n + 1)
                pool.tensor_tensor(rs[:], var[:], half[:], ALU.pow).then_inc(s["rs_ready"], 1)
            first(0)
            with pool.Fori(0, SEQ - 1) as b:
                first(b + 1)

        @block.vector
        def _(dve):
            dve.wait_ge(s["w_in"], 112)
            dve.tensor_copy(identb[:], ident[:])
            dve.tensor_copy(mask[:], maskf[:]).then_inc(s["mask_ready"], 1)

            def first(n):
                rows = H[:, bass.ds(n * 2, 2), :]
                norm_statistics(dve, rows, cen[:], sq[:], st)
                dve.tensor_scalar(var[:, 0], st[:, 2], 1.0 / D, LN_EPS, ALU.mult, ALU.add)
                dve.tensor_scalar(var[:, 1], st[:, 2], (1 + RMS_EPS) / D, RMS_EPS * LN_EPS, ALU.mult, ALU.add).then_inc(s["var_ready"], 1)
                kit.hold(dve, s["rs_ready"], n + 1)
                dve.tensor_tensor(u[:], cen[:], bcast(rs[:, 1], D), ALU.mult).then_inc(s["u_ready"], 1)
                dve.tensor_tensor(X2[:, bass.ds(n * 2, 2), :], cen[:], bcast(rs[:, 0], D), ALU.mult)
                rotate(q, s["q_out"], n * 2 + 1)
                return n

            def rotate(dst, out, count):
                kit.hold(dve, s["proj"], count)
                dve.tensor_tensor(t1[:], ps_a[:, 0:LEN], rope[:, 0], ALU.mult)
                dve.tensor_tensor(t2[:], ps_a[:, LEN:2 * LEN], rope[:, 1], ALU.mult)
                dve.drain()
                dve.tensor_tensor(dst[:], t1[:], t2[:], ALU.add).then_inc(out, 1)

            def second(b, first_of_next, n):
                kit.hold(dve, s["scores"], b + 1)
                dve.tensor_reduce(mx[:, 0], ps_s[:, :, 0:P], AX_X, ALU.max)
                dve.tensor_reduce(mx[:, 1], ps_s[:, :, LEN:2 * LEN], AX_X, ALU.max)
                dve.drain()
                dve.tensor_scalar(nm[:], mx[:], -SCALE, None, ALU.mult).then_inc(s["nm_ready"], 1)
                first_of_next()
                kit.hold(dve, s["t_done"], b * 3 + 2)
                dve.tensor_copy(ET[:, 1], ps_t[:, 1]).then_inc(s["t_outd"], 1)
                if n is not None:
                    rotate(k, s["k_out"], n * 2 + 2)
                kit.hold(dve, s["exps"], b + 1)
                dve.reciprocal(rsum[:], sums[:])
                dve.drain()
                kit.hold(dve, s["y_done"], b + 1)
                for t in range(2):
                    w = dve.tensor_tensor(y[:, t].rearrange("p (h c) -> p h c", h=4), ps_b[:, 64 * t:64 * t + 64].rearrange("p (h c) -> p h c", h=4),
                                          bcast(rsum[:, t], 16), ALU.mult)
                w.then_inc(s["y_out"], 1)
                kit.hold(dve, s["o_done"], b + 1)
                xx = X2[:, bass.ds(b * 2, 2), :]
                dve.tensor_tensor(xx, xx, ps_b[:, 384:512].rearrange("p (t d) -> p t d", t=2), ALU.add).then_inc(s["o_out"], 1)

            first(0)
            rotate(k, s["k_out"], 2)
            with dve.Fori(0, SEQ - 1) as b:
                second(b, lambda: first(b + 1), b + 1)
            second(SEQ - 1, lambda: None, None)

        @block.scalar
        def _(act):
            act.wait_ge(s["w_in"], 112)

            def transposed(n):
                kit.hold(act, s["ht_done"], n + 1)
                act.activation(ht[:], ps_a[0:64, 0:LEN], ACT.Copy, scale=ln1[:]).then_inc(s["ht_out"], 1)

            def values(n):
                kit.hold(act, s["v_done"], n + 1)
                act.activation(v[:].rearrange("p t c -> p (t c)"), ps_a[:, 0:64], ACT.Copy).then_inc(s["v_out"], 1)

            def second(b, n):
                kit.hold(act, s["nm_ready"], b + 1)
                for h in range(4):
                    act.activation(E[:, h, 0:P], ps_s[:, h, 0:P], ACT.Exp, bias=nm[:, 0, h:h + 1], scale=SCALE, accum_out=sums[:, 0, h:h + 1])
                    e = act.activation(E[:, h, P:3 * P], ps_s[:, h, LEN:2 * LEN], ACT.Exp, bias=nm[:, 1, h:h + 1], scale=SCALE,
                                       accum_out=sums[:, 1, h:h + 1])
                e.then_inc(s["exps"], 1)
                if n is not None:
                    transposed(n)
                for g in (0, 2):
                    kit.hold(act, s["t_done"], b * 3 + g + 1)
                    act.activation(ET[:, g], ps_t[:, 0], ACT.Copy).then_inc(s["t_outa"], 1)
                if n is not None:
                    values(n)
                kit.hold(act, s["yt_done"], b + 1)
                act.activation(yt[:], ps_b[0:64, P:3 * P], ACT.Copy).then_inc(s["yt_out"], 1)

            transposed(0)
            values(0)
            with act.Fori(0, SEQ - 1) as b:
                second(b, b + 1)
            second(SEQ - 1, None)

        @block.tensor
        def _(pe):
            pe.wait_ge(s["w_in"], 112)
            pe.wait_ge(s["mask_ready"], 1)

            def transposes(n):
                kit.hold(pe, s["u_ready"], n + 1)
                for t in range(2):
                    mm = pe.transpose(ps_a[0:64, P * t:P * t + P], u[:, t, :], ident[:])
                mm.then_inc(s["ht_done"], 1)

            def project(n, which):
                for j in range(2):
                    mm = pe.matmul(ps_a[:, LEN * j:LEN * j + LEN], wqkv[:, P * (2 * which + j):P * (2 * which + j) + P], ht[:], start=True, stop=True)
                mm.then_inc(s["proj"], 1)

            def values(n):
                kit.hold(pe, s["k_out"], n + 1)
                for t in range(2):
                    mm = pe.matmul(ps_a[:, 32 * t:32 * t + 32], ht[:, P * t:P * t + P], wqkv[:, 4 * P:4 * P + 32], start=True, stop=True)
                mm.then_inc(s["v_done"], 1)

            def turn(b, g):
                for h in range(4):
                    mm = pe.transpose(ps_t[:, g % 2, h, :], E[:, h, P * g:P * g + P], ident[:])
                mm.then_inc(s["t_done"], 1)

            def second(b, n):
                kit.hold(pe, s["k_out"], b + 1)
                for h in range(4):
                    r = slice(32 * h, 32 * h + 32)
                    skip = dict(skip_group_check=True)
                    pe.matmul(ps_s[:, h, 0:P], identb[:], mask[:], start=True, stop=False, **skip)
                    pe.matmul(ps_s[:, h, 3 * P:4 * P], identb[:], mask[:], start=False, stop=False, **skip)
                for h in range(4):
                    r = slice(32 * h, 32 * h + 32)
                    pe.matmul(ps_s[:, h, 0:P], q[r, 0:P], k[r, 0:P], start=False, stop=False, tile_position=(32 * h, 0), **skip)
                    mm = pe.matmul(ps_s[:, h, LEN:2 * LEN], q[r, P:LEN], k[r, :], start=False, stop=True, tile_position=(32 * h, 0), **skip)
                mm.then_inc(s["scores"], 1)
                if n is not None:
                    kit.hold(pe, s["v_out"], n)
                    transposes(n)
                    kit.hold(pe, s["ht_out"], n + 1)
                    project(n, 0)
                kit.hold(pe, s["exps"], b + 1)
                turn(b, 0)
                turn(b, 1)
                if n is not None:
                    kit.hold(pe, s["q_out"], n + 1)
                    project(n, 1)
                kit.hold(pe, s["t_outa"], b * 2 + 1)
                turn(b, 2)
                kit.hold(pe, s["t_outa"], b * 2 + 2)
                kit.hold(pe, s["t_outd"], b + 1)
                kit.hold(pe, s["v_out"], b + 1)
                for h in range(4):
                    kv = slice(16 * (h // 2), 16 * (h // 2) + 16)
                    pe.matmul(ps_b[:, 16 * h:16 * h + 16], ET[:, 0, h, :], v[:, 0, kv], start=(h == 0), stop=False, **skip)
                    pe.matmul(ps_b[:, 64 + 16 * h:80 + 16 * h], ET[:, 1, h, :], v[:, 0, kv], start=False, stop=False, **skip)
                    mm = pe.matmul(ps_b[:, 64 + 16 * h:80 + 16 * h], ET[:, 2, h, :], v[:, 1, kv], start=False, stop=(h == 3), **skip)
                mm.then_inc(s["y_done"], 1)
                if n is not None:
                    values(n)
                kit.hold(pe, s["y_out"], b + 1)
                for t in range(2):
                    mm = pe.transpose(ps_b[0:64, P + P * t:2 * P + P * t], y[:, t, :], ident[:])
                mm.then_inc(s["yt_done"], 1)
                kit.hold(pe, s["yt_out"], b + 1)
                for t in range(2):
                    mm = pe.matmul(ps_b[:, 384 + 64 * t:448 + 64 * t], yt[:, P * t:P * t + P], wo[:], start=True, stop=True)
                mm.then_inc(s["o_done"], 1)

            transposes(0)
            pe.wait_ge(s["ht_out"], 1)
            project(0, 0)
            pe.wait_ge(s["q_out"], 1)
            project(0, 1)
            values(0)
            with pe.Fori(0, SEQ - 1) as b:
                second(b, b + 1)
            second(SEQ - 1, None)


def dense_experts(nc, kit, a, H, X2):
    NE, HID = 8, 170
    ROWS = NE * HID
    CH = -(-ROWS // P)
    T = 4
    BLOCKS = TILES // T
    W = T * P
    size = [min(P, ROWS - P * j) for j in range(CH)]
    with ExitStack() as c:
        sb = lambda n, s, d=F32: kit.sb(c, n, s, d)
        sem = lambda n: kit.sem(c, n)
        ident = sb("ident5", [P, P])
        identb = sb("identb5", [P, P], BF16)
        w1 = sb("w1_5", [64, ROWS])
        w3 = sb("w3_5", [64, ROWS])
        w2 = sb("w2_5", [P, CH, D])
        wr = sb("wr_5", [64, NE])
        ln2 = sb("ln2", [64, 1])
        spreadf = sb("spreadf", [24, ROWS])
        spread = sb("spread", [24, ROWS], BF16)
        iota = sb("iota5", [P, T, NE])
        iotai = sb("iotai5", [P, T, NE], I32)
        sq = sb("sq5", [P, T, D])
        st = sb("st5", [P, T])
        var = sb("var5", [P, T])
        half = sb("half5", [P, T])
        rs = sb("rs5", [P, T])
        fl = sb("fl5", [P, T, D])
        flt = sb("flt", [64, 2, W])
        lg = sb("lg5", [P, T, NE])
        pr = sb("pr5", [P, T, NE])
        m = sb("m5", [P, 4, T])
        top = sb("top5", [P, T, 8])
        topi = sb("topi5", [P, T, 8], U32)
        topf = sb("topf5", [P, T, 8])
        hot = sb("hot5", [P, 2, T, NE])
        wt = sb("wt5", [P, T, NE])
        rest = sb("rest5", [P, 2, T, NE])
        w3b = sb("w3b", [P, T, 3, NE], BF16)
        wtt = sb("wtt", [24, 2, W], BF16)
        gate = sb("gate5", [P, 2, W])
        up = sb("up5", [P, 2, W])
        hid = sb("hid5", [P, 2, W])
        acc = sb("acc5", [P, T, D])
        ps_u = kit.ps(c, "ps_u", [P, 2, 2, W])
        ps_w = kit.ps(c, "ps_w", [P, W])
        ps_d = kit.ps(c, "ps_d", [P, 512])
        ps_r = kit.ps(c, "ps_r", [P, W])
        ps_x = kit.ps(c, "ps_x", [P, 1024], BF16)
        names = ("w_in ready var_ready rs_ready fl_ready flt_done flt_out router lg_ready exp_done w_ready wtt_done wtt_out "
                 "ups wide gated hidden down out").split()
        s = {n: sem(n + "_5") for n in names}
        block = kit.block(c)

        @block.sync
        def _(sp):
            for dst, src in ((ident[:], a["ident"]), (w1[:], a["moe0_w1"]), (w3[:], a["moe0_w3"]), (w2[:], a["moe0_w2"]),
                             (wr[:], a["moe0_wr"]), (ln2[:], a["ffn_ln2"]), (spreadf[:], a["moe0_spread"])):
                sp.dma_start(dst, src).then_inc(s["w_in"], 16)

        @block.gpsimd
        def _(pool):
            pool.memset(half[:], -0.5)
            pool.iota(iotai[:], pattern=[[0, T], [1, NE]], base=0, channel_multiplier=0).then_inc(s["ready"], 1)
            pool.drain()

            def first(n):
                kit.hold(pool, s["var_ready"], n + 1)
                pool.tensor_tensor(rs[:], var[:], half[:], ALU.pow).then_inc(s["rs_ready"], 1)
            first(0)
            with pool.Fori(0, BLOCKS - 1) as i:
                first(i + 1)

        @block.vector
        def _(dve):
            dve.wait_ge(s["w_in"], 112)
            dve.wait_ge(s["ready"], 1)
            dve.tensor_copy(identb[:], ident[:])
            dve.tensor_copy(spread[:], spreadf[:])
            dve.tensor_copy(iota[:], iotai[:]).then_inc(s["ready"], 1)
            dve.drain()

            def norm(n):
                x = X2[:, bass.ds(n * T, T), :]
                dve.tensor_tensor(sq[:], x, x, ALU.mult)
                dve.drain()
                dve.tensor_reduce(st[:], sq[:], AX_X, ALU.add)
                dve.drain()
                dve.tensor_scalar(var[:], st[:], 1.0 / D, RMS_EPS, ALU.mult, ALU.add).then_inc(s["var_ready"], 1)
                kit.hold(dve, s["rs_ready"], n + 1)
                dve.tensor_tensor(fl[:], x, bcast(rs[:], D), ALU.mult).then_inc(s["fl_ready"], 1)

            def shifted(n):
                kit.hold(dve, s["router"], n + 1)
                dve.tensor_copy(lg[:], ps_r[:, 0:T * NE].rearrange("p (t e) -> p t e", e=NE))
                dve.drain()
                dve.tensor_reduce(m[:, 0], lg[:], AX_X, ALU.max)
                dve.drain()
                dve.tensor_tensor(lg[:], lg[:], bcast(m[:, 0], NE), ALU.subtract).then_inc(s["lg_ready"], 1)

            def weights(n):
                kit.hold(dve, s["exp_done"], n + 1)
                dve.tensor_reduce(m[:, 1], pr[:], AX_X, ALU.add)
                dve.drain()
                dve.reciprocal(m[:, 2], m[:, 1])
                dve.drain()
                dve.tensor_tensor(pr[:], pr[:], bcast(m[:, 2], NE), ALU.mult)
                dve.drain()
                for t in range(T):
                    dve.max(top[:, t], pr[:, t])
                dve.drain()
                for t in range(T):
                    dve.max_index(topi[:, t], top[:, t], pr[:, t])
                dve.tensor_tensor(m[:, 1], top[:, :, 0], top[:, :, 1], ALU.add)
                dve.drain()
                dve.tensor_scalar(m[:, 2], m[:, 1], 1e-9, None, ALU.add)
                dve.tensor_copy(topf[:], topi[:])
                dve.drain()
                dve.reciprocal(m[:, 3], m[:, 2])
                for j in range(2):
                    dve.tensor_tensor(hot[:, j], iota[:], topf[:, :, j:j + 1].to_broadcast([P, T, NE]), ALU.is_equal)
                dve.drain()
                dve.tensor_tensor(hot[:, 0], hot[:, 0], hot[:, 1], ALU.add)
                dve.tensor_tensor(wt[:], pr[:], bcast(m[:, 3], NE), ALU.mult)
                dve.drain()
                dve.tensor_tensor(wt[:], wt[:], hot[:, 0], ALU.mult)
                dve.drain()
                dve.tensor_copy(w3b[:, :, 0], wt[:])
                dve.drain()
                dve.tensor_tensor(rest[:, 0], wt[:], w3b[:, :, 0], ALU.subtract)
                dve.drain()
                dve.tensor_copy(w3b[:, :, 1], rest[:, 0])
                dve.drain()
                dve.tensor_tensor(rest[:, 1], rest[:, 0], w3b[:, :, 1], ALU.subtract)
                dve.drain()
                dve.tensor_copy(w3b[:, :, 2], rest[:, 1]).then_inc(s["w_ready"], 1)

            def hidden(n, j):
                r = slice(0, size[j])
                kit.hold(dve, s["gated"], n * CH + j + 1)
                dve.tensor_tensor(up[r, j % 2], ps_u[r, j % 2, 1], gate[r, j % 2], ALU.mult)
                dve.drain()
                kit.hold(dve, s["wide"], n * CH + j + 1)
                dve.tensor_tensor(hid[r, j % 2], ps_w[r], up[r, j % 2], ALU.mult).then_inc(s["hidden"], 1)

            def block_of(i, n):
                for j in range(CH):
                    hidden(i, j)
                    if n is not None:
                        {0: norm, 3: shifted, 5: weights}.get(j, lambda n: None)(n)
                rows = H[:, bass.ds(i * T, T), :]
                dve.tensor_tensor(acc[:], X2[:, bass.ds(i * T, T), :], rows, ALU.add)
                dve.drain()
                kit.hold(dve, s["down"], i + 1)
                dve.tensor_tensor(rows, acc[:], ps_d[:, 0:T * D].rearrange("p (t d) -> p t d", t=T), ALU.add).then_inc(s["out"], 1)

            norm(0)
            shifted(0)
            weights(0)
            with dve.Fori(0, BLOCKS - 1) as i:
                block_of(i, i + 1)
            block_of(BLOCKS - 1, None)

        @block.scalar
        def _(act):
            act.wait_ge(s["w_in"], 112)

            def flat_at(n, b):
                kit.hold(act, s["flt_done"], n + 1)
                act.activation(flt[:, b], ps_r[0:64, :], ACT.Copy, scale=ln2[:]).then_inc(s["flt_out"], 1)

            def exps(n):
                kit.hold(act, s["lg_ready"], n + 1)
                act.activation(pr[:], lg[:], ACT.Exp).then_inc(s["exp_done"], 1)

            def turned(n, b):
                kit.hold(act, s["wtt_done"], n + 1)
                act.activation(wtt[:, b], ps_x[0:24, 0:W], ACT.Copy).then_inc(s["wtt_out"], 1)

            def block_of(i, n, b):
                for j in range(CH):
                    r = slice(0, size[j])
                    kit.hold(act, s["ups"], i * CH + j + 1)
                    act.activation(gate[r, j % 2], ps_u[r, j % 2, 0], ACT.Silu).then_inc(s["gated"], 1)
                    if n is not None:
                        if j == 1:
                            flat_at(n, b)
                        if j == 4:
                            exps(n)
                        if j == 8:
                            turned(n, b)

            flat_at(0, 0)
            exps(0)
            turned(0, 0)
            with act.Fori(0, BLOCKS // 2 - 1) as i:
                block_of(i * 2, i * 2 + 1, 1)
                block_of(i * 2 + 1, i * 2 + 2, 0)
            block_of(BLOCKS - 2, BLOCKS - 1, 1)
            block_of(BLOCKS - 1, None, None)

        @block.tensor
        def _(pe):
            pe.wait_ge(s["w_in"], 112)
            pe.wait_ge(s["ready"], 2)
            skip = dict(skip_group_check=True)

            def turn_rows(n):
                kit.hold(pe, s["fl_ready"], n + 1)
                for t in range(T):
                    mm = pe.transpose(ps_r[0:64, P * t:P * t + P], fl[:, t, :], ident[:])
                mm.then_inc(s["flt_done"], 1)

            def router(n, b):
                kit.hold(pe, s["flt_out"], n + 1)
                for t in range(T):
                    mm = pe.matmul(ps_r[:, NE * t:NE * t + NE], flt[:, b, P * t:P * t + P], wr[:], start=True, stop=True)
                mm.then_inc(s["router"], 1)

            def turn_weights(n):
                kit.hold(pe, s["w_ready"], n + 1)
                for t in range(T):
                    mm = pe.transpose(ps_x[0:24, P * t:P * t + P], w3b[:, t].rearrange("p k e -> p (k e)"), identb[:])
                mm.then_inc(s["wtt_done"], 1)

            def ups(i, j, b):
                r = slice(0, size[j])
                cols = slice(P * j, P * j + size[j])
                pe.matmul(ps_u[r, j % 2, 0], w1[:, cols], flt[:, b], start=True, stop=True)
                pe.matmul(ps_u[r, j % 2, 1], w3[:, cols], flt[:, b], start=True, stop=True).then_inc(s["ups"], 1)

            def wide(i, j, b):
                r = slice(0, size[j])
                pe.matmul(ps_w[r], spread[:, P * j:P * j + size[j]], wtt[:, b], start=True, stop=True).then_inc(s["wide"], 1)

            def block_of(i, n, b):
                kit.hold(pe, s["wtt_out"], i + 1)
                ups(i, 0, b)
                wide(i, 0, b)
                for j in range(CH):
                    if j + 1 < CH:
                        ups(i, j + 1, b)
                    kit.hold(pe, s["hidden"], i * CH + j + 1)
                    if j + 1 < CH:
                        wide(i, j + 1, b)
                    r = slice(0, size[j])
                    for t in range(T):
                        mm = pe.matmul(ps_d[:, D * t:D * t + D], hid[r, j % 2, P * t:P * t + P], w2[r, j, :],
                                       start=(j == 0 and t == 0), stop=(j == CH - 1 and t == T - 1), **skip)
                    if n is not None:
                        if j == 1:
                            turn_rows(n)
                        if j == 2:
                            router(n, 1 - b)
                        if j == 8:
                            turn_weights(n)
                mm.then_inc(s["down"], 1)

            turn_rows(0)
            router(0, 0)
            turn_weights(0)
            with pe.Fori(0, BLOCKS // 2 - 1) as i:
                block_of(i * 2, i * 2 + 1, 0)
                block_of(i * 2 + 1, i * 2 + 2, 1)
            block_of(BLOCKS - 2, BLOCKS - 1, 0)
            block_of(BLOCKS - 1, None, 1)


def store_rows(nc, kit, H, dram, name):
    with ExitStack() as c:
        stored = kit.sem(c, "stored_" + name)
        block = kit.block(c)

        @block.sync
        def _(sp):
            sp.dma_start(dram.rearrange("s (two p) d -> p (s two) d", p=P), H[:]).then_inc(stored, 16)
            sp.wait_ge(stored, 16)


UNDERFLOW = -104.0


def mamba(nc, kit, a, H, bc_dram):
    CHUNKS, SC = 8, 8
    STEPS = SC // 2
    W = 2 * LEN
    CW = SC * LEN
    NS, DI, RANK = 64, 128, 16
    with ExitStack() as c:
        sb = lambda n, s, d=F32: kit.sb(c, n, s, d)
        sem = lambda n: kit.sem(c, n)
        ident = sb("ident6", [P, P])
        w_in = sb("w_in6w", [D, 2 * DI])
        w_x = sb("w_x6", [DI, RANK + 2 * NS])
        w_dt = sb("w_dt6", [RANK, DI])
        w_out = sb("w_out6", [DI, D])
        chan = sb("chan6", [DI, 7])
        A = sb("A6", [DI, NS])
        before = sb("before6", [NS, NS])
        slots = sb("slots6", [NS, NS])
        slots_i = sb("slots_i6", [NS, NS], I32)
        index = sb("index6", [NS, 1])
        index_i = sb("index_i6", [NS, 1], I32)
        half = sb("half6", [P, 4])
        keep = sb("keep6", [P, SC, LEN])
        cen = sb("cen6", [P, 4, D])
        sq = sb("sq6", [P, 4, D])
        st = sb("st6", [P, 3, 4])
        var = sb("var6", [P, 4])
        rs = sb("rs6", [P, 4])
        x = sb("x6", [P, 4, D])
        xt = sb("xt6", [D, W])
        xpad = sb("xpad6", [DI, 2, LEN + 3])
        conv = sb("conv6", [DI, 2, LEN])
        u = sb("u6", [DI, W])
        dl = sb("dl6", [RANK, W])
        bc = sb("bc6", [NS, 2, 2, LEN])
        az = sb("az6", [DI, W])
        ey = sb("ey6", [DI, W])
        lw = sb("lw6", [DI, W])
        rl = sb("rl6", [DI, W])
        delta = sb("delta6", [DI, 2, LEN])
        later = sb("later6", [DI, 2, LEN])
        S = sb("S6", [DI, SC, LEN])
        DU = sb("DU6", [DI, SC, LEN])
        Y = sb("Y6", [DI, SC, LEN])
        Gt = sb("G6", [DI, SC, LEN])
        last = sb("last6", [NS, 2, SC])
        least = sb("least6", [DI, 1])
        cand = sb("cand6", [DI, NS])
        flag = sb("flag6", [NS, 4])
        place = sb("place6", [NS, NS])
        dead = sb("dead6", [NS, DI])
        lastbc = sb("lastbc6", [NS, SC])
        tail = sb("tail6", [DI, SC])
        todo = sb("todo6", [1, NS + 2])
        todo_i = sb("todo_i6", [1, NS + 2], I32)
        acol = sb("acol6", [DI, 1])
        tiny = sb("tiny6", [DI, 1])
        Bb = sb("Bb6", [DI, SC, LEN])
        Cb = sb("Cb6", [DI, SC, LEN])
        e = sb("e6", [DI, SC, LEN])
        r = sb("r6", [DI, SC, LEN])
        t = sb("t6", [DI, SC, LEN])
        yg = sb("yg6", [DI, W])
        ps_x = kit.ps(c, "ps_x6", [P, W])
        ps_i = kit.ps(c, "ps_i6", [P, W])
        ps_g = kit.ps(c, "ps_g6", [P, W])
        ps_b = kit.ps(c, "ps_b6", [P, W])
        ps_c = kit.ps(c, "ps_c6", [P, W])
        ps_f = kit.ps(c, "ps_f6", [P, W])
        ps_o = kit.ps(c, "ps_o6", [P, W])
        names = ("w_in consts var_ready rs_ready x_ready xt_done xt_out in_done xi_out conv_ready u_ready dl_done dl_out dt_done "
                 "bc_done bc_out bc_stored ey_ready lw_ready cand_ready cand_done flag_ready rank_done place_ready list_done "
                 "todo_ready acol_ready e_ready r_ready bc_in bc_free scanned yg_ready o_done h_out g_ready").split()
        s = {n: sem(n + "_6") for n in names}
        block = kit.block(c)

        def flat(ap):
            return ap.rearrange("p a l -> p (a l)")

        @block.sync
        def _(sp):
            for dst, src in ((ident[:], a["ident"]), (w_in[:], a["mb_win"]), (w_x[:], a["mb_wx"]), (w_dt[:], a["mb_wdt"]),
                             (w_out[:], a["mb_wout"]), (chan[:], a["mb_chan"]), (A[:], a["mb_alog"]), (before[:], a["before"])):
                sp.dma_start(dst, src).then_inc(s["w_in"], 16)
            with sp.Fori(0, CHUNKS) as ch:
                with sp.Fori(0, STEPS) as i:
                    n = ch * STEPS + i
                    kit.hold(sp, s["bc_out"], n + 1)
                    sp.dma_start(bc_dram.rearrange("k n (g w) -> g n k w", w=W)[bass.ds(n, 1), :, :, :].rearrange("g n k w -> (g n) k w"),
                                 bc[:].rearrange("n k a l -> n k (a l)")).then_inc(s["bc_stored"], 16)
                kit.hold(sp, s["bc_stored"], (ch + 1) * (16 * STEPS) + 16)
                kit.hold(sp, s["todo_ready"], ch + 1)
                count = sp.value_load(todo_i[0:1, NS:NS + 1], min_val=0, max_val=NS)
                done = sp.value_load(todo_i[0:1, NS + 1:NS + 2], min_val=0, max_val=NS * CHUNKS)
                with sp.Fori(0, NS) as k:
                    with sp.If(k < count):
                        state = sp.value_load(todo_i[0:1, bass.ds(k, 1)], min_val=0, max_val=NS - 1)
                        kit.hold(sp, s["bc_free"], done + k + 1)
                        for j, dst in ((0, Bb), (1, Cb)):
                            row = bc_dram[j, bass.ds(state, 1), bass.ds(ch * CW, CW)]
                            sp.dma_start(flat(dst[:]), row.to_broadcast([DI, CW])).then_inc(s["bc_in"], 16)

        @block.gpsimd
        def _(pool):
            pool.memset(half[:], -0.5)
            pool.iota(slots_i[:], pattern=[[1, NS]], base=0, channel_multiplier=0)
            pool.iota(index_i[:], pattern=[[0, 1]], base=0, channel_multiplier=1).then_inc(s["consts"], 1)
            pool.drain()
            with pool.Fori(0, CHUNKS * STEPS) as n:
                kit.hold(pool, s["var_ready"], n + 1)
                pool.tensor_tensor(rs[:], var[:], half[:], ALU.pow).then_inc(s["rs_ready"], 1)

        @block.scalar
        def _(act):
            act.wait_ge(s["w_in"], 128)
            act.wait_ge(s["consts"], 2)
            act.activation(A[:], A[:], ACT.Exp).then_inc(s["consts"], 1)
            with act.Fori(0, CHUNKS) as ch:
                with act.Fori(0, STEPS) as i:
                    n = ch * STEPS + i
                    kit.hold(act, s["xt_done"], n + 1)
                    act.activation(xt[:], ps_x[0:D, :], ACT.Copy).then_inc(s["xt_out"], 1)
                    kit.hold(act, s["in_done"], n + 1)
                    act.activation(xpad[:, :, 3:LEN + 3], ps_i[:].rearrange("p (a l) -> p a l", a=2), ACT.Copy).then_inc(s["xi_out"], 1)
                    act.activation(Gt[:, bass.ds(i * 2, 2), :], ps_g[:].rearrange("p (a l) -> p a l", a=2), ACT.Silu).then_inc(s["g_ready"], 1)
                    kit.hold(act, s["conv_ready"], n + 1)
                    act.activation(u[:], flat(conv[:]), ACT.Silu, bias=chan[:, 4:5]).then_inc(s["u_ready"], 1)
                    kit.hold(act, s["dl_done"], n + 1)
                    act.activation(dl[:], ps_x[0:RANK, :], ACT.Copy).then_inc(s["dl_out"], 1)
                    kit.hold(act, s["bc_done"], n + 1)
                    kit.hold(act, s["bc_stored"], n * 16 + 16)
                    act.activation(bc[:, 0], ps_b[0:NS, :].rearrange("p (a l) -> p a l", a=2), ACT.Copy)
                    act.activation(bc[:, 1], ps_c[0:NS, :].rearrange("p (a l) -> p a l", a=2), ACT.Copy).then_inc(s["bc_out"], 1)
                    kit.hold(act, s["dt_done"], n + 1)
                    act.activation(az[:], ps_i[:], ACT.Abs, bias=chan[:, 5:6])
                    act.drain()
                    act.activation(ey[:], az[:], ACT.Exp, scale=-1.0).then_inc(s["ey_ready"], 1)
                    act.drain()
                    act.activation(lw[:], ey[:], ACT.Ln, bias=1.0).then_inc(s["lw_ready"], 1)
                kit.hold(act, s["todo_ready"], ch + 1)
                count = act.value_load(todo_i[0:1, NS:NS + 1], min_val=0, max_val=NS)
                done = act.value_load(todo_i[0:1, NS + 1:NS + 2], min_val=0, max_val=NS * CHUNKS)
                with act.Fori(0, NS) as k:
                    with act.If(k < count):
                        kit.hold(act, s["acol_ready"], done + k + 1)
                        act.activation(e[:], S[:], ACT.Exp, scale=acol[:]).then_inc(s["e_ready"], 1)
                        act.drain()
                        act.activation(r[:], e[:], ACT.Ln, bias=tiny[:])
                        act.drain()
                        act.activation(r[:], r[:], ACT.Exp, scale=-1.0).then_inc(s["r_ready"], 1)

        @block.vector
        def _(dve):
            dve.sem_inc(s["bc_stored"], 16)
            dve.sem_inc(s["bc_free"], 1)
            dve.memset(xpad[:], 0.0)
            dve.memset(later[:], 0.0)
            dve.memset(tiny[:], 1e-12)
            dve.memset(todo[:], 0.0)
            dve.memset(keep[:], 1.0)
            dve.drain()
            dve.memset(keep[:, :, 0:1], 0.0).then_inc(s["consts"], 1)
            dve.wait_ge(s["w_in"], 128)
            dve.wait_ge(s["consts"], 3)
            dve.tensor_scalar(A[:], A[:], -1.0, None, ALU.mult)
            dve.tensor_copy(slots[:], slots_i[:])
            dve.tensor_copy(index[:], index_i[:])
            dve.drain()
            with dve.Fori(0, CHUNKS) as ch:
                with dve.Fori(0, STEPS) as i:
                    n = ch * STEPS + i
                    norm_statistics(dve, H[:, bass.ds(n * 4, 4), :], cen[:], sq[:], st)
                    dve.tensor_scalar(var[:], st[:, 2], 1.0 / D, LN_EPS, ALU.mult, ALU.add).then_inc(s["var_ready"], 1)
                    kit.hold(dve, s["rs_ready"], n + 1)
                    dve.tensor_tensor(x[:], cen[:], bcast(rs[:], D), ALU.mult).then_inc(s["x_ready"], 1)
                    kit.hold(dve, s["xi_out"], n + 1)
                    dve.tensor_scalar(conv[:], xpad[:, :, 0:LEN], chan[:, 0:1], None, ALU.mult)
                    for tap in range(1, 4):
                        dve.drain()
                        w = dve.scalar_tensor_tensor(conv[:], xpad[:, :, tap:tap + LEN], chan[:, tap:tap + 1], conv[:], ALU.mult, ALU.add)
                    w.then_inc(s["conv_ready"], 1)
                    kit.hold(dve, s["ey_ready"], n + 1)
                    dve.tensor_scalar(rl[:], ps_i[:], chan[:, 5:6], 0.0, ALU.add, ALU.max)
                    dve.tensor_scalar(az[:], ey[:], 1.0, -1.0, ALU.add, ALU.add)
                    dve.drain()
                    dve.tensor_tensor(az[:], ey[:], az[:], ALU.subtract)
                    dve.drain()
                    dve.tensor_tensor(az[:], az[:], rl[:], ALU.add)
                    dve.drain()
                    kit.hold(dve, s["lw_ready"], n + 1)
                    dve.tensor_tensor(flat(delta[:]), az[:], lw[:], ALU.add)
                    dve.drain()
                    uu = u[:].rearrange("p (a l) -> p a l", a=2)
                    dve.tensor_tensor(DU[:, bass.ds(i * 2, 2), :], delta[:], uu, ALU.mult)
                    dve.tensor_scalar(Y[:, bass.ds(i * 2, 2), :], uu, chan[:, 6:7], None, ALU.mult)
                    for j in range(2):
                        dve.tensor_tensor_scan(later[:, j, LEN - 2::-1], keep[:, 0, 1:LEN], delta[:, j, :0:-1], 0.0, ALU.mult, ALU.add)
                    dve.drain()
                    dve.tensor_copy(S[:, bass.ds(i * 2, 2), :], later[:])
                    kit.hold(dve, s["bc_out"], n + 1)
                    for j in range(2):
                        dve.tensor_copy(last[:, j, bass.ds(i * 2, 2)], bc[:, j, :, LEN - 1])
                dve.drain()
                dve.tensor_reduce(least[:], S[:, :, LEN - 2], AX_X, ALU.min)
                dve.drain()
                dve.tensor_scalar(cand[:], A[:], least[:], None, ALU.mult).then_inc(s["cand_ready"], 1)
                kit.hold(dve, s["cand_done"], ch + 1)
                dve.tensor_reduce(flag[:, 0:1], ps_f[0:NS, 0:DI], AX_X, ALU.max)
                dve.drain()
                dve.tensor_scalar(flag[:, 2:3], flag[:, 0:1], UNDERFLOW, None, ALU.is_lt)
                dve.drain()
                dve.tensor_scalar(flag[:, 1:2], flag[:, 2:3], -1.0, 1.0, ALU.mult, ALU.add)
                dve.tensor_tensor(lastbc[:], last[:, 0], last[:, 1], ALU.mult)
                dve.tensor_copy(dead[:], flag[:, 2:3].to_broadcast([NS, DI])).then_inc(s["flag_ready"], 1)
                kit.hold(dve, s["rank_done"], ch + 1)
                dve.tensor_copy(flag[:, 3:4], ps_f[0:NS, 128:129])
                dve.tensor_tensor(tail[:], ps_f[:, 192:192 + SC], DU[:, :, LEN - 1], ALU.mult)
                dve.drain()
                dve.tensor_scalar(place[:], slots[:], flag[:, 3:4], flag[:, 1:2], ALU.is_equal, ALU.mult).then_inc(s["place_ready"], 1)
                dve.tensor_tensor(Y[:, :, LEN - 1], Y[:, :, LEN - 1], tail[:], ALU.add)
                dve.tensor_tensor(todo[:, NS + 1:NS + 2], todo[:, NS + 1:NS + 2], todo[:, NS:NS + 1], ALU.add)
                dve.drain()
                kit.hold(dve, s["list_done"], ch + 1)
                dve.tensor_copy(todo[:, 0:NS + 1], ps_f[0:1, 256:256 + NS + 1])
                dve.drain()
                dve.tensor_copy(todo_i[:], todo[:]).then_inc(s["todo_ready"], 1)
                kit.hold(dve, s["todo_ready"], ch + 1)
                count = dve.value_load(todo_i[0:1, NS:NS + 1], min_val=0, max_val=NS)
                done = dve.value_load(todo_i[0:1, NS + 1:NS + 2], min_val=0, max_val=NS * CHUNKS)
                with dve.Fori(0, NS) as k:
                    with dve.If(k < count):
                        state = dve.value_load(todo_i[0:1, bass.ds(k, 1)], min_val=0, max_val=NS - 1)
                        dve.tensor_copy(acol[:], A[:, bass.ds(state, 1)]).then_inc(s["acol_ready"], 1)
                        kit.hold(dve, s["bc_in"], (done + k + 1) * 32)
                        dve.tensor_tensor(t[:], DU[:], Bb[:], ALU.mult)
                        dve.drain()
                        kit.hold(dve, s["e_ready"], done + k + 1)
                        dve.tensor_tensor(t[:], t[:], e[:], ALU.mult)
                        dve.drain()
                        dve.tensor_tensor_scan(flat(t[:]), flat(keep[:]), flat(t[:]), 0.0, ALU.mult, ALU.add)
                        dve.drain()
                        kit.hold(dve, s["r_ready"], done + k + 1)
                        dve.tensor_tensor(t[:], t[:], r[:], ALU.mult)
                        dve.drain()
                        dve.tensor_tensor(t[:], t[:], Cb[:], ALU.mult).then_inc(s["bc_free"], 1)
                        dve.drain()
                        dve.tensor_tensor(Y[:], Y[:], t[:], ALU.add)
                        dve.drain()
                kit.hold(dve, s["g_ready"], (ch + 1) * STEPS)
                with dve.Fori(0, STEPS) as i:
                    n = ch * STEPS + i
                    dve.tensor_tensor(yg[:].rearrange("p (a l) -> p a l", a=2), Y[:, bass.ds(i * 2, 2), :], Gt[:, bass.ds(i * 2, 2), :], ALU.mult).then_inc(s["yg_ready"], 1)
                    kit.hold(dve, s["o_done"], n + 1)
                    rows = H[:, bass.ds(n * 4, 4), :]
                    dve.tensor_tensor(rows, rows, ps_o[:, 0:4 * D].rearrange("p (t d) -> p t d", t=4), ALU.add).then_inc(s["h_out"], 1)
                    dve.drain()

        @block.tensor
        def _(pe):
            pe.wait_ge(s["w_in"], 128)
            pe.wait_ge(s["consts"], 3)
            with pe.Fori(0, CHUNKS) as ch:
                with pe.Fori(0, STEPS) as i:
                    n = ch * STEPS + i
                    kit.hold(pe, s["x_ready"], n + 1)
                    for t4 in range(4):
                        mm = pe.transpose(ps_x[0:D, P * t4:P * t4 + P], x[:, t4, :], ident[:])
                    mm.then_inc(s["xt_done"], 1)
                    kit.hold(pe, s["xt_out"], n + 1)
                    pe.matmul(ps_i[:], w_in[:, 0:DI], xt[:], start=True, stop=True)
                    pe.matmul(ps_g[:], w_in[:, DI:2 * DI], xt[:], start=True, stop=True).then_inc(s["in_done"], 1)
                    kit.hold(pe, s["u_ready"], n + 1)
                    pe.matmul(ps_x[0:RANK, :], w_x[:, 0:RANK], u[:], start=True, stop=True).then_inc(s["dl_done"], 1)
                    pe.matmul(ps_b[0:NS, :], w_x[:, RANK:RANK + NS], u[:], start=True, stop=True)
                    pe.matmul(ps_c[0:NS, :], w_x[:, RANK + NS:RANK + 2 * NS], u[:], start=True, stop=True).then_inc(s["bc_done"], 1)
                    kit.hold(pe, s["dl_out"], n + 1)
                    pe.matmul(ps_i[:], w_dt[:], dl[:], start=True, stop=True).then_inc(s["dt_done"], 1)
                kit.hold(pe, s["cand_ready"], ch + 1)
                pe.transpose(ps_f[0:NS, 0:DI], cand[:], ident[:]).then_inc(s["cand_done"], 1)
                kit.hold(pe, s["flag_ready"], ch + 1)
                pe.matmul(ps_f[0:NS, 128:129], before[:], flag[:, 1:2], start=True, stop=True)
                pe.matmul(ps_f[:, 192:192 + SC], dead[:], lastbc[:], start=True, stop=True).then_inc(s["rank_done"], 1)
                kit.hold(pe, s["place_ready"], ch + 1)
                pe.matmul(ps_f[0:1, 256:256 + NS], index[:], place[:], start=True, stop=True)
                pe.matmul(ps_f[0:1, 256 + NS:257 + NS], flag[:, 1:2], flag[:, 1:2], start=True, stop=True).then_inc(s["list_done"], 1)
                with pe.Fori(0, STEPS) as i:
                    n = ch * STEPS + i
                    kit.hold(pe, s["yg_ready"], n + 1)
                    for t4 in range(4):
                        mm = pe.matmul(ps_o[:, D * t4:D * t4 + D], yg[:, P * t4:P * t4 + P], w_out[:], start=True, stop=True)
                    mm.then_inc(s["o_done"], 1)



def sparse_experts(nc, kit, a, H, out):
    NE, HID = 64, 128
    SLOTS = 2 * TILES + NE
    with ExitStack() as top:
        GATE = kit.sb(top, "GATE", [P, 2, TILES])
        SLOT = kit.sb(top, "SLOT", [P, 2, TILES], U32)
        OWNER = kit.sb(top, "OWNER", [1, SLOTS], I32)
        xs = nc.dram_tensor("xs_dram", (SLOTS * P, D), F32).ap()
        ys = nc.dram_tensor("ys_dram", (SLOTS * P, D), F32).ap()
        route_and_scatter(nc, kit, a, H, GATE, SLOT, OWNER, xs, SLOTS)
        run_experts(nc, kit, a, OWNER, xs, ys, SLOTS)
        combine(nc, kit, H, GATE, SLOT, ys, out)


def route_and_scatter(nc, kit, a, H, GATE, SLOT, OWNER, xs, SLOTS):
    NE, T = 64, 4
    STEPS = TILES // T
    G = 8
    Z = 2048
    with ExitStack() as c:
        sb = lambda n, s, d=F32: kit.sb(c, n, s, d)
        sem = lambda n: kit.sem(c, n)
        X = sb("X9", [P, TILES, D])
        ident = sb("ident9", [P, P])
        wr = sb("wr9", [D + 1, NE])
        prior_f = sb("prior_f9", [P, P])
        prior = sb("prior9", [P, P], BF16)
        ones = sb("ones9", [P, P], BF16)
        onesf = sb("onesf9", [P, P])
        zero = sb("zero9", [P, Z])
        iota_i = sb("iota_i9", [P, G, NE], I32)
        iota = sb("iota9", [P, G, NE])
        thr_i = sb("thr_i9", [P, 1], I32)
        thr = sb("thr9", [P, 1])
        kth_i = sb("kth_i9", [NE, SLOTS], I32)
        kth = sb("kth9", [NE, SLOTS])
        half = sb("half9", [P, T])
        cen = sb("cen9", [P, T, D])
        sq = sb("sq9", [P, T, D])
        st = sb("st9", [P, 3, T])
        var = sb("var9", [P, T])
        rs = sb("rs9", [P, T])
        x = sb("x9", [P, T, D])
        xt = sb("xt9", [D + 1, T * P])
        lg = sb("lg9", [P, T, NE])
        top = sb("top9", [P, T, 8])
        topi = sb("topi9", [P, T, 8], U32)
        hot = sb("hot9", [P, 2, T, NE])
        both = sb("both9", [P, T, NE], BF16)
        mt = sb("mt9", [P, 2, T, NE])
        seen = sb("seen9", [P, NE])
        seen_add = sb("seen_add9", [P, NE])
        seen_b = sb("seen_b9", [P, NE], BF16)
        L1 = sb("L1_9", [P, 2, TILES])
        IDX = sb("IDX9", [P, 2, TILES])
        RANK = sb("RANK9", [P, 2, TILES])
        total = sb("total9", [P, NE])
        full = sb("full9", [P, NE])
        tiles = sb("tiles9", [P, NE])
        end = sb("end9", [P, NE])
        base = sb("base9", [P, NE])
        endc = sb("endc9", [NE, 1])
        past = sb("past9", [NE, SLOTS])
        own = sb("own9", [1, SLOTS])
        big = sb("big9", [P, G, NE])
        off = sb("off9", [P, G])
        rows = sb("rows9", [P, 2, G, D])
        slot_now = sb("slot_now9", [P, 2, 2, G], U32)
        ps_x = kit.ps(c, "ps_x9", [P, T * P])
        ps_l = kit.ps(c, "ps_l9", [P, 512])
        ps_r = kit.ps(c, "ps_r9", [P, 512])
        ps_m = kit.ps(c, "ps_m9", [P, 512])
        names = ("w_in consts ready var_ready rs_ready x_ready xt_done xt_out l_done both_ready r_done seen_ready cleared "
                 "total_done full_ready tiles_done end_ready endc_done past_ready own_done diff_ready exp_done slots_ready rows_ready "
                 ).split()
        s = {n: sem(n + "_9") for n in names}
        s["scattered"] = [sem("scattered0_9"), sem("scattered1_9")]
        block = kit.block(c)

        @block.sync
        def _(sp):
            for dst, src in ((ident[:], a["ident"]), (wr[:], a["moe1_wr"]), (prior_f[:], a["prior"])):
                sp.dma_start(dst, src).then_inc(s["w_in"], 16)
            sp.wait_ge(s["ready"], 1)
            per = P * Z // D
            for j in range(SLOTS * P // per):
                sp.dma_start(xs[j * per:(j + 1) * per, :].rearrange("(p r) d -> p (r d)", p=P), zero[:]).then_inc(s["cleared"], 16)

        @block.gpsimd
        def _(pool):
            pool.memset(half[:], -0.5)
            pool.iota(iota_i[:], pattern=[[0, G], [1, NE]], base=0, channel_multiplier=0)
            pool.iota(thr_i[:], pattern=[[0, 1]], base=0, channel_multiplier=P)
            pool.iota(kth_i[:], pattern=[[1, SLOTS]], base=0, channel_multiplier=0).then_inc(s["consts"], 1)
            pool.drain()
            with pool.Fori(0, STEPS) as n:
                kit.hold(pool, s["var_ready"], n + 1)
                pool.tensor_tensor(rs[:], var[:], half[:], ALU.pow).then_inc(s["rs_ready"], 1)
            pool.wait_ge(s["cleared"], 16 * (SLOTS * D // Z))
            with pool.Fori(0, TILES // G // 2) as i:
                for b in range(2):
                    n = i * 2 + b
                    kit.hold(pool, s["rows_ready"], n + 1)
                    pool.tensor_copy(slot_now[:, b], SLOT[:, :, bass.ds(n * G, G)])
                    pool.drain()
                    for t in range(G):
                        for j in range(2):
                            pool.indirect_dma_start(xs, bass.IndirectOffsetOnAxis(ap=slot_now[:, b, j, t:t + 1], axis=0),
                                                    rows[:, b, t, :], None).then_inc(s["scattered"][b], 16)
            for b in range(2):
                pool.wait_ge(s["scattered"][b], 16 * TILES)

        @block.scalar
        def _(act):
            act.wait_ge(s["ready"], 1)
            with act.Fori(0, STEPS) as n:
                kit.hold(act, s["xt_done"], n + 1)
                act.activation(xt[0:D, :], ps_x[0:D, :], ACT.Copy).then_inc(s["xt_out"], 1)
            act.wait_ge(s["diff_ready"], 1)
            act.activation(GATE[:, 1], GATE[:, 1], ACT.Exp).then_inc(s["exp_done"], 1)

        @block.vector
        def _(dve):
            dve.memset(zero[:], 0.0)
            dve.memset(xt[D:D + 1, :], 1.0)
            dve.memset(seen[:], 0.0)
            dve.memset(ones[:], 1.0)
            dve.memset(onesf[:], 1.0)
            dve.memset(seen_b[:], 0.0)
            dve.drain().then_inc(s["ready"], 1)
            dve.wait_ge(s["w_in"], 48)
            dve.wait_ge(s["consts"], 1)
            dve.tensor_copy(prior[:], prior_f[:])
            dve.tensor_copy(iota[:], iota_i[:])
            dve.tensor_copy(thr[:], thr_i[:])
            dve.tensor_copy(kth[:], kth_i[:])
            dve.drain().then_inc(s["ready"], 1)
            with dve.Fori(0, STEPS) as n:
                here = bass.ds(n * T, T)
                norm_statistics(dve, H[:, here, :], cen[:], sq[:], st)
                dve.tensor_scalar(var[:], st[:, 2], 1.0 / D, LN_EPS, ALU.mult, ALU.add).then_inc(s["var_ready"], 1)
                kit.hold(dve, s["rs_ready"], n + 1)
                dve.tensor_tensor(x[:], cen[:], bcast(rs[:], D), ALU.mult).then_inc(s["x_ready"], 1)
                dve.drain()
                dve.tensor_copy(X[:, here, :], x[:])
                kit.hold(dve, s["l_done"], n + 1)
                dve.tensor_copy(lg[:], ps_l[:, 0:T * NE].rearrange("p (t e) -> p t e", e=NE))
                dve.drain()
                for t in range(T):
                    dve.max(top[:, t], lg[:, t])
                dve.drain()
                for t in range(T):
                    dve.max_index(topi[:, t], top[:, t], lg[:, t])
                dve.tensor_copy(L1[:, :, here].rearrange("p j t -> p t j"), top[:, :, 0:2])
                dve.drain()
                dve.tensor_copy(IDX[:, :, here].rearrange("p j t -> p t j"), topi[:, :, 0:2])
                dve.drain()
                for j in range(2):
                    dve.tensor_tensor(hot[:, j], iota[:, 0:T], bcast(IDX[:, j, here], NE), ALU.is_equal)
                dve.drain()
                dve.tensor_tensor(both[:], hot[:, 0], hot[:, 1], ALU.add).then_inc(s["both_ready"], 1)
                dve.drain()
                dve.tensor_reduce(seen_add[:], both[:].rearrange("p t e -> p e t"), AX_X, ALU.add)
                kit.hold(dve, s["r_done"], n + 1)
                for j in range(2):
                    dve.tensor_tensor(mt[:, j], ps_r[:, 0:T * NE].rearrange("p (t e) -> p t e", e=NE), hot[:, j], ALU.mult)
                dve.drain()
                for j in range(2):
                    dve.tensor_reduce(RANK[:, j, here], mt[:, j], AX_X, ALU.add)
                dve.tensor_tensor(seen[:], seen[:], seen_add[:], ALU.add)
                dve.drain()
                dve.tensor_copy(seen_b[:], seen[:]).then_inc(s["seen_ready"], 1)
            dve.drain()
            dve.tensor_tensor(GATE[:, 1], L1[:, 1], L1[:, 0], ALU.subtract).then_inc(s["diff_ready"], 1)
            dve.wait_ge(s["total_done"], 1)
            dve.tensor_copy(total[:], ps_m[:, 0:NE])
            dve.drain()
            dve.tensor_scalar(full[:], total[:], thr[:], None, ALU.is_gt).then_inc(s["full_ready"], 1)
            dve.wait_ge(s["tiles_done"], 1)
            dve.tensor_copy(tiles[:], ps_m[:, NE:2 * NE])
            dve.drain()
            dve.tensor_tensor_scan(end[:], onesf[:, 0:NE], tiles[:], 0.0, ALU.mult, ALU.add).then_inc(s["end_ready"], 1)
            dve.drain()
            dve.tensor_tensor(base[:], end[:], tiles[:], ALU.subtract)
            dve.drain()
            dve.tensor_scalar(base[:], base[:], float(P), None, ALU.mult)
            dve.wait_ge(s["endc_done"], 1)
            dve.tensor_copy(endc[:], ps_m[0:NE, 128:129])
            dve.drain()
            dve.tensor_scalar(past[:], kth[:], endc[:], None, ALU.is_ge).then_inc(s["past_ready"], 1)
            dve.wait_ge(s["own_done"], 1)
            dve.tensor_scalar(own[:], ps_l[0:1, 0:SLOTS], float(NE - 1), None, ALU.min)
            dve.drain()
            dve.tensor_copy(OWNER[:], own[:])
            dve.wait_ge(s["exp_done"], 1)
            dve.tensor_scalar(L1[:, 0], GATE[:, 1], 1.0, None, ALU.add)
            dve.drain()
            dve.reciprocal(GATE[:, 0], L1[:, 0])
            dve.drain()
            dve.tensor_tensor(GATE[:, 1], GATE[:, 1], GATE[:, 0], ALU.mult)

            def place_rows(i, b):
                n = i * 2 + b
                here = bass.ds(n * G, G)
                for j in range(2):
                    dve.tensor_tensor(big[:], iota[:], bcast(IDX[:, j, here], NE), ALU.is_equal)
                    dve.drain()
                    dve.tensor_tensor(big[:], big[:], base[:].unsqueeze(1).to_broadcast([P, G, NE]), ALU.mult)
                    dve.drain()
                    dve.tensor_reduce(off[:], big[:], AX_X, ALU.add)
                    dve.drain()
                    dve.tensor_tensor(off[:], off[:], RANK[:, j, here], ALU.add)
                    dve.drain()
                    dve.tensor_copy(SLOT[:, j, here], off[:])
                if not isinstance(i, int):
                    kit.hold(dve, s["scattered"][b], i * (16 * 2 * G))
                dve.tensor_copy(rows[:, b], X[:, here, :])
                dve.drain().then_inc(s["rows_ready"], 1)

            place_rows(0, 0)
            place_rows(0, 1)
            with dve.Fori(1, TILES // G // 2) as i:
                for b in range(2):
                    place_rows(i, b)

        @block.tensor
        def _(pe):
            pe.wait_ge(s["w_in"], 48)
            pe.wait_ge(s["ready"], 2)
            skip = dict(skip_group_check=True)
            with pe.Fori(0, STEPS) as n:
                kit.hold(pe, s["x_ready"], n + 1)
                for t in range(T):
                    mm = pe.transpose(ps_x[0:D, P * t:P * t + P], x[:, t, :], ident[:])
                mm.then_inc(s["xt_done"], 1)
                kit.hold(pe, s["xt_out"], n + 1)
                for t in range(T):
                    mm = pe.matmul(ps_l[:, NE * t:NE * t + NE], xt[:, P * t:P * t + P], wr[:], start=True, stop=True)
                mm.then_inc(s["l_done"], 1)
                kit.hold(pe, s["both_ready"], n + 1)
                pe.matmul(ps_r[:, 0:T * NE], prior[:], both[:].rearrange("p t e -> p (t e)"), start=True, stop=False, **skip)
                for t in range(T):
                    src, to = (seen_b[:], T) if t == 0 else (both[:, t - 1], T - t)
                    mm = pe.matmul(ps_r[:, NE * (T - to):NE * T].rearrange("p (t e) -> p t e", e=NE), ones[:], src.unsqueeze(1).to_broadcast([P, to, NE]),
                                   start=False, stop=(t == T - 1), **skip)
                mm.then_inc(s["r_done"], 1)
            pe.wait_ge(s["seen_ready"], STEPS)
            pe.matmul(ps_m[:, 0:NE], ones[:], seen_b[:], start=True, stop=True).then_inc(s["total_done"], 1)
            pe.wait_ge(s["full_ready"], 1)
            pe.matmul(ps_m[:, NE:2 * NE], onesf[:], full[:], start=True, stop=True).then_inc(s["tiles_done"], 1)
            pe.wait_ge(s["end_ready"], 1)
            pe.matmul(ps_m[0:NE, 128:129], end[0:1, :], onesf[0:1, 0:1], start=True, stop=True).then_inc(s["endc_done"], 1)
            pe.wait_ge(s["past_ready"], 1)
            pe.matmul(ps_l[0:1, 0:SLOTS], onesf[0:NE, 0:1], past[:], start=True, stop=True).then_inc(s["own_done"], 1)


def run_experts(nc, kit, a, OWNER, xs, ys, SLOTS):
    NE, HID, T = 64, 128, 4
    GROUPS = SLOTS // T
    with ExitStack() as c:
        sb = lambda n, s, d=F32: kit.sb(c, n, s, d)
        sem = lambda n: kit.sem(c, n)
        ident = sb("ident10", [P, P])
        x = sb("x10", [P, 2, T, D])
        xt = sb("xt10", [D + 1, 2, T * P])
        w1 = sb("w1_10", [D + 1, 2, T, HID])
        w2 = sb("w2_10", [HID, 2, T, D])
        b2 = sb("b2_10", [1, 2, T, D])
        one = sb("one10", [1, P])
        h = sb("h10", [HID, 2, T * P])
        y = sb("y10", [P, 2, T, D])
        ps_x = kit.ps(c, "ps_x10", [P, T * P])
        ps_h = kit.ps(c, "ps_h10", [P, T * P])
        ps_y = kit.ps(c, "ps_y10", [P, 512])
        names = "w_in ready t_done xt_out h_done h_out y_done y_out".split()
        s = {n: sem(n + "_10") for n in names}
        s.update({n: [sem(n + "0_10"), sem(n + "1_10")] for n in ("x_in", "w_got", "stored")})
        block = kit.block(c)

        @block.sync
        def _(sp):
            sp.dma_start(ident[:], a["ident"]).then_inc(s["w_in"], 16)
            with sp.Fori(0, GROUPS // 2) as i:
                for b in range(2):
                    g = i * 2 + b
                    kit.hold(sp, s["t_done"], g + 1)
                    sp.dma_start(x[:, b], xs.rearrange("(g t p) d -> g p t d", t=T, p=P)[bass.ds(g, 1), :, :, :].rearrange("g p t d -> (g p) t d")).then_inc(s["x_in"][b], 16)
                    kit.hold(sp, s["y_done"], g + 1)
                    for t in range(T):
                        e = sp.value_load(OWNER[0:1, bass.ds(g * T + t, 1)], min_val=0, max_val=NE - 1)
                        sp.dma_start(w1[:, b, t], a["moe1_w1"][bass.ds(e, 1), :, :].rearrange("e k n -> (e k) n")).then_inc(s["w_got"][b], 16)
                        sp.dma_start(w2[:, b, t], a["moe1_w2"][bass.ds(e, 1), :, :].rearrange("e k n -> (e k) n")).then_inc(s["w_got"][b], 16)
                        sp.dma_start(b2[:, b, t], a["moe1_b2"][bass.ds(e, 1), :]).then_inc(s["w_got"][b], 16)

        @block.scalar
        def _(act):
            def rows(g, b):
                kit.hold(act, s["t_done"], g + 3)
                act.activation(xt[0:D, b], ps_x[0:D, :], ACT.Copy).then_inc(s["xt_out"], 1)

            def hidden(g, b):
                kit.hold(act, s["h_done"], g + 1)
                act.activation(h[:, b], ps_h[:], ACT.Relu).then_inc(s["h_out"], 1)

            def store(g, b):
                kit.hold(act, s["y_out"], g + 2)
                act.dma_start(ys.rearrange("(g t p) d -> g p t d", t=T, p=P)[bass.ds(g, 1), :, :, :].rearrange("g p t d -> (g p) t d"), y[:, b]).then_inc(s["stored"][b], 16)

            rows(0, 0)
            hidden(0, 0)
            with act.Fori(0, GROUPS // 2 - 1) as i:
                for b in range(2):
                    rows(i * 2 + b + 1, 1 - b)
                    store(i * 2 + b, b)
                    hidden(i * 2 + b + 1, 1 - b)
            rows(GROUPS - 1, 1)
            store(GROUPS - 2, 0)
            hidden(GROUPS - 1, 1)
            store(GROUPS - 1, 1)
            for b in range(2):
                act.wait_ge(s["stored"][b], 16 * (GROUPS // 2 + 1))

        @block.vector
        def _(dve):
            dve.memset(xt[D:D + 1, :, :], 1.0)
            dve.memset(one[:], 1.0)
            dve.drain().then_inc(s["ready"], 1)
            dve.sem_inc(s["t_done"], 2)
            dve.sem_inc(s["y_done"], 2)
            dve.sem_inc(s["y_out"], 1)
            dve.sem_inc(s["stored"][0], 16)
            dve.sem_inc(s["stored"][1], 16)
            with dve.Fori(0, GROUPS // 2) as i:
                for b in range(2):
                    g = i * 2 + b
                    kit.hold(dve, s["y_done"], g + 3)
                    kit.hold(dve, s["stored"][b], i * 16 + 16)
                    dve.tensor_copy(y[:, b], ps_y[:, 0:T * D].rearrange("p (t d) -> p t d", t=T)).then_inc(s["y_out"], 1)

        @block.tensor
        def _(pe):
            pe.wait_ge(s["w_in"], 16)
            pe.wait_ge(s["ready"], 1)
            skip = dict(skip_group_check=True)

            def turn(use, b):
                kit.hold(pe, s["x_in"][b], use * 16 + 16)
                for t in range(T):
                    mm = pe.transpose(ps_x[0:D, P * t:P * t + P], x[:, b, t, :], ident[:])
                mm.then_inc(s["t_done"], 1)

            def hidden(g, use, b):
                kit.hold(pe, s["xt_out"], g + 1)
                kit.hold(pe, s["w_got"][b], use * (48 * T) + 48 * T)
                for t in range(T):
                    mm = pe.matmul(ps_h[:, P * t:P * t + P], w1[:, b, t], xt[:, b, P * t:P * t + P], start=True, stop=True)
                mm.then_inc(s["h_done"], 1)

            def down(g, b):
                kit.hold(pe, s["h_out"], g + 1)
                kit.hold(pe, s["y_out"], g + 1)
                pe.matmul(ps_y[:, 0:T * D], one[:], b2[:, b].rearrange("o t d -> o (t d)"), start=True, stop=False, **skip)
                for t in range(T):
                    mm = pe.matmul(ps_y[:, D * t:D * t + D], h[:, b, P * t:P * t + P], w2[:, b, t], start=False, stop=True, **skip)
                mm.then_inc(s["y_done"], 1)

            turn(0, 0)
            hidden(0, 0, 0)
            with pe.Fori(0, GROUPS // 2 - 1) as i:
                for b in range(2):
                    turn(i + b, 1 - b)
                    down(i * 2 + b, b)
                    hidden(i * 2 + b + 1, i + b, 1 - b)
            turn(GROUPS // 2 - 1, 1)
            down(GROUPS - 2, 0)
            hidden(GROUPS - 1, GROUPS // 2 - 1, 1)
            down(GROUPS - 1, 1)


def combine(nc, kit, H, GATE, SLOT, ys, out):
    T = 8
    STEPS = TILES // T
    with ExitStack() as c:
        sb = lambda n, s, d=F32: kit.sb(c, n, s, d)
        sem = lambda n: kit.sem(c, n)
        now = sb("now11", [P, 2, 2, T], U32)
        got = sb("got11", [P, 2, 2, T, D])
        acc = sb("acc11", [P, 2, 2, T, D])
        picked = [sem("picked11_0"), sem("picked11_1")]
        free, ready = sem("free11"), sem("ready11")
        stored = [sem("stored11_0"), sem("stored11_1")]
        block = kit.block(c)

        @block.gpsimd
        def _(pool):
            with pool.Fori(0, STEPS // 2) as i:
                for b in range(2):
                    kit.hold(pool, free, i * 2 + b + 1)
                    pool.tensor_copy(now[:, b], SLOT[:, :, bass.ds((i * 2 + b) * T, T)])
                    pool.drain()
                    for t in range(T):
                        for j in range(2):
                            pool.indirect_dma_start(got[:, b, j, t, :], None, ys,
                                                    bass.IndirectOffsetOnAxis(ap=now[:, b, j, t:t + 1], axis=0)).then_inc(picked[b], 16)

        @block.vector
        def _(dve):
            dve.sem_inc(free, 2)
            dve.sem_inc(stored[0], 16)
            dve.sem_inc(stored[1], 16)
            with dve.Fori(0, STEPS // 2) as i:
                for b in range(2):
                    n = i * 2 + b
                    here = bass.ds(n * T, T)
                    kit.hold(dve, picked[b], (i + 1) * (32 * T))
                    kit.hold(dve, stored[b], i * 16 + 16)
                    dve.tensor_tensor(acc[:, b, 0], got[:, b, 0], bcast(GATE[:, 0, here], D), ALU.mult)
                    dve.tensor_tensor(acc[:, b, 1], got[:, b, 1], bcast(GATE[:, 1, here], D), ALU.mult).then_inc(free, 1)
                    dve.drain()
                    dve.tensor_tensor(acc[:, b, 0], acc[:, b, 0], acc[:, b, 1], ALU.add)
                    dve.drain()
                    dve.tensor_tensor(acc[:, b, 0], acc[:, b, 0], H[:, here, :], ALU.add).then_inc(ready, 1)

        @block.sync
        def _(sp):
            o = out.rearrange("s (two p) d -> p (s two) d", p=P)
            with sp.Fori(0, STEPS // 2) as i:
                for b in range(2):
                    n = i * 2 + b
                    kit.hold(sp, ready, n + 1)
                    sp.dma_start(o[:, bass.ds(n * T, T), :], acc[:, b, 0]).then_inc(stored[b], 16)
            for b in range(2):
                sp.wait_ge(stored[b], 16 * (STEPS // 2 + 1))


def build(nc, a, out):
    h1 = nc.dram_tensor("h1", (SEQ, LEN, D), F32).ap()
    with ExitStack() as top:
        kit = Kit(nc, top)
        with ExitStack() as c:
            H = kit.sb(c, "H_rows", [P, TILES, D])
            YT = kit.sb(c, "YT", [P, TILES // 2, P])
            LOGITS = kit.sb(c, "LOGITS", [P, 4, SEQ])
            MIX = kit.sb(c, "MIX", [P, 8, P])
            embed_and_logits(nc, kit, a, H, YT, LOGITS)
            row_softmax(nc, kit, a, LOGITS, MIX)
            row_attention_out(nc, kit, a, H, YT, MIX, h1)
        H = kit.sb(top, "H", [P, TILES, D])
        with ExitStack() as c:
            X2 = kit.sb(c, "X2", [P, TILES, D])
            causal_attention(nc, kit, a, h1, H, X2)
            dense_experts(nc, kit, a, H, X2)
        bc_dram = nc.dram_tensor("bc_dram", (2, 64, SEQ * LEN), F32).ap()
        mamba(nc, kit, a, H, bc_dram)
        sparse_experts(nc, kit, a, H, out)


def kernel(**inputs):
    import numpy as np
    import concourse.bacc as _bacc
    from concourse.bass_utils import run_bass_kernel_spmd as _run

    w = {k: np.ascontiguousarray(v) for k, v in inputs.items()}
    f32 = np.float32
    feed = {"x": w["x"], "emb2": w["L0_tok_emb_2"], "emb3": w["L0_tok_emb_3"], "emb4": w["L0_tok_emb_4"],
            "ident": np.eye(128, dtype=f32)}
    wqk = np.zeros((2, 64, 2, 4, 2, 2, 32), f32)
    for k, name in enumerate(("Wq", "Wk")):
        wh = w["L0_attn_" + name].reshape(64, 4, 2, 32)
        for j in range(2):
            wqk[j, :, k, :, :, j, :] = wh
    feed["attn_wqk"] = wqk.reshape(128, 8, 128)
    feed["attn_gb"] = np.tile(np.stack([w["L0_attn_gamma"], w["L0_attn_beta"]], 1), (2, 1))
    wvg = np.zeros((2, 64, 2, 512), f32)
    for j in range(2):
        wvg[j, :, j] = np.concatenate([w["L0_attn_Wv"], w["L0_attn_Wg"]], 1)
    feed["attn_wvg"] = wvg.reshape(128, 2, 512)
    feed["attn_wo"] = w["L0_attn_Wo"].reshape(2, 128, 64).transpose(1, 0, 2)
    feed["attn_bg"] = w["L0_attn_bg"].reshape(1, 256)
    feed["attn_bo"] = w["L0_attn_bo"].reshape(1, 64)
    def heads(wt, kv):
        o = np.zeros((2, 64, 4, 32), f32)
        for h in range(4):
            rows = wt[(h // 2 if kv else h) * 16:][:16]
            o[0, :, h, :16] = rows.T
            o[1, :, h, :8], o[1, :, h, 8:16] = rows[8:].T, rows[:8].T
        return o.reshape(2, 64, 128)
    wq, wk = heads(w["L0_ffn_wq"], False), heads(w["L0_ffn_wk"], True)
    feed["ffn_wqkv"] = np.concatenate([wq[0], wq[1], wk[0], wk[1], w["L0_ffn_wv"].T], 1)
    feed["ffn_wo"] = w["L0_ffn_wo"].T
    feed["ffn_ln1"] = w["L0_ffn_ln1_w"].reshape(64, 1)
    feed["ffn_ln2"] = w["L0_ffn_ln2_w"].reshape(64, 1)
    freq = 1.0 / 10000.0 ** (np.arange(0, 16, 2, dtype=f32) / 16)
    ang = np.outer(np.arange(256, dtype=f32), freq).astype(f32)
    rope = np.zeros((4, 32, 2, 256), f32)
    rope[:, :8, 0] = rope[:, 8:16, 0] = np.cos(ang).T
    rope[:, :8, 1], rope[:, 8:16, 1] = -np.sin(ang).T, np.sin(ang).T
    feed["rope"] = rope.reshape(128, 2, 256)
    feed["causal"] = np.where(np.tril(np.ones((128, 128), bool)), 0.0, NEG).astype(f32)
    feed["moe0_w1"] = w["L0_ffn_w1"].reshape(1360, 64).T
    feed["moe0_w3"] = w["L0_ffn_w3"].reshape(1360, 64).T
    w2 = np.zeros((11 * 128, 64), f32)
    w2[:1360] = w["L0_ffn_w2"].transpose(0, 2, 1).reshape(1360, 64)
    feed["moe0_w2"] = w2.reshape(11, 128, 64).transpose(1, 0, 2)
    feed["moe0_wr"] = w["L0_ffn_router_w"].T
    feed["moe0_spread"] = np.tile(np.repeat(np.eye(8, dtype=f32), 170, axis=1), (3, 1))
    feed["mb_win"], feed["mb_wx"] = w["L1_attn_W_in"], w["L1_attn_W_x"]
    feed["mb_wdt"], feed["mb_wout"] = w["L1_attn_W_dt"], w["L1_attn_W_out"]
    feed["mb_chan"] = np.concatenate([w["L1_attn_conv_k"].T, np.stack([w["L1_attn_conv_b"], w["L1_attn_b_dt"], w["L1_attn_D_param"]], 1)], 1)
    feed["mb_alog"] = w["L1_attn_A_log"]
    feed["before"] = np.triu(np.ones((64, 64), f32), 1)
    feed["moe1_wr"] = np.concatenate([w["L1_ffn_Wr"], w["L1_ffn_br"][None]], 0)
    feed["moe1_w1"] = np.concatenate([w["L1_ffn_W1"], w["L1_ffn_b1"][:, None]], 1)
    feed["moe1_w2"], feed["moe1_b2"] = w["L1_ffn_W2"], w["L1_ffn_b2"]
    feed["prior"] = np.triu(np.ones((128, 128), f32), 1)

    nc = _bacc.Bacc("TRN2", target_bir_lowering=False, num_devices=1)
    arrays, aps = {}, {}
    for name, v in feed.items():
        v = np.ascontiguousarray(v)
        arrays["in_" + name] = v
        aps[name] = nc.dram_tensor("in_" + name, v.shape, mybir.dt.from_np(v.dtype), kind="ExternalInput").ap()
    out = nc.dram_tensor("out_0", (SEQ, LEN, D), F32, kind="ExternalOutput").ap()
    build(nc, aps, out)
    r = _run(nc, [arrays], core_ids=[0])
    return r.results[0]["out_0"]
```

```python
import math
from contextlib import ExitStack

import concourse.bass as bass
from concourse import mybir

F32 = mybir.dt.float32
BF16 = mybir.dt.bfloat16
I32 = mybir.dt.int32
U32 = mybir.dt.uint32
ALU = mybir.AluOpType
ACT = mybir.ActivationFunctionType
AX_X = mybir.AxisListType.X

P = 128
SEQ, LEN, D = 64, 256, 64
TILES = SEQ * LEN // P
VOCAB, PRIME = 125000, 31
LN_EPS, RMS_EPS = 1e-5, 1e-6


class Kit:

    def __init__(self, nc, ctx):
        self.nc, self.ctx = nc, ctx
        self.held = ctx.enter_context(nc.semaphore("held"))
        self.used = []

    def sb(self, ctx, name, shape, dt=F32):
        return ctx.enter_context(self.nc.sbuf_tensor(name, shape, dt))

    def ps(self, ctx, name, shape, dt=F32):
        return ctx.enter_context(self.nc.psum_tensor(name, shape, dt))

    def sem(self, ctx, name):
        handle = ctx.enter_context(self.nc.semaphore(name))
        self.used.append(handle)
        return handle

    def block(self, ctx):
        ctx.callback(self.clear)
        return ctx.enter_context(self.nc.Block())

    def clear(self):
        done, self.used = self.used, []
        with self.nc.Block() as block:
            @block.sync
            def _(sp):
                for handle in done:
                    sp.sem_clear(handle)

    def hold(self, eng, sem, value):
        eng.wait_ge(sem, value)
        eng.sem_inc(self.held, 1)


def bcast(ap, n):
    return ap.unsqueeze(2).to_broadcast([ap.shape[0], ap.shape[1], n])


def embed_and_logits(nc, kit, a, H, YT, LOGITS):
    G = 8
    STEPS = TILES // G
    with ExitStack() as c:
        sb = lambda n, s, d=F32: kit.sb(c, n, s, d)
        sem = lambda n: kit.sem(c, n)
        tok_i = sb("tok_i", [P, 4 + LEN], I32)
        tok = sb("tok", [P, 4 + LEN])
        hs = sb("hs", [P, 3, TILES])
        quo = sb("quo", [P, 3, TILES])
        quo_i = sb("quo_i", [P, 3, TILES], I32)
        rows = sb("rows", [P, 3, TILES], U32)
        rows_now = sb("rows_now", [P, 2, 3, G], U32)
        gath = sb("gath", [P, 2, 3, G, D])
        h_now = sb("h_now", [P, G, D])
        cen = sb("cen", [P, G, D])
        sq = sb("sq", [P, G, D])
        ys = sb("ys", [P, G, D])
        st = sb("st", [P, 4, G])
        eps2 = sb("eps2", [P, 1])
        ident = sb("ident1", [P, P])
        wqk = sb("wqk", [P, 8, P])
        gb = sb("gb", [P, 2])
        yt = sb("yt_now", [P, 4, P])
        qk = sb("qk", [P, 2, 2, 4 * P])
        zer = sb("zer", [P, 256])
        ps_t = kit.ps(c, "ps_t", [P, 4, P])
        ps_qk = kit.ps(c, "ps_qk", [P, 2, 2, 4 * P])
        ps_att = kit.ps(c, "ps_att", [P, 4, SEQ])
        tok_in, w_in, rows_ready, cleared = sem("tok_in"), sem("w_in"), sem("rows_ready"), sem("cleared")
        picked = [sem("picked0"), sem("picked1")]
        gath_free, ssum, root, ys_ready, t_done = sem("gath_free"), sem("ssum"), sem("root"), sem("ys_ready"), sem("t_done")
        yt_ready, proj, q_out, k_out, att_done = sem("yt_ready"), sem("proj"), sem("q_out"), sem("k_out"), sem("att_done")
        zero_ready = sem("zero_ready")
        block = kit.block(c)

        @block.sync
        def _(sp):
            sp.wait_ge(zero_ready, 1)
            sp.dma_start(tok_i[0:64, 4:260], a["x"]).then_inc(tok_in, 16)
            sp.dma_start(tok_i[64:128, 3:259], a["x"]).then_inc(tok_in, 16)
            sp.dma_start(ident[:], a["ident"]).then_inc(w_in, 16)
            sp.dma_start(wqk[:], a["attn_wqk"]).then_inc(w_in, 16)
            sp.dma_start(gb[:], a["attn_gb"]).then_inc(w_in, 16)

        @block.gpsimd
        def _(pool):
            pool.wait_ge(rows_ready, 1)
            pool.wait_ge(cleared, 2)
            with pool.Fori(0, STEPS // 2) as i:
                for b in range(2):
                    step = i * 2 + b
                    kit.hold(pool, gath_free, step + 1)
                    pool.tensor_copy(rows_now[:, b], rows[:, :, bass.ds(step * G, G)])
                    pool.drain()
                    for t in range(G):
                        for n in range(3):
                            pool.indirect_dma_start(
                                gath[:, b, n, t, :], None, a[f"emb{n + 2}"],
                                bass.IndirectOffsetOnAxis(ap=rows_now[:, b, n, t:t + 1], axis=0),
                                bounds_check=VOCAB - 1, oob_is_err=False).then_inc(picked[b], 16)

        @block.vector
        def _(dve):
            dve.memset(tok_i[:], 0).then_inc(zero_ready, 1)
            dve.memset(gath[:, 0], 0.0).then_inc(cleared, 1)
            dve.memset(gath[:, 1], 0.0).then_inc(cleared, 1)
            dve.memset(zer[:], 0.0).then_inc(cleared, 1)
            dve.memset(eps2[:], LN_EPS * LN_EPS).then_inc(cleared, 1)
            dve.sem_inc(gath_free, 2)
            dve.wait_ge(tok_in, 32)
            dve.tensor_copy(tok[:], tok_i[:])
            dve.drain()
            tv = tok[:].rearrange("p (l two) -> p l two", two=2)

            def back(k):
                o = 4 - k
                return tok[:, o:o + 2 * TILES - 1:2] if o + 2 * TILES - 1 <= 260 else tok[:, o:260:2]
            dve.scalar_tensor_tensor(hs[:, 0], back(1), float(PRIME), back(0), ALU.mult, ALU.add)
            dve.drain()
            dve.scalar_tensor_tensor(hs[:, 1], back(2), float(PRIME ** 2 % VOCAB), hs[:, 0], ALU.mult, ALU.add)
            dve.drain()
            dve.scalar_tensor_tensor(hs[:, 2], back(3), float(PRIME ** 3 % VOCAB), hs[:, 1], ALU.mult, ALU.add)
            dve.drain()
            dve.tensor_scalar(quo[:], hs[:], 1.0 / VOCAB, None, ALU.mult)
            dve.drain()
            dve.tensor_copy(quo_i[:], quo[:])
            dve.drain()
            dve.tensor_copy(quo[:], quo_i[:])
            dve.drain()
            dve.scalar_tensor_tensor(hs[:], quo[:], -float(VOCAB), hs[:], ALU.mult, ALU.add)
            dve.drain()
            for cmp, shift in ((ALU.is_lt, float(VOCAB)), (ALU.is_ge, -float(VOCAB))):
                edge = 0.0 if cmp == ALU.is_lt else float(VOCAB)
                dve.tensor_scalar(quo[:], hs[:], edge, shift, cmp, ALU.mult)
                dve.drain()
                dve.tensor_tensor(hs[:], hs[:], quo[:], ALU.add)
                dve.drain()
            dve.memset(hs[0:64, 0, 0:1], 2.0 ** 20)
            dve.memset(hs[:, 1:3, 0:1], 2.0 ** 20)
            dve.memset(hs[0:64, 2, 1:2], 2.0 ** 20)
            dve.drain()
            dve.tensor_copy(rows[:], hs[:]).then_inc(rows_ready, 1)
            with dve.Fori(0, STEPS // 2) as i:
                for b in range(2):
                    step = i * 2 + b
                    kit.hold(dve, picked[b], 16 * 3 * G * i + 16 * 3 * G)
                    dve.tensor_tensor(sq[:], gath[:, b, 0], gath[:, b, 1], ALU.add)
                    dve.drain()
                    dve.tensor_tensor(cen[:], sq[:], gath[:, b, 2], ALU.add).then_inc(gath_free, 1)
                    dve.drain()
                    dve.tensor_scalar(h_now[:], cen[:], 0.25, None, ALU.mult)
                    dve.drain()
                    dve.tensor_copy(H[:, bass.ds(step * G, G), :], h_now[:])
                    dve.tensor_reduce(st[:, 0], h_now[:], AX_X, ALU.add)
                    dve.drain()
                    dve.tensor_scalar(st[:, 1], st[:, 0], 1.0 / D, None, ALU.mult)
                    dve.drain()
                    dve.tensor_tensor(cen[:], h_now[:], bcast(st[:, 1], D), ALU.subtract)
                    dve.drain()
                    dve.tensor_tensor(sq[:], cen[:], cen[:], ALU.mult)
                    dve.drain()
                    dve.tensor_reduce(st[:, 2], sq[:], AX_X, ALU.add).then_inc(ssum, 1)
                    dve.wait_ge(root, step + 1)
                    dve.reciprocal(st[:, 3], st[:, 1])
                    dve.drain()
                    dve.tensor_tensor(ys[:], cen[:], bcast(st[:, 3], D), ALU.mult).then_inc(ys_ready, 1)
                    for p in range(4):
                        kit.hold(dve, proj, step * 4 + p + 1)
                        dve.tensor_copy(qk[:, p % 2, 1, :], ps_qk[:, p % 2, 1, :]).then_inc(k_out, 1)
            dve.wait_ge(att_done, 1)
            dve.tensor_copy(LOGITS[:], ps_att[:])

        @block.scalar
        def _(act):
            act.wait_ge(w_in, 48)
            act.wait_ge(cleared, 4)
            with act.Fori(0, STEPS) as i:
                kit.hold(act, ssum, i + 1)
                act.activation(st[:, 1], st[:, 2], ACT.Sqrt, bias=eps2[:], scale=(1 + LN_EPS) / D).then_inc(root, 1)
                kit.hold(act, t_done, i + 1)
                act.activation(yt[:], ps_t[:], ACT.Identity, bias=gb[:, 1:2], scale=gb[:, 0:1]).then_inc(yt_ready, 1)
                act.activation(YT[:, bass.ds(i * 4, 4), :], ps_t[:], ACT.Identity, bias=gb[:, 1:2], scale=gb[:, 0:1]).then_inc(yt_ready, 1)
                for p in range(4):
                    kit.hold(act, proj, i * 4 + p + 1)
                    act.activation(qk[:, p % 2, 0, :], ps_qk[:, p % 2, 0, :], ACT.Copy).then_inc(q_out, 1)

        @block.tensor
        def _(pe):
            pe.wait_ge(w_in, 48)
            pe.wait_ge(cleared, 4)
            pe.matmul(ps_att[:].rearrange("p a t -> p (a t)"), zer[:, 0:P], zer[:], start=True, stop=False, skip_group_check=True)

            def project(p, b):
                pe.matmul(ps_qk[:, b, 0, :], wqk[:, p, :], yt[:].rearrange("p a t -> p (a t)"), start=True, stop=True)
                pe.matmul(ps_qk[:, b, 1, :], wqk[:, 4 + p, :], yt[:].rearrange("p a t -> p (a t)"), start=True, stop=True).then_inc(proj, 1)

            def logits(p, i):
                kit.hold(pe, q_out, i * 4 + p + 1)
                kit.hold(pe, k_out, i * 4 + p + 1)
                for h in range(2):
                    r = slice(64 * h, 64 * h + 64)
                    for s in range(8):
                        mm = pe.matmul(ps_att[r, p, :], qk[r, p % 2, 0, 64 * s:64 * s + 64], qk[r, p % 2, 1, 64 * s:64 * s + 64],
                                       start=False, stop=False, skip_group_check=True)
                return mm

            with pe.Fori(0, STEPS) as i:
                kit.hold(pe, ys_ready, i + 1)
                for t in range(4):
                    tr = pe.transpose(ps_t[:, t, :], ys[:, 2 * t:2 * t + 2, :].rearrange("p a d -> p (a d)"), ident[:])
                tr.then_inc(t_done, 1)
                kit.hold(pe, yt_ready, 2 * i + 2)
                project(0, 0)
                project(1, 1)
                logits(0, i)
                project(2, 0)
                logits(1, i)
                project(3, 1)
                logits(2, i)
                logits(3, i)
            pe.matmul(ps_att[:].rearrange("p a t -> p (a t)"), zer[:, 0:P], zer[:], start=False, stop=True,
                      skip_group_check=True).then_inc(att_done, 1)


def row_softmax(nc, kit, a, LOGITS, MIX):
    scale = 1.0 / (32 ** 0.5) / (LEN ** 0.5)
    with ExitStack() as c:
        sb = lambda n, s, d=F32: kit.sb(c, n, s, d)
        sem = lambda n: kit.sem(c, n)
        ident = sb("ident2", [P, P])
        prob = sb("prob", [P, 4, SEQ])
        twice = sb("twice", [P, 4, 2, SEQ])
        st = sb("st2", [P, 3, 4])
        ps_t = kit.ps(c, "ps_t2", [P, 4, P])
        w_in, lmax, expd, twice_ready, t_done = sem("w_in2"), sem("lmax"), sem("expd"), sem("twice_ready"), sem("t_done2")
        block = kit.block(c)

        @block.sync
        def _(sp):
            sp.dma_start(ident[:], a["ident"]).then_inc(w_in, 16)

        @block.vector
        def _(dve):
            dve.memset(MIX[:], 0.0)
            dve.tensor_reduce(st[:, 0], LOGITS[:], AX_X, ALU.max)
            dve.drain()
            dve.tensor_tensor(prob[:], LOGITS[:], bcast(st[:, 0], SEQ), ALU.subtract).then_inc(lmax, 1)
            dve.wait_ge(expd, 1)
            dve.tensor_reduce(st[:, 1], prob[:], AX_X, ALU.add)
            dve.drain()
            dve.reciprocal(st[:, 2], st[:, 1])
            dve.drain()
            for k in range(2):
                w = dve.tensor_tensor(twice[:, :, k, :], prob[:], bcast(st[:, 2], SEQ), ALU.mult)
            w.then_inc(twice_ready, 1)
            dve.wait_ge(t_done, 1)
            for k in range(2):
                r = slice(64 * k, 64 * k + 64)
                dve.tensor_copy(MIX[r, :, r].rearrange("t (p h) s -> t p h s", h=2), ps_t[r, :, :].rearrange("t p (h s) -> t p h s", h=2))

        @block.scalar
        def _(act):
            act.wait_ge(lmax, 1)
            act.activation(prob[:], prob[:], ACT.Exp, scale=scale).then_inc(expd, 1)

        @block.tensor
        def _(pe):
            pe.wait_ge(w_in, 16)
            pe.wait_ge(twice_ready, 1)
            for p in range(4):
                tr = pe.transpose(ps_t[:, p, :], twice[:, p, :, :].rearrange("p k s -> p (k s)"), ident[:])
            tr.then_inc(t_done, 1)


def row_attention_out(nc, kit, a, H, YT, MIX, h1):
    N = TILES // 2
    with ExitStack() as c:
        sb = lambda n, s, d=F32: kit.sb(c, n, s, d)
        sem = lambda n: kit.sem(c, n)
        ident = sb("ident3", [P, P])
        wvg = sb("wvg", [P, 2, 512])
        wo = sb("wo", [P, 2, D])
        bg = sb("bg", [P, 256])
        bo = sb("bo", [P, D])
        yt = sb("yt3", [P, 2, P])
        v = sb("v", [P, 2, 2, 256])
        gz = sb("gz", [P, 2, 2, 256])
        og = sb("og", [P, 2, 2, 256])
        ogt = sb("ogt", [P, 2, 2, 2, P])
        res = sb("res3", [P, 4, D])
        ps_vg = kit.ps(c, "ps_vg", [P, 2, 2, 2, 256])
        ps_o = kit.ps(c, "ps_o", [P, 2, 8, 2, 32])
        ps_t = kit.ps(c, "ps_t3", [P, 2, 2, P])
        ps_h = kit.ps(c, "ps_h", [P, 4, D])
        w_in, yt_ready, vg_done, v_out, gz_out, sig = (sem(n) for n in ("w_in3", "yt_ready3", "vg_done", "v_out", "gz_out", "sig"))
        o_done, og_out, t_done, ogt_out, h_done, h_out, stored = (sem(n) for n in ("o_done", "og_out", "t_done3", "ogt_out", "h_done", "h_out", "stored3"))
        block = kit.block(c)

        @block.sync
        def _(sp):
            for dst, src in ((ident[:], a["ident"]), (wvg[:], a["attn_wvg"]), (wo[:], a["attn_wo"]),
                             (bg[:], a["attn_bg"].to_broadcast([P, 256])), (bo[:], a["attn_bo"].to_broadcast([P, D]))):
                sp.dma_start(dst, src).then_inc(w_in, 16)
            sp.wait_ge(h_out, N)
            for l2 in range(2):
                sp.dma_start(h1.rearrange("s (lp l2) d -> l2 s lp d", l2=2)[l2], H[64 * l2:64 * l2 + 64, :, :]).then_inc(stored, 16)
            sp.wait_ge(stored, 32)

        @block.gpsimd
        def _(pool):
            with pool.Fori(0, N // 2) as i:
                for b in range(2):
                    kit.hold(pool, vg_done, i * 2 + b + 1)
                    pool.tensor_copy(yt[:, b, :], YT[:, bass.ds(i * 2 + b, 1), :].rearrange("p a t -> p (a t)")).then_inc(yt_ready, 1)

        @block.scalar
        def _(act):
            with act.Fori(0, N // 2) as i:
                for b in range(2):
                    kit.hold(act, vg_done, i * 2 + b + 3)
                    act.activation(v[:, b], ps_vg[:, b, 0], ACT.Copy).then_inc(v_out, 1)
                    kit.hold(act, gz_out, i * 2 + b + 1)
                    act.activation(gz[:, b], gz[:, b], ACT.Sigmoid).then_inc(sig, 1)
                for b in range(2):
                    kit.hold(act, t_done, i * 2 + b + 1)
                    act.activation(ogt[:, b].rearrange("p l k t -> p (l k t)"), ps_t[:].rearrange("p l k t -> p (l k t)"), ACT.Copy).then_inc(ogt_out, 1)

        @block.vector
        def _(dve):
            dve.sem_inc(vg_done, 2)
            dve.wait_ge(w_in, 80)
            with dve.Fori(0, N // 2) as i:
                for b in range(2):
                    kit.hold(dve, vg_done, i * 2 + b + 3)
                    dve.tensor_tensor(gz[:, b], ps_vg[:, b, 1], bg[:].unsqueeze(1).to_broadcast([P, 2, 256]), ALU.add).then_inc(gz_out, 1)
                for b in range(2):
                    kit.hold(dve, sig, i * 2 + b + 1)
                    kit.hold(dve, o_done, i * 2 + b + 1)
                    dve.tensor_tensor(og[:, b].rearrange("p l (h c) -> p h l c", h=8), ps_o[:, b], gz[:, b].rearrange("p l (h c) -> p h l c", h=8), ALU.mult).then_inc(og_out, 1)
                kit.hold(dve, h_done, i * 2 + 2)
                dve.tensor_tensor(res[:], ps_h[:], bo[:].unsqueeze(1).to_broadcast([P, 4, D]), ALU.add)
                dve.drain()
                hh = H[:, bass.ds(i * 4, 4), :]
                dve.tensor_tensor(hh, hh, res[:], ALU.add).then_inc(h_out, 2)

        @block.tensor
        def _(pe):
            pe.wait_ge(w_in, 80)
            with pe.Fori(0, N // 2) as i:
                for b in range(2):
                    kit.hold(pe, yt_ready, i * 2 + b + 1)
                    for j in range(2):
                        for k in range(2):
                            mm = pe.matmul(ps_vg[:, b, k, j, :], yt[:, b, :], wvg[:, j, 256 * k:256 * k + 256], start=True, stop=True)
                    mm.then_inc(vg_done, 1)
                for b in range(2):
                    kit.hold(pe, v_out, i * 2 + b + 1)
                    for h in range(8):
                        mm = pe.matmul(ps_o[:, b, h], MIX[:, h, :], v[:, b, :, 32 * h:32 * h + 32], start=True, stop=True)
                    mm.then_inc(o_done, 1)
                for b in range(2):
                    kit.hold(pe, og_out, i * 2 + b + 1)
                    if b == 1:
                        kit.hold(pe, ogt_out, i * 2 + 1)
                    for l in range(2):
                        for k in range(2):
                            mm = pe.transpose(ps_t[:, l, k, :], og[:, b, l, 128 * k:128 * k + 128], ident[:])
                    mm.then_inc(t_done, 1)
                for b in range(2):
                    kit.hold(pe, ogt_out, i * 2 + b + 1)
                    for l in range(2):
                        for k in range(2):
                            mm = pe.matmul(ps_h[:, 2 * b + l, :], ogt[:, b, l, k, :], wo[:, k, :], start=(k == 0), stop=(k == 1))
                    mm.then_inc(h_done, 1)


NEG = -1e30


def norm_statistics(dve, src, cen, sq, st):
    dve.tensor_reduce(st[:, 0], src, AX_X, ALU.add)
    dve.drain()
    dve.tensor_scalar(st[:, 1], st[:, 0], 1.0 / D, None, ALU.mult)
    dve.drain()
    dve.tensor_tensor(cen, src, bcast(st[:, 1], D), ALU.subtract)
    dve.drain()
    dve.tensor_tensor(sq, cen, cen, ALU.mult)
    dve.drain()
    dve.tensor_reduce(st[:, 2], sq, AX_X, ALU.add)
    dve.drain()


def causal_attention(nc, kit, a, h1, H, X2):
    with ExitStack() as c:
        sb = lambda n, s, d=F32: kit.sb(c, n, s, d)
        sem = lambda n: kit.sem(c, n)
        ident = sb("ident4", [P, P])
        identb = sb("identb4", [P, P], BF16)
        maskf = sb("maskf", [P, P])
        mask = sb("mask", [P, P], BF16)
        wqkv = sb("wqkv", [64, 4 * P + D])
        wo = sb("wo4", [64, D])
        ln1 = sb("ln1", [64, 1])
        rope = sb("rope", [P, 2, LEN])
        cen = sb("cen4", [P, 2, D])
        sq = sb("sq4", [P, 2, D])
        u = sb("u4", [P, 2, D])
        st = sb("st4", [P, 3, 2])
        var = sb("var4", [P, 2, 2])
        half = sb("half4", [P, 2, 2])
        rs = sb("rs4", [P, 2, 2])
        ht = sb("ht", [64, LEN])
        q = sb("q4", [P, LEN])
        k = sb("k4", [P, LEN])
        t1 = sb("t14", [P, LEN])
        t2 = sb("t24", [P, LEN])
        v = sb("v4", [P, 2, 2, 4 * 80])
        mx = sb("mx4", [P, 2, 4])
        nm = sb("nm4", [P, 2, 4])
        sums = sb("sums4", [P, 2, 2, 4])
        rsum = sb("rsum4", [P, 2, 4])
        E = sb("E4", [P, 2, 4, 3 * P])
        ET = sb("ET4", [P, 3, 4, P])
        rwide = sb("rwide4", [P, 2, D])
        rwt = sb("rwt4", [D, LEN])
        yt = sb("yt4", [64, LEN])
        ps_s = kit.ps(c, "ps_s", [P, 4, 512])
        ps_t = kit.ps(c, "ps_t4", [P, 2, 4, P])
        ps_a = kit.ps(c, "ps_a4", [P, 512])
        ps_b = kit.ps(c, "ps_b4", [P, 512])
        names = ("w_in var_ready u_ready ht_done ht_out proj q_out k_out v_done v_out scores nm_ready "
                 "exps t_done t_outa t_outd y_done rw_ready rwt_done rwt_out zeroed yt_out o_done o_out mask_ready").split()
        s = {n: sem(n + "_4") for n in names}
        block = kit.block(c)
        SCALE = 16 ** -0.5

        def steps(eng, step):
            step(-2, 0, tail=False, middle=False)
            step(-1, 1, tail=False)
            with eng.Fori(0, SEQ // 2 - 1) as i:
                step(i * 2, 0)
                step(i * 2 + 1, 1)
            step(SEQ - 2, 0, head=False)
            step(SEQ - 1, 1, head=False, middle=False)

        @block.sync
        def _(sp):
            for dst, src in ((ident[:], a["ident"]), (maskf[:], a["causal"]), (wqkv[:], a["ffn_wqkv"]), (wo[:], a["ffn_wo"]),
                             (ln1[:], a["ffn_ln1"]), (rope[:], a["rope"])):
                sp.dma_start(dst, src).then_inc(s["w_in"], 16)
            sp.dma_start(H[:], h1.rearrange("s (two p) d -> p (s two) d", p=P)).then_inc(s["w_in"], 16)

        @block.gpsimd
        def _(pool):
            pool.memset(half[:], -0.5)
            pool.drain()

            def step(b, par, tail=True, middle=True, head=True):
                if head:
                    n = b + 2
                    kit.hold(pool, s["var_ready"], n + 1)
                    pool.tensor_tensor(rs[:], var[:], half[:], ALU.pow)
                    pool.drain()
                    pool.tensor_tensor(X2[:, bass.ds(n * 2, 2), :], cen[:], bcast(rs[:, 0], D), ALU.mult)
                    pool.tensor_tensor(u[:], cen[:], bcast(rs[:, 1], D), ALU.mult).then_inc(s["u_ready"], 1)

            steps(pool, step)

        @block.vector
        def _(dve):
            dve.wait_ge(s["w_in"], 112)
            dve.tensor_copy(identb[:], ident[:])
            dve.tensor_copy(mask[:], maskf[:]).then_inc(s["mask_ready"], 1)

            dve.memset(v[:], 0.0).then_inc(s["zeroed"], 1)
            dve.sem_inc(s["v_out"], 1)
            dve.sem_inc(s["exps"], 1)

            def rotate(dst, out, count):
                kit.hold(dve, s["proj"], count)
                dve.tensor_tensor(t1[:], ps_a[:, 0:LEN], rope[:, 0], ALU.mult)
                dve.tensor_tensor(t2[:], ps_a[:, LEN:2 * LEN], rope[:, 1], ALU.mult)
                dve.drain()
                dve.tensor_tensor(dst[:], t1[:], t2[:], ALU.add).then_inc(out, 1)

            def step(b, par, tail=True, middle=True, head=True):
                n = b + 2
                if tail:
                    kit.hold(dve, s["exps"], b + 2)
                    dve.reciprocal(rsum[:], sums[:, par])
                    dve.drain()
                    dve.tensor_copy(rwide[:].rearrange("p t (h c) -> p t h c", h=4),
                                    rsum[:].unsqueeze(3).to_broadcast([P, 2, 4, 16])).then_inc(s["rw_ready"], 1)
                if head:
                    norm_statistics(dve, H[:, bass.ds(n * 2, 2), :], cen[:], sq[:], st)
                    dve.tensor_scalar(var[:, 0], st[:, 2], 1.0 / D, LN_EPS, ALU.mult, ALU.add)
                    dve.tensor_scalar(var[:, 1], st[:, 2], (1 + RMS_EPS) / D, RMS_EPS * LN_EPS, ALU.mult, ALU.add).then_inc(s["var_ready"], 1)
                if tail:
                    kit.hold(dve, s["t_done"], b * 3 + 2)
                    dve.tensor_copy(ET[:, 1], ps_t[:, 1]).then_inc(s["t_outd"], 1)
                if middle:
                    kit.hold(dve, s["scores"], b + 2)
                    dve.tensor_reduce(mx[:, 0], ps_s[:, :, 0:P], AX_X, ALU.max)
                    dve.tensor_reduce(mx[:, 1], ps_s[:, :, LEN:2 * LEN], AX_X, ALU.max)
                    dve.drain()
                    dve.tensor_scalar(nm[:], mx[:], -SCALE, None, ALU.mult).then_inc(s["nm_ready"], 1)
                if head:
                    rotate(q, s["q_out"], n * 2 + 1)
                if tail:
                    kit.hold(dve, s["y_done"], b + 1)
                    kit.hold(dve, s["rwt_out"], b + 1)
                    dve.tensor_tensor(yt[:], ps_b[0:64, 0:LEN], rwt[:], ALU.mult).then_inc(s["yt_out"], 1)
                if head:
                    rotate(k, s["k_out"], n * 2 + 2)
                if tail:
                    kit.hold(dve, s["o_done"], b + 1)
                    xx = X2[:, bass.ds(b * 2, 2), :]
                    dve.tensor_tensor(xx, xx, ps_b[:, 384:512].rearrange("p (t d) -> p t d", t=2), ALU.add).then_inc(s["o_out"], 1)

            steps(dve, step)

        @block.scalar
        def _(act):
            act.wait_ge(s["w_in"], 112)
            act.wait_ge(s["zeroed"], 1)

            def step(b, par, tail=True, middle=True, head=True):
                n = b + 2
                if tail:
                    kit.hold(act, s["t_done"], b * 3 + 1)
                    act.activation(ET[:, 0], ps_t[:, 0], ACT.Copy).then_inc(s["t_outa"], 1)
                if middle:
                    kit.hold(act, s["v_done"], b + 2)
                    act.activation(v[:, 1 - par].rearrange("p t (h w) -> p t h w", h=4)[:, :, :, 0:16],
                                   ps_a[:, 0:2 * D].rearrange("p (t h c) -> p t h c", t=2, h=4), ACT.Copy).then_inc(s["v_out"], 1)
                if tail:
                    kit.hold(act, s["rwt_done"], b + 1)
                    act.activation(rwt[:], ps_b[0:64, LEN:2 * LEN], ACT.Copy).then_inc(s["rwt_out"], 1)
                if head:
                    kit.hold(act, s["ht_done"], n + 1)
                    act.activation(ht[:], ps_a[0:64, 0:LEN], ACT.Copy, scale=ln1[:]).then_inc(s["ht_out"], 1)
                if tail:
                    kit.hold(act, s["t_done"], b * 3 + 3)
                    act.activation(ET[:, 2], ps_t[:, 0], ACT.Copy).then_inc(s["t_outa"], 1)
                if middle:
                    kit.hold(act, s["nm_ready"], b + 2)
                    other = 1 - par
                    for h in range(4):
                        act.activation(E[:, other, h, 0:P], ps_s[:, h, 0:P], ACT.Exp, bias=nm[:, 0, h:h + 1], scale=SCALE,
                                       accum_out=sums[:, other, 0, h:h + 1])
                        e = act.activation(E[:, other, h, P:3 * P], ps_s[:, h, LEN:2 * LEN], ACT.Exp, bias=nm[:, 1, h:h + 1], scale=SCALE,
                                           accum_out=sums[:, other, 1, h:h + 1])
                    e.then_inc(s["exps"], 1)

            steps(act, step)

        @block.tensor
        def _(pe):
            pe.wait_ge(s["w_in"], 112)
            pe.wait_ge(s["mask_ready"], 1)

            skip = dict(skip_group_check=True)

            def scores(n):
                kit.hold(pe, s["k_out"], n + 1)
                kit.hold(pe, s["exps"], n + 1)
                for h in range(4):
                    pe.matmul(ps_s[:, h, 0:P], identb[:], mask[:], start=True, stop=False, **skip)
                    pe.matmul(ps_s[:, h, 3 * P:4 * P], identb[:], mask[:], start=False, stop=False, **skip)
                for h in range(4):
                    r = slice(32 * h, 32 * h + 32)
                    pe.matmul(ps_s[:, h, 0:P], q[r, 0:P], k[r, 0:P], start=False, stop=False, tile_position=(32 * h, 0), **skip)
                    mm = pe.matmul(ps_s[:, h, LEN:2 * LEN], q[r, P:LEN], k[r, :], start=False, stop=True, tile_position=(32 * h, 0), **skip)
                mm.then_inc(s["scores"], 1)

            def project(which):
                for j in range(2):
                    mm = pe.matmul(ps_a[:, LEN * j:LEN * j + LEN], wqkv[:, P * (2 * which + j):P * (2 * which + j) + P], ht[:], start=True, stop=True)
                mm.then_inc(s["proj"], 1)

            def turn(par, g):
                for h in range(4):
                    mm = pe.transpose(ps_t[:, g % 2, h, :], E[:, par, h, P * g:P * g + P], ident[:])
                mm.then_inc(s["t_done"], 1)

            def values(n):
                kit.hold(pe, s["k_out"], n + 1)
                for t in range(2):
                    mm = pe.matmul(ps_a[:, D * t:D * t + D], ht[:, P * t:P * t + P], wqkv[:, 4 * P:4 * P + D], start=True, stop=True)
                mm.then_inc(s["v_done"], 1)

            def step(b, par, tail=True, middle=True, head=True):
                n = b + 2
                if tail:
                    kit.hold(pe, s["exps"], b + 2)
                    turn(par, 0)
                    turn(par, 1)
                if middle:
                    values(b + 1)
                if tail:
                    kit.hold(pe, s["rw_ready"], b + 1)
                    for t in range(2):
                        mm = pe.transpose(ps_b[0:64, LEN + P * t:LEN + P * t + P], rwide[:, t, :], ident[:])
                    mm.then_inc(s["rwt_done"], 1)
                if middle:
                    scores(b + 1)
                if head:
                    kit.hold(pe, s["v_out"], n + 1)
                    kit.hold(pe, s["u_ready"], n + 1)
                    for t in range(2):
                        mm = pe.transpose(ps_a[0:64, P * t:P * t + P], u[:, t, :], ident[:])
                    mm.then_inc(s["ht_done"], 1)
                if tail:
                    kit.hold(pe, s["t_outa"], b * 2 + 1)
                    turn(par, 2)
                if head:
                    kit.hold(pe, s["ht_out"], n + 1)
                    project(0)
                if tail:
                    kit.hold(pe, s["t_outa"], b * 2 + 2)
                    kit.hold(pe, s["t_outd"], b + 1)
                    kit.hold(pe, s["v_out"], b + 2)
                    kit.hold(pe, s["rwt_out"], b + 1)
                    for t, g, keys in ((0, 0, 0), (1, 1, 0), (1, 2, 1)):
                        for h in range(4):
                            mm = pe.matmul(ps_b[0:64, P * t:P * t + P], v[:, par, keys, 64 * h:64 * h + 64], ET[:, g, h, :],
                                           start=(g < 2 and h == 0), stop=(g != 1 and h == 3), **skip)
                    mm.then_inc(s["y_done"], 1)
                if head:
                    kit.hold(pe, s["q_out"], n + 1)
                    project(1)
                if tail:
                    kit.hold(pe, s["yt_out"], b + 1)
                    for t in range(2):
                        mm = pe.matmul(ps_b[:, 384 + 64 * t:448 + 64 * t], yt[:, P * t:P * t + P], wo[:], start=True, stop=True)
                    mm.then_inc(s["o_done"], 1)

            steps(pe, step)


def dense_experts(nc, kit, a, H, X2):
    NE, HID = 8, 170
    ROWS = NE * HID
    CH = -(-ROWS // P)
    T = 4
    BLOCKS = TILES // T
    W = T * P
    size = [min(P, ROWS - P * j) for j in range(CH)]
    with ExitStack() as c:
        sb = lambda n, s, d=F32: kit.sb(c, n, s, d)
        sem = lambda n: kit.sem(c, n)
        ident = sb("ident5", [P, P])
        identb = sb("identb5", [P, P], BF16)
        wide_w = sb("wide_w5", [P, ROWS])
        w_split = sb("w_split5", [P, 2, 3, ROWS], BF16)
        w2 = sb("w2_5", [P, CH, D])
        wr = sb("wr_5", [64, NE])
        ln2 = sb("ln2", [P, 1])
        spreadf = sb("spreadf", [24, ROWS])
        spread = sb("spread", [24, ROWS], BF16)
        iota = sb("iota5", [P, T, NE])
        iotai = sb("iotai5", [P, T, NE], I32)
        sq = sb("sq5", [P, T, D])
        st = sb("st5", [P, T])
        var = sb("var5", [P, T])
        half = sb("half5", [P, T])
        euler = sb("euler5", [P, T, NE])
        rs = sb("rs5", [P, T])
        fl = sb("fl5", [P, T, 2, D])
        flt = sb("flt", [P, W])
        xa = sb("xa5", [P, 2, W], BF16)
        xb = sb("xb5", [P, 2, W], BF16)
        lg = sb("lg5", [P, T, NE])
        pr = sb("pr5", [P, T, NE])
        m = sb("m5", [P, 4, T])
        top = sb("top5", [P, T, 8])
        topi = sb("topi5", [P, T, 8], U32)
        topf = sb("topf5", [P, T, 8])
        hot = sb("hot5", [P, 2, T, NE])
        wt = sb("wt5", [P, T, NE])
        rest = sb("rest5", [P, 2, T, NE])
        w3b = sb("w3b", [P, T, 3, NE], BF16)
        wtt = sb("wtt", [24, 2, W], BF16)
        gate = sb("gate5", [P, 2, W])
        up = sb("up5", [P, 2, W])
        hid = sb("hid5", [P, 2, W])
        acc = sb("acc5", [P, T, D])
        ps_u = kit.ps(c, "ps_u", [P, 2, 2, W])
        ps_w = kit.ps(c, "ps_w", [P, W])
        ps_d = kit.ps(c, "ps_d", [P, 512])
        ps_r = kit.ps(c, "ps_r", [P, W])
        ps_x = kit.ps(c, "ps_x", [P, 1024], BF16)
        names = ("w_in ready sq_ready var_ready fl_ready flt_done flt_out router lg_ready exp_done w_ready wtt_done wtt_out "
                 "ups split x0_out half_ready wide gated hidden down out").split()
        s = {n: sem(n + "_5") for n in names}
        block = kit.block(c)

        @block.sync
        def _(sp):
            for dst, src in ((ident[:], a["ident"]), (w2[:], a["moe0_w2"]), (wr[:], a["moe0_wr"]), (ln2[:], a["ffn_ln2"]), (spreadf[:], a["moe0_spread"])):
                sp.dma_start(dst, src).then_inc(s["w_in"], 16)
            for j, name in enumerate(("moe0_w1", "moe0_w3")):
                if j:
                    sp.wait_ge(s["half_ready"], 1)
                sp.dma_start(wide_w[:], a[name]).then_inc(s["w_in"], 16)

        @block.gpsimd
        def _(pool):
            pool.memset(half[:], -0.5)
            pool.memset(euler[:], math.e)
            pool.iota(iotai[:], pattern=[[0, T], [1, NE]], base=0, channel_multiplier=0).then_inc(s["ready"], 1)
            pool.drain()

            def squares(n):
                if n is None:
                    return
                x = X2[:, bass.ds(n * T, T), :]
                pool.tensor_tensor(sq[:], x, x, ALU.mult).then_inc(s["sq_ready"], 1)

            def flat_rows(n):
                kit.hold(pool, s["var_ready"], n + 1)
                pool.tensor_tensor(rs[:], var[:], half[:], ALU.pow)
                pool.drain()
                x = X2[:, bass.ds(n * T, T), :]
                pool.tensor_tensor(fl[:, :, 0], x, bcast(rs[:], D), ALU.mult)
                pool.tensor_tensor(fl[:, :, 1], x, bcast(rs[:], D), ALU.mult).then_inc(s["fl_ready"], 1)

            def exps(n):
                kit.hold(pool, s["lg_ready"], n + 1)
                pool.tensor_tensor(pr[:], euler[:], lg[:], ALU.pow).then_inc(s["exp_done"], 1)

            squares(0)
            flat_rows(0)
            exps(0)
            squares(1)
            with pool.Fori(0, BLOCKS - 2) as i:
                flat_rows(i + 1)
                exps(i + 1)
                squares(i + 2)
            flat_rows(BLOCKS - 1)
            exps(BLOCKS - 1)

        @block.vector
        def _(dve):
            dve.wait_ge(s["w_in"], 96)
            dve.wait_ge(s["ready"], 1)
            dve.tensor_copy(identb[:], ident[:])
            dve.tensor_copy(spread[:], spreadf[:])
            dve.tensor_copy(iota[:], iotai[:]).then_inc(s["ready"], 1)
            dve.drain()
            for j in range(2):
                if j:
                    dve.wait_ge(s["w_in"], 112)
                w0, w1, w2_ = w_split[:, j, 0], w_split[:, j, 1], w_split[:, j, 2]
                dve.tensor_copy(w0, wide_w[:])
                dve.drain()
                dve.tensor_tensor(wide_w[:], wide_w[:], w0, ALU.subtract)
                dve.drain()
                dve.tensor_copy(w1, wide_w[:])
                dve.drain()
                dve.tensor_tensor(w2_[0:64], wide_w[0:64], w1[0:64], ALU.subtract)
                dve.tensor_copy(w2_[64:P], w0[64:P])
                dve.drain()
                dve.sem_inc(s["half_ready"], 1)

            def variance(n):
                kit.hold(dve, s["sq_ready"], n + 1)
                dve.tensor_reduce(st[:], sq[:], AX_X, ALU.add)
                dve.drain()
                dve.tensor_scalar(var[:], st[:], 1.0 / D, RMS_EPS, ALU.mult, ALU.add).then_inc(s["var_ready"], 1)

            def split(n, b):
                kit.hold(dve, s["x0_out"], n + 1)
                dve.tensor_tensor(flt[64:P], flt[64:P], xa[64:P, b], ALU.subtract)
                dve.drain()
                dve.tensor_copy(xa[64:P, b], flt[64:P])
                dve.drain()
                dve.tensor_tensor(xb[64:P, b], flt[64:P], xa[64:P, b], ALU.subtract).then_inc(s["split"], 1)

            def shifted(n):
                kit.hold(dve, s["router"], n + 1)
                dve.tensor_copy(lg[:], ps_r[:, 0:T * NE].rearrange("p (t e) -> p t e", e=NE))
                dve.drain()
                dve.tensor_reduce(m[:, 0], lg[:], AX_X, ALU.max)
                dve.drain()
                dve.tensor_tensor(lg[:], lg[:], bcast(m[:, 0], NE), ALU.subtract).then_inc(s["lg_ready"], 1)

            def shares(n):
                kit.hold(dve, s["exp_done"], n + 1)
                dve.tensor_reduce(m[:, 1], pr[:], AX_X, ALU.add)
                dve.drain()
                dve.reciprocal(m[:, 2], m[:, 1])
                dve.drain()
                dve.tensor_tensor(pr[:], pr[:], bcast(m[:, 2], NE), ALU.mult)
                dve.drain()

            def best(n):
                for t in range(T):
                    dve.max(top[:, t], pr[:, t])
                dve.drain()
                for t in range(T):
                    dve.max_index(topi[:, t], top[:, t], pr[:, t])
                dve.tensor_tensor(m[:, 1], top[:, :, 0], top[:, :, 1], ALU.add)
                dve.drain()

            def chosen(n):
                dve.tensor_scalar(m[:, 2], m[:, 1], 1e-9, None, ALU.add)
                dve.tensor_copy(topf[:], topi[:])
                dve.drain()
                dve.reciprocal(m[:, 3], m[:, 2])
                for j in range(2):
                    dve.tensor_tensor(hot[:, j], iota[:], topf[:, :, j:j + 1].to_broadcast([P, T, NE]), ALU.is_equal)
                dve.drain()

            def weights(n):
                dve.tensor_tensor(hot[:, 0], hot[:, 0], hot[:, 1], ALU.add)
                dve.tensor_tensor(wt[:], pr[:], bcast(m[:, 3], NE), ALU.mult)
                dve.drain()
                dve.tensor_tensor(wt[:], wt[:], hot[:, 0], ALU.mult)
                dve.drain()

            def parts(n):
                dve.tensor_copy(w3b[:, :, 0], wt[:])
                dve.drain()
                dve.tensor_tensor(rest[:, 0], wt[:], w3b[:, :, 0], ALU.subtract)
                dve.drain()
                dve.tensor_copy(w3b[:, :, 1], rest[:, 0])
                dve.drain()
                dve.tensor_tensor(rest[:, 1], rest[:, 0], w3b[:, :, 1], ALU.subtract)
                dve.drain()
                dve.tensor_copy(w3b[:, :, 2], rest[:, 1]).then_inc(s["w_ready"], 1)

            def hidden(n, j, b):
                r, buf = slice(0, size[j]), (j + b) % 2
                kit.hold(dve, s["gated"], n * CH + j + 1)
                dve.tensor_tensor(up[r, buf], ps_u[r, buf, 1], gate[r, buf], ALU.mult)
                dve.drain()
                kit.hold(dve, s["wide"], n * CH + j + 1)
                dve.tensor_tensor(hid[r, buf], ps_w[r], up[r, buf], ALU.mult).then_inc(s["hidden"], 1)

            def block_of(i, n, b):
                for j in range(CH):
                    hidden(i, j, b)
                    if n is not None:
                        if j == 9:
                            split(n, 1 - b)
                        {0: variance, 3: shifted, 4: shares, 5: best, 6: chosen, 7: weights, 8: parts}.get(j, lambda n: None)(n)
                rows = H[:, bass.ds(i * T, T), :]
                dve.tensor_tensor(acc[:], X2[:, bass.ds(i * T, T), :], rows, ALU.add)
                dve.drain()
                kit.hold(dve, s["down"], i + 1)
                dve.tensor_tensor(rows, acc[:], ps_d[:, 0:T * D].rearrange("p (t d) -> p t d", t=T), ALU.add).then_inc(s["out"], 1)

            variance(0)
            shifted(0)
            split(0, 0)
            for piece in (shares, best, chosen, weights, parts):
                piece(0)
            with dve.Fori(0, BLOCKS // 2 - 1) as i:
                block_of(i * 2, i * 2 + 1, 0)
                block_of(i * 2 + 1, i * 2 + 2, 1)
            block_of(BLOCKS - 2, BLOCKS - 1, 0)
            block_of(BLOCKS - 1, None, 1)

        @block.scalar
        def _(act):
            act.wait_ge(s["w_in"], 112)

            def flat_at(n):
                kit.hold(act, s["flt_done"], n + 1)
                act.activation(flt[:], ps_r[:], ACT.Copy, scale=ln2[:]).then_inc(s["flt_out"], 1)
                act.drain()

            def whole(b):
                act.activation(xa[:, b], flt[:], ACT.Copy)

            def lower(b):
                act.activation(xb[0:64, b], flt[0:64], ACT.Copy).then_inc(s["x0_out"], 1)

            def turned(n, b):
                kit.hold(act, s["wtt_done"], n + 1)
                act.activation(wtt[:, b], ps_x[0:24, 0:W], ACT.Copy).then_inc(s["wtt_out"], 1)

            def block_of(i, n, b):
                for j in range(CH):
                    r, buf = slice(0, size[j]), (j + b) % 2
                    kit.hold(act, s["ups"], i * CH + j + 1)
                    act.activation(gate[r, buf], ps_u[r, buf, 0], ACT.Silu).then_inc(s["gated"], 1)
                    if n is not None:
                        if j == 2:
                            flat_at(n)
                        if j == 3:
                            whole(1 - b)
                        if j == 4:
                            lower(1 - b)
                        if j == 9:
                            turned(n, 1 - b)

            flat_at(0)
            whole(0)
            lower(0)
            turned(0, 0)
            with act.Fori(0, BLOCKS // 2 - 1) as i:
                block_of(i * 2, i * 2 + 1, 0)
                block_of(i * 2 + 1, i * 2 + 2, 1)
            block_of(BLOCKS - 2, BLOCKS - 1, 0)
            block_of(BLOCKS - 1, None, 1)

        @block.tensor
        def _(pe):
            pe.wait_ge(s["w_in"], 112)
            pe.wait_ge(s["ready"], 2)
            pe.wait_ge(s["half_ready"], 2)
            skip = dict(skip_group_check=True)

            def turn_rows(n):
                kit.hold(pe, s["fl_ready"], n + 1)
                for t in range(T):
                    mm = pe.transpose(ps_r[:, P * t:P * t + P], fl[:, t].rearrange("p k d -> p (k d)"), ident[:])
                mm.then_inc(s["flt_done"], 1)

            def router(n, b):
                kit.hold(pe, s["flt_out"], n + 1)
                for t in range(T):
                    mm = pe.matmul(ps_r[:, NE * t:NE * t + NE], flt[0:64, P * t:P * t + P], wr[:], start=True, stop=True)
                mm.then_inc(s["router"], 1)

            def turn_weights(n):
                kit.hold(pe, s["w_ready"], n + 1)
                for t in range(T):
                    mm = pe.transpose(ps_x[0:24, P * t:P * t + P], w3b[:, t].rearrange("p k e -> p (k e)"), identb[:])
                mm.then_inc(s["wtt_done"], 1)

            def ups(i, j, b):
                r = slice(0, size[j])
                cols = slice(P * j, P * j + size[j])
                for which in range(2):
                    for part, x in ((0, xa), (1, xa), (2, xb)):
                        mm = pe.matmul(ps_u[r, (j + b) % 2, which], w_split[:, which, part, cols], x[:, b], start=(part == 0), stop=(part == 2))
                mm.then_inc(s["ups"], 1)

            def wide(i, j, b):
                r = slice(0, size[j])
                pe.matmul(ps_w[r], spread[:, P * j:P * j + size[j]], wtt[:, b], start=True, stop=True).then_inc(s["wide"], 1)

            def block_of(i, n, b):
                for j in range(CH):
                    if j + 1 < CH:
                        ups(i, j + 1, b)
                    elif n is not None:
                        kit.hold(pe, s["split"], n + 1)
                        ups(n, 0, 1 - b)
                    kit.hold(pe, s["hidden"], i * CH + j + 1)
                    if j + 1 < CH:
                        wide(i, j + 1, b)
                    elif n is not None:
                        kit.hold(pe, s["wtt_out"], n + 1)
                        wide(n, 0, 1 - b)
                    r = slice(0, size[j])
                    for t in range(T):
                        mm = pe.matmul(ps_d[:, D * t:D * t + D], hid[r, (j + b) % 2, P * t:P * t + P], w2[r, j, :],
                                       start=(j == 0 and t == 0), stop=(j == CH - 1 and t == T - 1), **skip)
                    if n is not None:
                        if j == 1:
                            turn_rows(n)
                        if j == 2:
                            router(n, 1 - b)
                        if j == 9:
                            turn_weights(n)
                mm.then_inc(s["down"], 1)

            turn_rows(0)
            router(0, 0)
            turn_weights(0)
            pe.wait_ge(s["split"], 1)
            ups(0, 0, 0)
            pe.wait_ge(s["wtt_out"], 1)
            wide(0, 0, 0)
            with pe.Fori(0, BLOCKS // 2 - 1) as i:
                block_of(i * 2, i * 2 + 1, 0)
                block_of(i * 2 + 1, i * 2 + 2, 1)
            block_of(BLOCKS - 2, BLOCKS - 1, 0)
            block_of(BLOCKS - 1, None, 1)


def store_rows(nc, kit, H, dram, name):
    with ExitStack() as c:
        stored = kit.sem(c, "stored_" + name)
        block = kit.block(c)

        @block.sync
        def _(sp):
            sp.dma_start(dram.rearrange("s (two p) d -> p (s two) d", p=P), H[:]).then_inc(stored, 16)
            sp.wait_ge(stored, 16)


UNDERFLOW = -104.0


def mamba(nc, kit, a, H, bc_dram):
    CHUNKS, SC = 8, 8
    PIECES = SC // 2
    TC = SC * LEN // P
    W = 2 * LEN
    CW = SC * LEN
    NS, DI, RANK = 64, 128, 16
    GROUP = 8
    with ExitStack() as c:
        sb = lambda n, s, d=F32: kit.sb(c, n, s, d)
        sem = lambda n: kit.sem(c, n)
        ident = sb("ident6", [P, P])
        w_in = sb("w_in6w", [D, 2 * DI])
        w_x = sb("w_x6", [DI, RANK + 2 * NS])
        w_dt = sb("w_dt6", [RANK, DI])
        w_out = sb("w_out6", [DI, D])
        chan = sb("chan6", [DI, 7])
        A = sb("A6", [DI, NS])
        before = sb("before6", [NS, NS])
        slots = sb("slots6", [NS, NS])
        slots_i = sb("slots_i6", [NS, NS], I32)
        index = sb("index6", [NS, 1])
        index_i = sb("index_i6", [NS, 1], I32)
        half = sb("half6", [P, TC])
        keep = sb("keep6", [P, SC, LEN])
        cen = sb("cen6", [P, TC, D])
        sq = sb("sq6", [P, TC, D])
        st = sb("st6", [P, 3, TC])
        var = sb("var6", [P, TC])
        rs = sb("rs6", [P, TC])
        x = sb("x6", [P, TC, D])
        xt = sb("xt6", [D, PIECES, W])
        xpad = sb("xpad6", [DI, SC, LEN + 3])
        u = sb("u6", [DI, SC, LEN])
        dl = sb("dl6", [RANK, 2, W])
        bc = sb("bc6", [2 * NS, SC, LEN])
        delta = sb("delta6", [DI, SC, LEN])
        S = sb("S6", [DI, SC, LEN])
        DU = sb("DU6", [DI, SC, LEN])
        Y = sb("Y6", [DI, SC, LEN])
        Gt = sb("G6", [DI, SC, LEN])
        last_c = sb("last_c6", [NS, SC])
        least = sb("least6", [DI, 1])
        cand = sb("cand6", [DI, NS])
        flag = sb("flag6", [NS, 4])
        place = sb("place6", [NS, NS])
        dead = sb("dead6", [NS, DI])
        lastbc = sb("lastbc6", [NS, SC])
        tail = sb("tail6", [DI, SC])
        todo = sb("todo6", [1, NS + 2])
        todo_i = sb("todo_i6", [1, NS + 2], I32)
        acol = sb("acol6", [DI, 1])
        tiny = sb("tiny6", [DI, 1])
        Bb = sb("Bb6", [DI, SC, LEN])
        Cb = sb("Cb6", [DI, SC, LEN])
        e = sb("e6", [DI, SC, LEN])
        r = sb("r6", [DI, SC, LEN])
        t = sb("t6", [DI, SC, LEN])
        conv, az, rl, ey, lw, yg = t, e, r, Bb, Cb, e
        ps_x = [kit.ps(c, f"ps_x6{b}", [P, W]) for b in range(2)]
        ps_i = [kit.ps(c, f"ps_i6{b}", [P, W]) for b in range(2)]
        ps_g = kit.ps(c, "ps_g6", [P, W])
        ps_b = kit.ps(c, "ps_b6", [P, W])
        ps_f = kit.ps(c, "ps_f6", [P, W])
        ps_o = [kit.ps(c, "ps_o6", [P, W]), ps_b]
        names = ("w_in consts var_ready rs_ready x_ready xt_done xt_out in_done xi_out conv_ready u_ready y_ready dl_done dl_out dt_done z_out "
                 "bc_done bc_out bc_stored ey_ready lw_ready cand_ready cand_done flag_ready rank_done place_ready list_done "
                 "todo_ready acol_ready e_ready r_ready bc_in bc_free scanned yg_ready o_done h_out g_ready").split()
        s = {n: sem(n + "_6") for n in names}
        block = kit.block(c)

        def flat(ap):
            return ap.rearrange("p a l -> p (a l)")

        def pair(ps):
            return ps[:].rearrange("p (a l) -> p a l", a=2)

        @block.sync
        def _(sp):
            for dst, src in ((ident[:], a["ident"]), (w_in[:], a["mb_win"]), (w_x[:], a["mb_wx"]), (w_dt[:], a["mb_wdt"]),
                             (w_out[:], a["mb_wout"]), (chan[:], a["mb_chan"]), (A[:], a["mb_alog"]), (before[:], a["before"])):
                sp.dma_start(dst, src).then_inc(s["w_in"], 16)
            with sp.Fori(0, CHUNKS) as ch:
                kit.hold(sp, s["bc_out"], (ch + 1) * PIECES)
                sp.dma_start(bc_dram.rearrange("j n (g w) -> g (j n) w", w=CW)[bass.ds(ch, 1), :, :].rearrange("g n w -> (g n) w"),
                             flat(bc[:])).then_inc(s["bc_stored"], 16)
                kit.hold(sp, s["bc_stored"], ch * 16 + 32)
                kit.hold(sp, s["todo_ready"], ch + 1)
                count = sp.value_load(todo_i[0:1, NS:NS + 1], min_val=0, max_val=NS)
                done = sp.value_load(todo_i[0:1, NS + 1:NS + 2], min_val=0, max_val=NS * CHUNKS)
                with sp.Fori(0, NS // GROUP) as group:
                    with sp.If(group * GROUP < count):
                        with sp.Fori(0, GROUP) as within:
                            k = group * GROUP + within
                            with sp.If(k < count):
                                state = sp.value_load(todo_i[0:1, bass.ds(k, 1)], min_val=0, max_val=NS - 1)
                                kit.hold(sp, s["bc_free"], done + k + 1)
                                for j, dst in ((0, Bb), (1, Cb)):
                                    row = bc_dram[j, bass.ds(state, 1), bass.ds(ch * CW, CW)]
                                    sp.dma_start(flat(dst[:]), row.to_broadcast([DI, CW])).then_inc(s["bc_in"], 16)

        @block.gpsimd
        def _(pool):
            pool.memset(half[:], -0.5)
            pool.iota(slots_i[:], pattern=[[1, NS]], base=0, channel_multiplier=0)
            pool.iota(index_i[:], pattern=[[0, 1]], base=0, channel_multiplier=1).then_inc(s["consts"], 1)
            pool.drain()
            with pool.Fori(0, CHUNKS) as n:
                kit.hold(pool, s["var_ready"], n + 1)
                pool.tensor_tensor(rs[:], var[:], half[:], ALU.pow).then_inc(s["rs_ready"], 1)

        @block.scalar
        def _(act):
            act.wait_ge(s["w_in"], 128)
            act.wait_ge(s["consts"], 2)
            act.activation(A[:], A[:], ACT.Exp).then_inc(s["consts"], 1)
            with act.Fori(0, CHUNKS) as ch:
                def count(p):
                    return ch * PIECES + p + 1

                def two(p):
                    return slice(2 * p, 2 * p + 2)

                def tokens(p):
                    kit.hold(act, s["xt_done"], count(p))
                    act.activation(xt[:, p], ps_x[p % 2][0:D, :], ACT.Copy).then_inc(s["xt_out"], 1)

                def halves(p):
                    kit.hold(act, s["in_done"], count(p))
                    act.activation(xpad[:, two(p), 3:LEN + 3], pair(ps_i[p % 2]), ACT.Copy).then_inc(s["xi_out"], 1)
                    act.activation(Gt[:, two(p), :], pair(ps_g), ACT.Silu).then_inc(s["g_ready"], 1)

                def convolved(p):
                    kit.hold(act, s["conv_ready"], count(p))
                    act.activation(u[:, two(p)], conv[:, two(p)], ACT.Silu, bias=chan[:, 4:5]).then_inc(s["u_ready"], 1)

                def projected(p):
                    kit.hold(act, s["dl_done"], count(p))
                    act.activation(dl[:, p % 2], ps_x[p % 2][0:RANK, :], ACT.Copy).then_inc(s["dl_out"], 1)
                    if p == 0:
                        kit.hold(act, s["bc_stored"], ch * 16 + 16)
                    kit.hold(act, s["bc_done"], count(p))
                    act.activation(bc[:, two(p)], pair(ps_b), ACT.Copy).then_inc(s["bc_out"], 1)

                def sizes(p):
                    kit.hold(act, s["dt_done"], count(p))
                    act.activation(az[:, two(p)], pair(ps_i[p % 2]), ACT.Abs, bias=chan[:, 5:6])
                    act.activation(rl[:, two(p)], pair(ps_i[p % 2]), ACT.Relu, bias=chan[:, 5:6]).then_inc(s["z_out"], 1)

                tokens(0)
                tokens(1)
                halves(0)
                tokens(2)
                halves(1)
                tokens(3)
                halves(2)
                convolved(0)
                projected(0)
                halves(3)
                convolved(1)
                sizes(0)
                projected(1)
                convolved(2)
                sizes(1)
                projected(2)
                convolved(3)
                sizes(2)
                projected(3)
                sizes(3)
                act.activation(Y[:], u[:], ACT.Copy, scale=chan[:, 6:7]).then_inc(s["y_ready"], 1)
                act.drain()
                act.activation(ey[:], az[:], ACT.Exp, scale=-1.0).then_inc(s["ey_ready"], 1)
                act.drain()
                act.activation(lw[:], ey[:], ACT.Ln, bias=1.0).then_inc(s["lw_ready"], 1)
                kit.hold(act, s["todo_ready"], ch + 1)
                count = act.value_load(todo_i[0:1, NS:NS + 1], min_val=0, max_val=NS)
                done = act.value_load(todo_i[0:1, NS + 1:NS + 2], min_val=0, max_val=NS * CHUNKS)
                with act.Fori(0, NS // GROUP) as group:
                    with act.If(group * GROUP < count):
                        with act.Fori(0, GROUP) as within:
                            k = group * GROUP + within
                            with act.If(k < count):
                                kit.hold(act, s["acol_ready"], done + k + 1)
                                act.activation(e[:], S[:], ACT.Exp, scale=acol[:]).then_inc(s["e_ready"], 1)
                                act.drain()
                                act.activation(r[:], e[:], ACT.Ln, bias=tiny[:])
                                act.drain()
                                act.activation(r[:], r[:], ACT.Exp, scale=-1.0).then_inc(s["r_ready"], 1)

        @block.vector
        def _(dve):
            dve.sem_inc(s["bc_stored"], 16)
            dve.sem_inc(s["bc_free"], 1)
            dve.memset(xpad[:], 0.0)
            dve.memset(S[:], 0.0)
            dve.memset(tiny[:], 1e-12)
            dve.memset(todo[:], 0.0)
            dve.memset(keep[:], 1.0)
            dve.drain()
            dve.memset(keep[:, :, 0:1], 0.0).then_inc(s["consts"], 1)
            dve.wait_ge(s["w_in"], 128)
            dve.wait_ge(s["consts"], 3)
            dve.tensor_scalar(A[:], A[:], -1.0, None, ALU.mult)
            dve.tensor_copy(slots[:], slots_i[:])
            dve.tensor_copy(index[:], index_i[:])
            dve.drain()
            with dve.Fori(0, CHUNKS) as ch:
                norm_statistics(dve, H[:, bass.ds(ch * TC, TC), :], cen[:], sq[:], st)
                dve.tensor_scalar(var[:], st[:, 2], 1.0 / D, LN_EPS, ALU.mult, ALU.add).then_inc(s["var_ready"], 1)
                kit.hold(dve, s["rs_ready"], ch + 1)
                dve.tensor_tensor(x[:], cen[:], bcast(rs[:], D), ALU.mult).then_inc(s["x_ready"], 1)
                for p in range(PIECES):
                    two = slice(2 * p, 2 * p + 2)
                    kit.hold(dve, s["xi_out"], ch * PIECES + p + 1)
                    dve.tensor_scalar(conv[:, two], xpad[:, two, 0:LEN], chan[:, 0:1], None, ALU.mult)
                    for tap in range(1, 4):
                        dve.drain()
                        w = dve.scalar_tensor_tensor(conv[:, two], xpad[:, two, tap:tap + LEN], chan[:, tap:tap + 1], conv[:, two], ALU.mult, ALU.add)
                    w.then_inc(s["conv_ready"], 1)
                kit.hold(dve, s["ey_ready"], ch + 1)
                dve.tensor_scalar(az[:], ey[:], 1.0, -1.0, ALU.add, ALU.add)
                dve.drain()
                dve.tensor_tensor(az[:], ey[:], az[:], ALU.subtract)
                dve.drain()
                dve.tensor_tensor(az[:], az[:], rl[:], ALU.add)
                dve.drain()
                kit.hold(dve, s["lw_ready"], ch + 1)
                dve.tensor_tensor(delta[:], az[:], lw[:], ALU.add)
                dve.drain()
                dve.tensor_tensor(DU[:], delta[:], u[:], ALU.mult)
                for j in range(SC):
                    dve.tensor_tensor_scan(S[:, j, LEN - 2::-1], keep[:, 0, 1:LEN], delta[:, j, :0:-1], 0.0, ALU.mult, ALU.add)
                dve.tensor_copy(last_c[:], bc[NS:2 * NS, :, LEN - 1])
                dve.drain()
                dve.tensor_reduce(least[:], S[:, :, LEN - 2], AX_X, ALU.min)
                dve.drain()
                dve.tensor_scalar(cand[:], A[:], least[:], None, ALU.mult).then_inc(s["cand_ready"], 1)
                kit.hold(dve, s["cand_done"], ch + 1)
                dve.tensor_reduce(flag[:, 0:1], ps_f[0:NS, 0:DI], AX_X, ALU.max)
                dve.drain()
                dve.tensor_scalar(flag[:, 2:3], flag[:, 0:1], UNDERFLOW, None, ALU.is_lt)
                dve.drain()
                dve.tensor_scalar(flag[:, 1:2], flag[:, 2:3], -1.0, 1.0, ALU.mult, ALU.add)
                dve.tensor_tensor(lastbc[:], bc[0:NS, :, LEN - 1], last_c[:], ALU.mult)
                dve.tensor_copy(dead[:], flag[:, 2:3].to_broadcast([NS, DI])).then_inc(s["flag_ready"], 1)
                kit.hold(dve, s["rank_done"], ch + 1)
                dve.tensor_copy(flag[:, 3:4], ps_f[0:NS, 128:129])
                dve.tensor_tensor(tail[:], ps_f[:, 192:192 + SC], DU[:, :, LEN - 1], ALU.mult)
                dve.drain()
                dve.tensor_scalar(place[:], slots[:], flag[:, 3:4], flag[:, 1:2], ALU.is_equal, ALU.mult).then_inc(s["place_ready"], 1)
                kit.hold(dve, s["y_ready"], ch + 1)
                dve.tensor_tensor(Y[:, :, LEN - 1], Y[:, :, LEN - 1], tail[:], ALU.add)
                dve.tensor_tensor(todo[:, NS + 1:NS + 2], todo[:, NS + 1:NS + 2], todo[:, NS:NS + 1], ALU.add)
                dve.drain()
                kit.hold(dve, s["list_done"], ch + 1)
                dve.tensor_copy(todo[:, 0:NS + 1], ps_f[0:1, 256:256 + NS + 1])
                dve.drain()
                dve.tensor_copy(todo_i[:], todo[:]).then_inc(s["todo_ready"], 1)
                kit.hold(dve, s["todo_ready"], ch + 1)
                count = dve.value_load(todo_i[0:1, NS:NS + 1], min_val=0, max_val=NS)
                done = dve.value_load(todo_i[0:1, NS + 1:NS + 2], min_val=0, max_val=NS * CHUNKS)
                with dve.Fori(0, NS // GROUP) as group:
                    with dve.If(group * GROUP < count):
                        with dve.Fori(0, GROUP) as within:
                            k = group * GROUP + within
                            with dve.If(k < count):
                                state = dve.value_load(todo_i[0:1, bass.ds(k, 1)], min_val=0, max_val=NS - 1)
                                dve.tensor_copy(acol[:], A[:, bass.ds(state, 1)]).then_inc(s["acol_ready"], 1)
                                kit.hold(dve, s["bc_in"], (done + k + 1) * 32)
                                dve.tensor_tensor(t[:], DU[:], Bb[:], ALU.mult)
                                dve.drain()
                                kit.hold(dve, s["e_ready"], done + k + 1)
                                dve.tensor_tensor(t[:], t[:], e[:], ALU.mult)
                                dve.drain()
                                dve.tensor_tensor_scan(flat(t[:]), flat(keep[:]), flat(t[:]), 0.0, ALU.mult, ALU.add)
                                dve.drain()
                                kit.hold(dve, s["r_ready"], done + k + 1)
                                dve.tensor_tensor(t[:], t[:], r[:], ALU.mult)
                                dve.drain()
                                dve.tensor_tensor(t[:], t[:], Cb[:], ALU.mult).then_inc(s["bc_free"], 1)
                                dve.drain()
                                dve.tensor_tensor(Y[:], Y[:], t[:], ALU.add)
                                dve.drain()
                kit.hold(dve, s["g_ready"], (ch + 1) * PIECES)
                for p in range(PIECES):
                    two = slice(2 * p, 2 * p + 2)
                    dve.tensor_tensor(yg[:, two], Y[:, two], Gt[:, two], ALU.mult).then_inc(s["yg_ready"], 1)
                for g in range(2):
                    kit.hold(dve, s["o_done"], ch * 2 + g + 1)
                    rows = H[:, bass.ds(ch * TC + g * (TC // 2), TC // 2), :]
                    dve.tensor_tensor(rows, rows, ps_o[g][:].rearrange("p (t d) -> p t d", d=D), ALU.add).then_inc(s["h_out"], 1)
                dve.drain()

        @block.tensor
        def _(pe):
            pe.wait_ge(s["w_in"], 128)
            pe.wait_ge(s["consts"], 3)
            with pe.Fori(0, CHUNKS) as ch:
                def count(p):
                    return ch * PIECES + p + 1

                def turn(p):
                    if p > 1:
                        kit.hold(pe, s["xt_out"], count(p - 2))
                    for t4 in range(4):
                        mm = pe.transpose(ps_x[p % 2][0:D, P * t4:P * t4 + P], x[:, 4 * p + t4, :], ident[:])
                    mm.then_inc(s["xt_done"], 1)

                def inner(p):
                    kit.hold(pe, s["xt_out"], count(p))
                    if p > 0:
                        kit.hold(pe, s["g_ready"], count(p - 1))
                    pe.matmul(ps_i[p % 2][:], w_in[:, 0:DI], xt[:, p], start=True, stop=True)
                    pe.matmul(ps_g[:], w_in[:, DI:2 * DI], xt[:, p], start=True, stop=True).then_inc(s["in_done"], 1)

                def project(p):
                    kit.hold(pe, s["u_ready"], count(p))
                    if p > 0:
                        kit.hold(pe, s["bc_out"], count(p - 1))
                    pe.matmul(ps_x[p % 2][0:RANK, :], w_x[:, 0:RANK], u[:, 2 * p:2 * p + 2], start=True, stop=True).then_inc(s["dl_done"], 1)
                    pe.matmul(ps_b[:], w_x[:, RANK:RANK + 2 * NS], u[:, 2 * p:2 * p + 2], start=True, stop=True).then_inc(s["bc_done"], 1)

                def sizes(p):
                    kit.hold(pe, s["dl_out"], count(p))
                    if p > 1:
                        kit.hold(pe, s["z_out"], count(p - 2))
                    else:
                        kit.hold(pe, s["xi_out"], count(p + 2))
                    pe.matmul(ps_i[p % 2][:], w_dt[:], dl[:, p % 2], start=True, stop=True).then_inc(s["dt_done"], 1)

                kit.hold(pe, s["x_ready"], ch + 1)
                turn(0)
                turn(1)
                inner(0)
                turn(2)
                inner(1)
                turn(3)
                inner(2)
                project(0)
                inner(3)
                sizes(0)
                project(1)
                sizes(1)
                project(2)
                sizes(2)
                project(3)
                sizes(3)
                kit.hold(pe, s["cand_ready"], ch + 1)
                pe.transpose(ps_f[0:NS, 0:DI], cand[:], ident[:]).then_inc(s["cand_done"], 1)
                kit.hold(pe, s["flag_ready"], ch + 1)
                pe.matmul(ps_f[0:NS, 128:129], before[:], flag[:, 1:2], start=True, stop=True)
                pe.matmul(ps_f[:, 192:192 + SC], dead[:], lastbc[:], start=True, stop=True).then_inc(s["rank_done"], 1)
                kit.hold(pe, s["place_ready"], ch + 1)
                pe.matmul(ps_f[0:1, 256:256 + NS], index[:], place[:], start=True, stop=True)
                pe.matmul(ps_f[0:1, 256 + NS:257 + NS], flag[:, 1:2], flag[:, 1:2], start=True, stop=True).then_inc(s["list_done"], 1)
                for p in range(PIECES):
                    kit.hold(pe, s["yg_ready"], ch * PIECES + p + 1)
                    for t4 in range(4):
                        at = D * (4 * (p % 2) + t4)
                        mm = pe.matmul(ps_o[p // 2][:, at:at + D], flat(yg[:])[:, P * (4 * p + t4):P * (4 * p + t4) + P], w_out[:], start=True, stop=True)
                    if p % 2:
                        mm.then_inc(s["o_done"], 1)

def sparse_experts(nc, kit, a, H, out):
    NE, HID = 64, 128
    SLOTS = 2 * TILES + NE
    with ExitStack() as top:
        GATE = kit.sb(top, "GATE", [P, 2, TILES])
        SLOT = kit.sb(top, "SLOT", [P, 2, TILES], U32)
        OWNER = kit.sb(top, "OWNER", [1, SLOTS], I32)
        xs = nc.dram_tensor("xs_dram", (SLOTS * P, D), F32).ap()
        ys = nc.dram_tensor("ys_dram", (SLOTS * P, D), F32).ap()
        route_and_scatter(nc, kit, a, H, GATE, SLOT, OWNER, xs, SLOTS)
        run_experts(nc, kit, a, OWNER, xs, ys, SLOTS)
        combine(nc, kit, H, GATE, SLOT, ys, out)


def route_and_scatter(nc, kit, a, H, GATE, SLOT, OWNER, xs, SLOTS):
    NE, T = 64, 4
    STEPS = TILES // T
    G = 8
    Z = 2048
    with ExitStack() as c:
        sb = lambda n, s, d=F32: kit.sb(c, n, s, d)
        sem = lambda n: kit.sem(c, n)
        X = sb("X9", [P, TILES, D])
        ident = sb("ident9", [P, P])
        wr = sb("wr9", [D + 1, NE])
        prior_f = sb("prior_f9", [P, P])
        prior = sb("prior9", [P, P], BF16)
        ones = sb("ones9", [P, P], BF16)
        onesf = sb("onesf9", [P, P])
        zero = sb("zero9", [P, Z])
        iota_i = sb("iota_i9", [P, G, NE], I32)
        iota = sb("iota9", [P, G, NE])
        thr_i = sb("thr_i9", [P, 1], I32)
        thr = sb("thr9", [P, 1])
        kth_i = sb("kth_i9", [NE, SLOTS], I32)
        kth = sb("kth9", [NE, SLOTS])
        half = sb("half9", [P, T])
        cen = sb("cen9", [P, T, D])
        sq = sb("sq9", [P, T, D])
        st = sb("st9", [P, 3, T])
        var = sb("var9", [P, T])
        rs = sb("rs9", [P, T])
        x = sb("x9", [P, T, D])
        xt = sb("xt9", [D + 1, T * P])
        lg = sb("lg9", [P, T, NE])
        top = sb("top9", [P, T, 8])
        topi = sb("topi9", [P, T, 8], U32)
        hot = sb("hot9", [P, 2, T, NE])
        both = sb("both9", [P, T, NE], BF16)
        mt = sb("mt9", [P, 2, T, NE])
        seen = sb("seen9", [P, NE])
        seen_add = sb("seen_add9", [P, NE])
        seen_b = sb("seen_b9", [P, NE], BF16)
        L1 = sb("L1_9", [P, 2, TILES])
        IDX = sb("IDX9", [P, 2, TILES])
        RANK = sb("RANK9", [P, 2, TILES])
        total = sb("total9", [P, NE])
        full = sb("full9", [P, NE])
        tiles = sb("tiles9", [P, NE])
        end = sb("end9", [P, NE])
        base = sb("base9", [P, NE])
        endc = sb("endc9", [NE, 1])
        past = sb("past9", [NE, SLOTS])
        own = sb("own9", [1, SLOTS])
        big = sb("big9", [P, G, NE])
        off = sb("off9", [P, G])
        rows = sb("rows9", [P, 2, G, D])
        slot_now = sb("slot_now9", [P, 2, 2, G], U32)
        ps_x = kit.ps(c, "ps_x9", [P, T * P])
        ps_l = kit.ps(c, "ps_l9", [P, 512])
        ps_r = kit.ps(c, "ps_r9", [P, 512])
        ps_m = kit.ps(c, "ps_m9", [P, 512])
        names = ("w_in consts ready var_ready rs_ready x_ready xt_done xt_out l_done both_ready r_done seen_ready cleared "
                 "total_done full_ready tiles_done end_ready endc_done past_ready own_done diff_ready exp_done slots_ready rows_ready "
                 ).split()
        s = {n: sem(n + "_9") for n in names}
        s["scattered"] = [sem("scattered0_9"), sem("scattered1_9")]
        block = kit.block(c)

        @block.sync
        def _(sp):
            for dst, src in ((ident[:], a["ident"]), (wr[:], a["moe1_wr"]), (prior_f[:], a["prior"])):
                sp.dma_start(dst, src).then_inc(s["w_in"], 16)
            sp.wait_ge(s["ready"], 1)
            per = P * Z // D
            for j in range(SLOTS * P // per):
                sp.dma_start(xs[j * per:(j + 1) * per, :].rearrange("(p r) d -> p (r d)", p=P), zero[:]).then_inc(s["cleared"], 16)

        @block.gpsimd
        def _(pool):
            pool.memset(half[:], -0.5)
            pool.iota(iota_i[:], pattern=[[0, G], [1, NE]], base=0, channel_multiplier=0)
            pool.iota(thr_i[:], pattern=[[0, 1]], base=0, channel_multiplier=P)
            pool.iota(kth_i[:], pattern=[[1, SLOTS]], base=0, channel_multiplier=0).then_inc(s["consts"], 1)
            pool.drain()
            with pool.Fori(0, STEPS) as n:
                kit.hold(pool, s["var_ready"], n + 1)
                pool.tensor_tensor(rs[:], var[:], half[:], ALU.pow).then_inc(s["rs_ready"], 1)
            pool.wait_ge(s["cleared"], 16 * (SLOTS * D // Z))
            with pool.Fori(0, TILES // G // 2) as i:
                for b in range(2):
                    n = i * 2 + b
                    kit.hold(pool, s["rows_ready"], n + 1)
                    pool.tensor_copy(slot_now[:, b], SLOT[:, :, bass.ds(n * G, G)])
                    pool.drain()
                    for t in range(G):
                        for j in range(2):
                            pool.indirect_dma_start(xs, bass.IndirectOffsetOnAxis(ap=slot_now[:, b, j, t:t + 1], axis=0),
                                                    rows[:, b, t, :], None).then_inc(s["scattered"][b], 16)
            for b in range(2):
                pool.wait_ge(s["scattered"][b], 16 * TILES)

        @block.scalar
        def _(act):
            act.wait_ge(s["ready"], 1)
            with act.Fori(0, STEPS) as n:
                kit.hold(act, s["xt_done"], n + 1)
                act.activation(xt[0:D, :], ps_x[0:D, :], ACT.Copy).then_inc(s["xt_out"], 1)
            act.wait_ge(s["diff_ready"], 1)
            act.activation(GATE[:, 1], GATE[:, 1], ACT.Exp).then_inc(s["exp_done"], 1)

        @block.vector
        def _(dve):
            dve.memset(zero[:], 0.0)
            dve.memset(xt[D:D + 1, :], 1.0)
            dve.memset(seen[:], 0.0)
            dve.memset(ones[:], 1.0)
            dve.memset(onesf[:], 1.0)
            dve.memset(seen_b[:], 0.0)
            dve.drain().then_inc(s["ready"], 1)
            dve.wait_ge(s["w_in"], 48)
            dve.wait_ge(s["consts"], 1)
            dve.tensor_copy(prior[:], prior_f[:])
            dve.tensor_copy(iota[:], iota_i[:])
            dve.tensor_copy(thr[:], thr_i[:])
            dve.tensor_copy(kth[:], kth_i[:])
            dve.drain().then_inc(s["ready"], 1)
            with dve.Fori(0, STEPS) as n:
                here = bass.ds(n * T, T)
                norm_statistics(dve, H[:, here, :], cen[:], sq[:], st)
                dve.tensor_scalar(var[:], st[:, 2], 1.0 / D, LN_EPS, ALU.mult, ALU.add).then_inc(s["var_ready"], 1)
                kit.hold(dve, s["rs_ready"], n + 1)
                dve.tensor_tensor(x[:], cen[:], bcast(rs[:], D), ALU.mult).then_inc(s["x_ready"], 1)
                dve.drain()
                dve.tensor_copy(X[:, here, :], x[:])
                kit.hold(dve, s["l_done"], n + 1)
                dve.tensor_copy(lg[:], ps_l[:, 0:T * NE].rearrange("p (t e) -> p t e", e=NE))
                dve.drain()
                for t in range(T):
                    dve.max(top[:, t], lg[:, t])
                dve.drain()
                for t in range(T):
                    dve.max_index(topi[:, t], top[:, t], lg[:, t])
                dve.tensor_copy(L1[:, :, here].rearrange("p j t -> p t j"), top[:, :, 0:2])
                dve.drain()
                dve.tensor_copy(IDX[:, :, here].rearrange("p j t -> p t j"), topi[:, :, 0:2])
                dve.drain()
                for j in range(2):
                    dve.tensor_tensor(hot[:, j], iota[:, 0:T], bcast(IDX[:, j, here], NE), ALU.is_equal)
                dve.drain()
                dve.tensor_tensor(both[:], hot[:, 0], hot[:, 1], ALU.add).then_inc(s["both_ready"], 1)
                dve.drain()
                dve.tensor_reduce(seen_add[:], both[:].rearrange("p t e -> p e t"), AX_X, ALU.add)
                kit.hold(dve, s["r_done"], n + 1)
                for j in range(2):
                    dve.tensor_tensor(mt[:, j], ps_r[:, 0:T * NE].rearrange("p (t e) -> p t e", e=NE), hot[:, j], ALU.mult)
                dve.drain()
                for j in range(2):
                    dve.tensor_reduce(RANK[:, j, here], mt[:, j], AX_X, ALU.add)
                dve.tensor_tensor(seen[:], seen[:], seen_add[:], ALU.add)
                dve.drain()
                dve.tensor_copy(seen_b[:], seen[:]).then_inc(s["seen_ready"], 1)
            dve.drain()
            dve.tensor_tensor(GATE[:, 1], L1[:, 1], L1[:, 0], ALU.subtract).then_inc(s["diff_ready"], 1)
            dve.wait_ge(s["total_done"], 1)
            dve.tensor_copy(total[:], ps_m[:, 0:NE])
            dve.drain()
            dve.tensor_scalar(full[:], total[:], thr[:], None, ALU.is_gt).then_inc(s["full_ready"], 1)
            dve.wait_ge(s["tiles_done"], 1)
            dve.tensor_copy(tiles[:], ps_m[:, NE:2 * NE])
            dve.drain()
            dve.tensor_tensor_scan(end[:], onesf[:, 0:NE], tiles[:], 0.0, ALU.mult, ALU.add).then_inc(s["end_ready"], 1)
            dve.drain()
            dve.tensor_tensor(base[:], end[:], tiles[:], ALU.subtract)
            dve.drain()
            dve.tensor_scalar(base[:], base[:], float(P), None, ALU.mult)
            dve.wait_ge(s["endc_done"], 1)
            dve.tensor_copy(endc[:], ps_m[0:NE, 128:129])
            dve.drain()
            dve.tensor_scalar(past[:], kth[:], endc[:], None, ALU.is_ge).then_inc(s["past_ready"], 1)
            dve.wait_ge(s["own_done"], 1)
            dve.tensor_scalar(own[:], ps_l[0:1, 0:SLOTS], float(NE - 1), None, ALU.min)
            dve.drain()
            dve.tensor_copy(OWNER[:], own[:])
            dve.wait_ge(s["exp_done"], 1)
            dve.tensor_scalar(L1[:, 0], GATE[:, 1], 1.0, None, ALU.add)
            dve.drain()
            dve.reciprocal(GATE[:, 0], L1[:, 0])
            dve.drain()
            dve.tensor_tensor(GATE[:, 1], GATE[:, 1], GATE[:, 0], ALU.mult)

            def place_rows(i, b):
                n = i * 2 + b
                here = bass.ds(n * G, G)
                for j in range(2):
                    dve.tensor_tensor(big[:], iota[:], bcast(IDX[:, j, here], NE), ALU.is_equal)
                    dve.drain()
                    dve.tensor_tensor(big[:], big[:], base[:].unsqueeze(1).to_broadcast([P, G, NE]), ALU.mult)
                    dve.drain()
                    dve.tensor_reduce(off[:], big[:], AX_X, ALU.add)
                    dve.drain()
                    dve.tensor_tensor(off[:], off[:], RANK[:, j, here], ALU.add)
                    dve.drain()
                    dve.tensor_copy(SLOT[:, j, here], off[:])
                if not isinstance(i, int):
                    kit.hold(dve, s["scattered"][b], i * (16 * 2 * G))
                dve.tensor_copy(rows[:, b], X[:, here, :])
                dve.drain().then_inc(s["rows_ready"], 1)

            place_rows(0, 0)
            place_rows(0, 1)
            with dve.Fori(1, TILES // G // 2) as i:
                for b in range(2):
                    place_rows(i, b)

        @block.tensor
        def _(pe):
            pe.wait_ge(s["w_in"], 48)
            pe.wait_ge(s["ready"], 2)
            skip = dict(skip_group_check=True)
            with pe.Fori(0, STEPS) as n:
                kit.hold(pe, s["x_ready"], n + 1)
                for t in range(T):
                    mm = pe.transpose(ps_x[0:D, P * t:P * t + P], x[:, t, :], ident[:])
                mm.then_inc(s["xt_done"], 1)
                kit.hold(pe, s["xt_out"], n + 1)
                for t in range(T):
                    mm = pe.matmul(ps_l[:, NE * t:NE * t + NE], xt[:, P * t:P * t + P], wr[:], start=True, stop=True)
                mm.then_inc(s["l_done"], 1)
                kit.hold(pe, s["both_ready"], n + 1)
                pe.matmul(ps_r[:, 0:T * NE], prior[:], both[:].rearrange("p t e -> p (t e)"), start=True, stop=False, **skip)
                for t in range(T):
                    src, to = (seen_b[:], T) if t == 0 else (both[:, t - 1], T - t)
                    mm = pe.matmul(ps_r[:, NE * (T - to):NE * T].rearrange("p (t e) -> p t e", e=NE), ones[:], src.unsqueeze(1).to_broadcast([P, to, NE]),
                                   start=False, stop=(t == T - 1), **skip)
                mm.then_inc(s["r_done"], 1)
            pe.wait_ge(s["seen_ready"], STEPS)
            pe.matmul(ps_m[:, 0:NE], ones[:], seen_b[:], start=True, stop=True).then_inc(s["total_done"], 1)
            pe.wait_ge(s["full_ready"], 1)
            pe.matmul(ps_m[:, NE:2 * NE], onesf[:], full[:], start=True, stop=True).then_inc(s["tiles_done"], 1)
            pe.wait_ge(s["end_ready"], 1)
            pe.matmul(ps_m[0:NE, 128:129], end[0:1, :], onesf[0:1, 0:1], start=True, stop=True).then_inc(s["endc_done"], 1)
            pe.wait_ge(s["past_ready"], 1)
            pe.matmul(ps_l[0:1, 0:SLOTS], onesf[0:NE, 0:1], past[:], start=True, stop=True).then_inc(s["own_done"], 1)


def run_experts(nc, kit, a, OWNER, xs, ys, SLOTS):
    NE, HID, T = 64, 128, 4
    GROUPS = SLOTS // T
    with ExitStack() as c:
        sb = lambda n, s, d=F32: kit.sb(c, n, s, d)
        sem = lambda n: kit.sem(c, n)
        ident = sb("ident10", [P, P])
        x = sb("x10", [P, 2, T, D])
        xt = sb("xt10", [D + 1, 2, T * P])
        w1 = sb("w1_10", [D + 1, 2, T, HID])
        w2 = sb("w2_10", [HID, 2, T, D])
        b2 = sb("b2_10", [1, 2, T, D])
        one = sb("one10", [1, P])
        h = sb("h10", [HID, 2, T * P])
        y = sb("y10", [P, 2, T, D])
        ps_x = kit.ps(c, "ps_x10", [P, T * P])
        ps_h = kit.ps(c, "ps_h10", [P, T * P])
        ps_y = kit.ps(c, "ps_y10", [P, 512])
        names = "w_in ready t_done xt_out h_done h_out y_done y_out".split()
        s = {n: sem(n + "_10") for n in names}
        s.update({n: [sem(n + "0_10"), sem(n + "1_10")] for n in ("x_in", "w_got", "stored")})
        block = kit.block(c)

        @block.sync
        def _(sp):
            sp.dma_start(ident[:], a["ident"]).then_inc(s["w_in"], 16)
            with sp.Fori(0, GROUPS // 2) as i:
                for b in range(2):
                    g = i * 2 + b
                    kit.hold(sp, s["t_done"], g + 1)
                    sp.dma_start(x[:, b], xs.rearrange("(g t p) d -> g p t d", t=T, p=P)[bass.ds(g, 1), :, :, :].rearrange("g p t d -> (g p) t d")).then_inc(s["x_in"][b], 16)
                    kit.hold(sp, s["y_done"], g + 1)
                    for t in range(T):
                        e = sp.value_load(OWNER[0:1, bass.ds(g * T + t, 1)], min_val=0, max_val=NE - 1)
                        sp.dma_start(w1[:, b, t], a["moe1_w1"][bass.ds(e, 1), :, :].rearrange("e k n -> (e k) n")).then_inc(s["w_got"][b], 16)
                        sp.dma_start(w2[:, b, t], a["moe1_w2"][bass.ds(e, 1), :, :].rearrange("e k n -> (e k) n")).then_inc(s["w_got"][b], 16)
                        sp.dma_start(b2[:, b, t], a["moe1_b2"][bass.ds(e, 1), :]).then_inc(s["w_got"][b], 16)

        @block.scalar
        def _(act):
            def rows(g, b):
                kit.hold(act, s["t_done"], g + 3)
                act.activation(xt[0:D, b], ps_x[0:D, :], ACT.Copy).then_inc(s["xt_out"], 1)

            def hidden(g, b):
                kit.hold(act, s["h_done"], g + 1)
                act.activation(h[:, b], ps_h[:], ACT.Relu).then_inc(s["h_out"], 1)

            def store(g, b):
                kit.hold(act, s["y_out"], g + 2)
                act.dma_start(ys.rearrange("(g t p) d -> g p t d", t=T, p=P)[bass.ds(g, 1), :, :, :].rearrange("g p t d -> (g p) t d"), y[:, b]).then_inc(s["stored"][b], 16)

            rows(0, 0)
            hidden(0, 0)
            with act.Fori(0, GROUPS // 2 - 1) as i:
                for b in range(2):
                    rows(i * 2 + b + 1, 1 - b)
                    store(i * 2 + b, b)
                    hidden(i * 2 + b + 1, 1 - b)
            rows(GROUPS - 1, 1)
            store(GROUPS - 2, 0)
            hidden(GROUPS - 1, 1)
            store(GROUPS - 1, 1)
            for b in range(2):
                act.wait_ge(s["stored"][b], 16 * (GROUPS // 2 + 1))

        @block.vector
        def _(dve):
            dve.memset(xt[D:D + 1, :, :], 1.0)
            dve.memset(one[:], 1.0)
            dve.drain().then_inc(s["ready"], 1)
            dve.sem_inc(s["t_done"], 2)
            dve.sem_inc(s["y_done"], 2)
            dve.sem_inc(s["y_out"], 1)
            dve.sem_inc(s["stored"][0], 16)
            dve.sem_inc(s["stored"][1], 16)
            with dve.Fori(0, GROUPS // 2) as i:
                for b in range(2):
                    g = i * 2 + b
                    kit.hold(dve, s["y_done"], g + 3)
                    kit.hold(dve, s["stored"][b], i * 16 + 16)
                    dve.tensor_copy(y[:, b], ps_y[:, 0:T * D].rearrange("p (t d) -> p t d", t=T)).then_inc(s["y_out"], 1)

        @block.tensor
        def _(pe):
            pe.wait_ge(s["w_in"], 16)
            pe.wait_ge(s["ready"], 1)
            skip = dict(skip_group_check=True)

            def turn(use, b):
                kit.hold(pe, s["x_in"][b], use * 16 + 16)
                for t in range(T):
                    mm = pe.transpose(ps_x[0:D, P * t:P * t + P], x[:, b, t, :], ident[:])
                mm.then_inc(s["t_done"], 1)

            def hidden(g, use, b):
                kit.hold(pe, s["xt_out"], g + 1)
                kit.hold(pe, s["w_got"][b], use * (48 * T) + 48 * T)
                for t in range(T):
                    mm = pe.matmul(ps_h[:, P * t:P * t + P], w1[:, b, t], xt[:, b, P * t:P * t + P], start=True, stop=True)
                mm.then_inc(s["h_done"], 1)

            def down(g, b):
                kit.hold(pe, s["h_out"], g + 1)
                kit.hold(pe, s["y_out"], g + 1)
                pe.matmul(ps_y[:, 0:T * D], one[:], b2[:, b].rearrange("o t d -> o (t d)"), start=True, stop=False, **skip)
                for t in range(T):
                    mm = pe.matmul(ps_y[:, D * t:D * t + D], h[:, b, P * t:P * t + P], w2[:, b, t], start=False, stop=True, **skip)
                mm.then_inc(s["y_done"], 1)

            turn(0, 0)
            hidden(0, 0, 0)
            with pe.Fori(0, GROUPS // 2 - 1) as i:
                for b in range(2):
                    turn(i + b, 1 - b)
                    down(i * 2 + b, b)
                    hidden(i * 2 + b + 1, i + b, 1 - b)
            turn(GROUPS // 2 - 1, 1)
            down(GROUPS - 2, 0)
            hidden(GROUPS - 1, GROUPS // 2 - 1, 1)
            down(GROUPS - 1, 1)


def combine(nc, kit, H, GATE, SLOT, ys, out):
    T = 8
    STEPS = TILES // T
    with ExitStack() as c:
        sb = lambda n, s, d=F32: kit.sb(c, n, s, d)
        sem = lambda n: kit.sem(c, n)
        now = sb("now11", [P, 2, 2, T], U32)
        got = sb("got11", [P, 2, 2, T, D])
        acc = sb("acc11", [P, 2, 2, T, D])
        picked = [sem("picked11_0"), sem("picked11_1")]
        free, ready = sem("free11"), sem("ready11")
        stored = [sem("stored11_0"), sem("stored11_1")]
        block = kit.block(c)

        @block.gpsimd
        def _(pool):
            with pool.Fori(0, STEPS // 2) as i:
                for b in range(2):
                    kit.hold(pool, free, i * 2 + b + 1)
                    pool.tensor_copy(now[:, b], SLOT[:, :, bass.ds((i * 2 + b) * T, T)])
                    pool.drain()
                    for t in range(T):
                        for j in range(2):
                            pool.indirect_dma_start(got[:, b, j, t, :], None, ys,
                                                    bass.IndirectOffsetOnAxis(ap=now[:, b, j, t:t + 1], axis=0)).then_inc(picked[b], 16)

        @block.vector
        def _(dve):
            dve.sem_inc(free, 2)
            dve.sem_inc(stored[0], 16)
            dve.sem_inc(stored[1], 16)
            with dve.Fori(0, STEPS // 2) as i:
                for b in range(2):
                    n = i * 2 + b
                    here = bass.ds(n * T, T)
                    kit.hold(dve, picked[b], (i + 1) * (32 * T))
                    kit.hold(dve, stored[b], i * 16 + 16)
                    dve.tensor_tensor(acc[:, b, 0], got[:, b, 0], bcast(GATE[:, 0, here], D), ALU.mult)
                    dve.tensor_tensor(acc[:, b, 1], got[:, b, 1], bcast(GATE[:, 1, here], D), ALU.mult).then_inc(free, 1)
                    dve.drain()
                    dve.tensor_tensor(acc[:, b, 0], acc[:, b, 0], acc[:, b, 1], ALU.add)
                    dve.drain()
                    dve.tensor_tensor(acc[:, b, 0], acc[:, b, 0], H[:, here, :], ALU.add).then_inc(ready, 1)

        @block.sync
        def _(sp):
            o = out.rearrange("s (two p) d -> p (s two) d", p=P)
            with sp.Fori(0, STEPS // 2) as i:
                for b in range(2):
                    n = i * 2 + b
                    kit.hold(sp, ready, n + 1)
                    sp.dma_start(o[:, bass.ds(n * T, T), :], acc[:, b, 0]).then_inc(stored[b], 16)
            for b in range(2):
                sp.wait_ge(stored[b], 16 * (STEPS // 2 + 1))


def build(nc, a, out):
    h1 = nc.dram_tensor("h1", (SEQ, LEN, D), F32).ap()
    with ExitStack() as top:
        kit = Kit(nc, top)
        with ExitStack() as c:
            H = kit.sb(c, "H_rows", [P, TILES, D])
            YT = kit.sb(c, "YT", [P, TILES // 2, P])
            LOGITS = kit.sb(c, "LOGITS", [P, 4, SEQ])
            MIX = kit.sb(c, "MIX", [P, 8, P])
            embed_and_logits(nc, kit, a, H, YT, LOGITS)
            row_softmax(nc, kit, a, LOGITS, MIX)
            row_attention_out(nc, kit, a, H, YT, MIX, h1)
        H = kit.sb(top, "H", [P, TILES, D])
        with ExitStack() as c:
            X2 = kit.sb(c, "X2", [P, TILES, D])
            causal_attention(nc, kit, a, h1, H, X2)
            dense_experts(nc, kit, a, H, X2)
        bc_dram = nc.dram_tensor("bc_dram", (2, 64, SEQ * LEN), F32).ap()
        mamba(nc, kit, a, H, bc_dram)
        sparse_experts(nc, kit, a, H, out)


def kernel(**inputs):
    import numpy as np
    import concourse.bacc as _bacc
    from concourse.bass_utils import run_bass_kernel_spmd as _run

    w = {k: np.ascontiguousarray(v) for k, v in inputs.items()}
    f32 = np.float32
    feed = {"x": w["x"], "emb2": w["L0_tok_emb_2"], "emb3": w["L0_tok_emb_3"], "emb4": w["L0_tok_emb_4"],
            "ident": np.eye(128, dtype=f32)}
    wqk = np.zeros((2, 64, 2, 4, 2, 2, 32), f32)
    for k, name in enumerate(("Wq", "Wk")):
        wh = w["L0_attn_" + name].reshape(64, 4, 2, 32)
        for j in range(2):
            wqk[j, :, k, :, :, j, :] = wh
    feed["attn_wqk"] = wqk.reshape(128, 8, 128)
    feed["attn_gb"] = np.tile(np.stack([w["L0_attn_gamma"], w["L0_attn_beta"]], 1), (2, 1))
    wvg = np.zeros((2, 64, 2, 512), f32)
    for j in range(2):
        wvg[j, :, j] = np.concatenate([w["L0_attn_Wv"], w["L0_attn_Wg"]], 1)
    feed["attn_wvg"] = wvg.reshape(128, 2, 512)
    feed["attn_wo"] = w["L0_attn_Wo"].reshape(2, 128, 64).transpose(1, 0, 2)
    feed["attn_bg"] = w["L0_attn_bg"].reshape(1, 256)
    feed["attn_bo"] = w["L0_attn_bo"].reshape(1, 64)
    def heads(wt, kv):
        o = np.zeros((2, 64, 4, 32), f32)
        for h in range(4):
            rows = wt[(h // 2 if kv else h) * 16:][:16]
            o[0, :, h, :16] = rows.T
            o[1, :, h, :8], o[1, :, h, 8:16] = rows[8:].T, rows[:8].T
        return o.reshape(2, 64, 128)
    wq, wk = heads(w["L0_ffn_wq"], False), heads(w["L0_ffn_wk"], True)
    wv = np.repeat(w["L0_ffn_wv"].reshape(2, 16, 64), 2, axis=0).reshape(64, 64).T
    feed["ffn_wqkv"] = np.concatenate([wq[0], wq[1], wk[0], wk[1], wv], 1)
    feed["ffn_wo"] = w["L0_ffn_wo"].T
    feed["ffn_ln1"] = w["L0_ffn_ln1_w"].reshape(64, 1)
    feed["ffn_ln2"] = np.tile(w["L0_ffn_ln2_w"].reshape(64, 1), (2, 1))
    freq = 1.0 / 10000.0 ** (np.arange(0, 16, 2, dtype=f32) / 16)
    ang = np.outer(np.arange(256, dtype=f32), freq).astype(f32)
    rope = np.zeros((4, 32, 2, 256), f32)
    rope[:, :8, 0] = rope[:, 8:16, 0] = np.cos(ang).T
    rope[:, :8, 1], rope[:, 8:16, 1] = -np.sin(ang).T, np.sin(ang).T
    feed["rope"] = rope.reshape(128, 2, 256)
    feed["causal"] = np.where(np.tril(np.ones((128, 128), bool)), 0.0, NEG).astype(f32)
    feed["moe0_w1"] = np.tile(w["L0_ffn_w1"].reshape(1360, 64).T, (2, 1))
    feed["moe0_w3"] = np.tile(w["L0_ffn_w3"].reshape(1360, 64).T, (2, 1))
    w2 = np.zeros((11 * 128, 64), f32)
    w2[:1360] = w["L0_ffn_w2"].transpose(0, 2, 1).reshape(1360, 64)
    feed["moe0_w2"] = w2.reshape(11, 128, 64).transpose(1, 0, 2)
    feed["moe0_wr"] = w["L0_ffn_router_w"].T
    feed["moe0_spread"] = np.tile(np.repeat(np.eye(8, dtype=f32), 170, axis=1), (3, 1))
    feed["mb_win"], feed["mb_wx"] = w["L1_attn_W_in"], w["L1_attn_W_x"]
    feed["mb_wdt"], feed["mb_wout"] = w["L1_attn_W_dt"], w["L1_attn_W_out"]
    feed["mb_chan"] = np.concatenate([w["L1_attn_conv_k"].T, np.stack([w["L1_attn_conv_b"], w["L1_attn_b_dt"], w["L1_attn_D_param"]], 1)], 1)
    feed["mb_alog"] = w["L1_attn_A_log"]
    feed["before"] = np.triu(np.ones((64, 64), f32), 1)
    feed["moe1_wr"] = np.concatenate([w["L1_ffn_Wr"], w["L1_ffn_br"][None]], 0)
    feed["moe1_w1"] = np.concatenate([w["L1_ffn_W1"], w["L1_ffn_b1"][:, None]], 1)
    feed["moe1_w2"], feed["moe1_b2"] = w["L1_ffn_W2"], w["L1_ffn_b2"]
    feed["prior"] = np.triu(np.ones((128, 128), f32), 1)

    nc = _bacc.Bacc("TRN2", target_bir_lowering=False, num_devices=1)
    arrays, aps = {}, {}
    for name, v in feed.items():
        v = np.ascontiguousarray(v)
        arrays["in_" + name] = v
        aps[name] = nc.dram_tensor("in_" + name, v.shape, mybir.dt.from_np(v.dtype), kind="ExternalInput").ap()
    out = nc.dram_tensor("out_0", (SEQ, LEN, D), F32, kind="ExternalOutput").ap()
    build(nc, aps, out)
    r = _run(nc, [arrays], core_ids=[0])
    return r.results[0]["out_0"]
```

```python
import math
from contextlib import ExitStack

import concourse.bass as bass
from concourse import mybir

F32 = mybir.dt.float32
BF16 = mybir.dt.bfloat16
I32 = mybir.dt.int32
U32 = mybir.dt.uint32
ALU = mybir.AluOpType
ACT = mybir.ActivationFunctionType
AX_X = mybir.AxisListType.X

P = 128
SEQ, LEN, D = 64, 256, 64
TILES = SEQ * LEN // P
VOCAB, PRIME = 125000, 31
LN_EPS, RMS_EPS = 1e-5, 1e-6


class Kit:

    def __init__(self, nc, ctx):
        self.nc, self.ctx = nc, ctx
        self.held = ctx.enter_context(nc.semaphore("held"))
        self.indirect = {stage: [ctx.enter_context(nc.semaphore(f"{stage}{b}")) for b in range(2)]
                         for stage in ("picked", "scattered", "fetched")}
        self.used = []

    def sb(self, ctx, name, shape, dt=F32):
        return ctx.enter_context(self.nc.sbuf_tensor(name, shape, dt))

    def ps(self, ctx, name, shape, dt=F32):
        return ctx.enter_context(self.nc.psum_tensor(name, shape, dt))

    def sem(self, ctx, name):
        handle = ctx.enter_context(self.nc.semaphore(name))
        self.used.append(handle)
        return handle

    def block(self, ctx, last=False):
        if not last:
            ctx.callback(self.clear)
        return ctx.enter_context(self.nc.Block())

    def clear(self):
        done, self.used = self.used, []
        with self.nc.Block() as block:
            @block.sync
            def _(sp):
                for handle in done[0::5]:
                    sp.sem_clear(handle)

            @block.gpsimd
            def _(pool):
                for handle in done[1::5]:
                    pool.sem_clear(handle)

            @block.scalar
            def _(act):
                for handle in done[2::5]:
                    act.sem_clear(handle)

            @block.vector
            def _(dve):
                for handle in done[3::5]:
                    dve.sem_clear(handle)

            @block.tensor
            def _(pe):
                for handle in done[4::5]:
                    pe.sem_clear(handle)

    def hold(self, eng, sem, value):
        eng.wait_ge(sem, value)
        eng.sem_inc(self.held, 1)


def bcast(ap, n):
    return ap.unsqueeze(2).to_broadcast([ap.shape[0], ap.shape[1], n])


def embed_and_logits(nc, kit, a, H, YT, LOGITS):
    G = 8
    STEPS = TILES // G
    with ExitStack() as c:
        sb = lambda n, s, d=F32: kit.sb(c, n, s, d)
        sem = lambda n: kit.sem(c, n)
        tok_i = sb("tok_i", [P, 4 + LEN], I32)
        tok = sb("tok", [P, 4 + LEN])
        hs = sb("hs", [P, 3, TILES])
        quo = sb("quo", [P, 3, TILES])
        quo_i = sb("quo_i", [P, 3, TILES], I32)
        rows = sb("rows", [P, 3, TILES], U32)
        rows_now = sb("rows_now", [P, 2, 3, G], U32)
        gath = sb("gath", [P, 2, 3, G, D])
        h_now = sb("h_now", [P, G, D])
        cen = sb("cen", [P, G, D])
        sq = sb("sq", [P, G, D])
        ys = sb("ys", [P, G, D])
        st = sb("st", [P, 4, G])
        eps2 = sb("eps2", [P, 1])
        ident = sb("ident1", [P, P])
        wqk = sb("wqk", [P, 8, P])
        gb = sb("gb", [P, 2])
        yt = sb("yt_now", [P, 4, P])
        qk = sb("qk", [P, 2, 2, 4 * P])
        zer = sb("zer", [P, 256])
        ps_t = kit.ps(c, "ps_t", [P, 4, P])
        ps_qk = kit.ps(c, "ps_qk", [P, 2, 2, 4 * P])
        ps_att = kit.ps(c, "ps_att", [P, 4, SEQ])
        tok_in, w_in, rows_ready, cleared = sem("tok_in"), sem("w_in"), sem("rows_ready"), sem("cleared")
        picked = kit.indirect["picked"]
        gath_free, ssum, root, ys_ready, t_done = sem("gath_free"), sem("ssum"), sem("root"), sem("ys_ready"), sem("t_done")
        yt_ready, proj, q_out, k_out, att_done = sem("yt_ready"), sem("proj"), sem("q_out"), sem("k_out"), sem("att_done")
        zero_ready = sem("zero_ready")
        block = kit.block(c)

        @block.sync
        def _(sp):
            sp.wait_ge(zero_ready, 1)
            sp.dma_start(tok_i[0:64, 4:260], a["x"]).then_inc(tok_in, 16)
            sp.dma_start(tok_i[64:128, 3:259], a["x"]).then_inc(tok_in, 16)
            sp.dma_start(ident[:], a["ident"]).then_inc(w_in, 16)
            sp.dma_start(wqk[:], a["attn_wqk"]).then_inc(w_in, 16)
            sp.dma_start(gb[:], a["attn_gb"]).then_inc(w_in, 16)

        @block.gpsimd
        def _(pool):
            pool.wait_ge(rows_ready, 1)
            pool.wait_ge(cleared, 2)
            with pool.Fori(0, STEPS // 2) as i:
                for b in range(2):
                    step = i * 2 + b
                    kit.hold(pool, gath_free, step + 1)
                    pool.tensor_copy(rows_now[:, b], rows[:, :, bass.ds(step * G, G)])
                    pool.drain()
                    for t in range(G):
                        for n in range(3):
                            pool.indirect_dma_start(
                                gath[:, b, n, t, :], None, a[f"emb{n + 2}"],
                                bass.IndirectOffsetOnAxis(ap=rows_now[:, b, n, t:t + 1], axis=0),
                                bounds_check=VOCAB - 1, oob_is_err=False).then_inc(picked[b], 16)

        @block.vector
        def _(dve):
            dve.memset(tok_i[:], 0).then_inc(zero_ready, 1)
            dve.memset(gath[:, 0], 0.0).then_inc(cleared, 1)
            dve.memset(gath[:, 1], 0.0).then_inc(cleared, 1)
            dve.memset(zer[:], 0.0).then_inc(cleared, 1)
            dve.memset(eps2[:], LN_EPS * LN_EPS).then_inc(cleared, 1)
            dve.sem_inc(gath_free, 2)
            dve.wait_ge(tok_in, 32)
            dve.tensor_copy(tok[:], tok_i[:])
            dve.drain()

            def back(k):
                o = 4 - k
                return tok[:, o:o + 2 * TILES - 1:2] if o + 2 * TILES - 1 <= 260 else tok[:, o:260:2]
            dve.scalar_tensor_tensor(hs[:, 0], back(1), float(PRIME), back(0), ALU.mult, ALU.add)
            dve.drain()
            dve.scalar_tensor_tensor(hs[:, 1], back(2), float(PRIME ** 2 % VOCAB), hs[:, 0], ALU.mult, ALU.add)
            dve.drain()
            dve.scalar_tensor_tensor(hs[:, 2], back(3), float(PRIME ** 3 % VOCAB), hs[:, 1], ALU.mult, ALU.add)
            dve.drain()
            dve.tensor_scalar(quo[:], hs[:], 1.0 / VOCAB, None, ALU.mult)
            dve.drain()
            dve.tensor_copy(quo_i[:], quo[:])
            dve.drain()
            dve.tensor_copy(quo[:], quo_i[:])
            dve.drain()
            dve.scalar_tensor_tensor(hs[:], quo[:], -float(VOCAB), hs[:], ALU.mult, ALU.add)
            dve.drain()
            for cmp, shift in ((ALU.is_lt, float(VOCAB)), (ALU.is_ge, -float(VOCAB))):
                edge = 0.0 if cmp == ALU.is_lt else float(VOCAB)
                dve.tensor_scalar(quo[:], hs[:], edge, shift, cmp, ALU.mult)
                dve.drain()
                dve.tensor_tensor(hs[:], hs[:], quo[:], ALU.add)
                dve.drain()
            dve.memset(hs[0:64, 0, 0:1], 2.0 ** 20)
            dve.memset(hs[:, 1:3, 0:1], 2.0 ** 20)
            dve.memset(hs[0:64, 2, 1:2], 2.0 ** 20)
            dve.drain()
            dve.tensor_copy(rows[:], hs[:]).then_inc(rows_ready, 1)
            with dve.Fori(0, STEPS // 2) as i:
                for b in range(2):
                    step = i * 2 + b
                    kit.hold(dve, picked[b], 16 * 3 * G * i + 16 * 3 * G)
                    dve.tensor_tensor(sq[:], gath[:, b, 0], gath[:, b, 1], ALU.add)
                    dve.drain()
                    dve.tensor_tensor(cen[:], sq[:], gath[:, b, 2], ALU.add).then_inc(gath_free, 1)
                    dve.drain()
                    dve.tensor_scalar(h_now[:], cen[:], 0.25, None, ALU.mult)
                    dve.drain()
                    dve.tensor_copy(H[:, bass.ds(step * G, G), :], h_now[:])
                    dve.tensor_reduce(st[:, 0], h_now[:], AX_X, ALU.add)
                    dve.drain()
                    dve.tensor_scalar(st[:, 1], st[:, 0], 1.0 / D, None, ALU.mult)
                    dve.drain()
                    dve.tensor_tensor(cen[:], h_now[:], bcast(st[:, 1], D), ALU.subtract)
                    dve.drain()
                    dve.tensor_tensor(sq[:], cen[:], cen[:], ALU.mult)
                    dve.drain()
                    dve.tensor_reduce(st[:, 2], sq[:], AX_X, ALU.add).then_inc(ssum, 1)
                    dve.wait_ge(root, step + 1)
                    dve.reciprocal(st[:, 3], st[:, 1])
                    dve.drain()
                    dve.tensor_tensor(ys[:], cen[:], bcast(st[:, 3], D), ALU.mult).then_inc(ys_ready, 1)
                    for p in range(4):
                        kit.hold(dve, proj, step * 4 + p + 1)
                        dve.tensor_copy(qk[:, p % 2, 1, :], ps_qk[:, p % 2, 1, :]).then_inc(k_out, 1)
            dve.wait_ge(att_done, 1)
            dve.tensor_copy(LOGITS[:], ps_att[:])

        @block.scalar
        def _(act):
            act.wait_ge(w_in, 48)
            act.wait_ge(cleared, 4)
            with act.Fori(0, STEPS) as i:
                kit.hold(act, ssum, i + 1)
                act.activation(st[:, 1], st[:, 2], ACT.Sqrt, bias=eps2[:], scale=(1 + LN_EPS) / D).then_inc(root, 1)
                kit.hold(act, t_done, i + 1)
                act.activation(yt[:], ps_t[:], ACT.Identity, bias=gb[:, 1:2], scale=gb[:, 0:1]).then_inc(yt_ready, 1)
                act.activation(YT[:, bass.ds(i * 4, 4), :], ps_t[:], ACT.Identity, bias=gb[:, 1:2], scale=gb[:, 0:1]).then_inc(yt_ready, 1)
                for p in range(4):
                    kit.hold(act, proj, i * 4 + p + 1)
                    act.activation(qk[:, p % 2, 0, :], ps_qk[:, p % 2, 0, :], ACT.Copy).then_inc(q_out, 1)

        @block.tensor
        def _(pe):
            pe.wait_ge(w_in, 48)
            pe.wait_ge(cleared, 4)
            pe.matmul(ps_att[:].rearrange("p a t -> p (a t)"), zer[:, 0:P], zer[:], start=True, stop=False, skip_group_check=True)

            def project(p, b):
                pe.matmul(ps_qk[:, b, 0, :], wqk[:, p, :], yt[:].rearrange("p a t -> p (a t)"), start=True, stop=True)
                pe.matmul(ps_qk[:, b, 1, :], wqk[:, 4 + p, :], yt[:].rearrange("p a t -> p (a t)"), start=True, stop=True).then_inc(proj, 1)

            def logits(p, i):
                kit.hold(pe, q_out, i * 4 + p + 1)
                kit.hold(pe, k_out, i * 4 + p + 1)
                for h in range(2):
                    r = slice(64 * h, 64 * h + 64)
                    for s in range(8):
                        mm = pe.matmul(ps_att[r, p, :], qk[r, p % 2, 0, 64 * s:64 * s + 64], qk[r, p % 2, 1, 64 * s:64 * s + 64],
                                       start=False, stop=False, skip_group_check=True)
                return mm

            with pe.Fori(0, STEPS) as i:
                kit.hold(pe, ys_ready, i + 1)
                for t in range(4):
                    tr = pe.transpose(ps_t[:, t, :], ys[:, 2 * t:2 * t + 2, :].rearrange("p a d -> p (a d)"), ident[:])
                tr.then_inc(t_done, 1)
                kit.hold(pe, yt_ready, 2 * i + 2)
                project(0, 0)
                project(1, 1)
                logits(0, i)
                project(2, 0)
                logits(1, i)
                project(3, 1)
                logits(2, i)
                logits(3, i)
            pe.matmul(ps_att[:].rearrange("p a t -> p (a t)"), zer[:, 0:P], zer[:], start=False, stop=True,
                      skip_group_check=True).then_inc(att_done, 1)


def row_softmax(nc, kit, a, LOGITS, MIX):
    scale = 1.0 / (32 ** 0.5) / (LEN ** 0.5)
    with ExitStack() as c:
        sb = lambda n, s, d=F32: kit.sb(c, n, s, d)
        sem = lambda n: kit.sem(c, n)
        ident = sb("ident2", [P, P])
        prob = sb("prob", [P, 4, SEQ])
        twice = sb("twice", [P, 4, 2, SEQ])
        st = sb("st2", [P, 3, 4])
        ps_t = kit.ps(c, "ps_t2", [P, 4, P])
        w_in, lmax, expd, twice_ready, t_done = sem("w_in2"), sem("lmax"), sem("expd"), sem("twice_ready"), sem("t_done2")
        block = kit.block(c)

        @block.sync
        def _(sp):
            sp.dma_start(ident[:], a["ident"]).then_inc(w_in, 16)

        @block.vector
        def _(dve):
            dve.memset(MIX[:], 0.0)
            dve.tensor_reduce(st[:, 0], LOGITS[:], AX_X, ALU.max)
            dve.drain()
            dve.tensor_tensor(prob[:], LOGITS[:], bcast(st[:, 0], SEQ), ALU.subtract).then_inc(lmax, 1)
            dve.wait_ge(expd, 1)
            dve.tensor_reduce(st[:, 1], prob[:], AX_X, ALU.add)
            dve.drain()
            dve.reciprocal(st[:, 2], st[:, 1])
            dve.drain()
            for k in range(2):
                w = dve.tensor_tensor(twice[:, :, k, :], prob[:], bcast(st[:, 2], SEQ), ALU.mult)
            w.then_inc(twice_ready, 1)
            dve.wait_ge(t_done, 1)
            for k in range(2):
                r = slice(64 * k, 64 * k + 64)
                dve.tensor_copy(MIX[r, :, r].rearrange("t (p h) s -> t p h s", h=2), ps_t[r, :, :].rearrange("t p (h s) -> t p h s", h=2))

        @block.scalar
        def _(act):
            act.wait_ge(lmax, 1)
            act.activation(prob[:], prob[:], ACT.Exp, scale=scale).then_inc(expd, 1)

        @block.tensor
        def _(pe):
            pe.wait_ge(w_in, 16)
            pe.wait_ge(twice_ready, 1)
            for p in range(4):
                tr = pe.transpose(ps_t[:, p, :], twice[:, p, :, :].rearrange("p k s -> p (k s)"), ident[:])
            tr.then_inc(t_done, 1)


def row_attention_out(nc, kit, a, H, YT, MIX, h1):
    N = TILES // 2
    with ExitStack() as c:
        sb = lambda n, s, d=F32: kit.sb(c, n, s, d)
        sem = lambda n: kit.sem(c, n)
        ident = sb("ident3", [P, P])
        wvg = sb("wvg", [P, 2, 512])
        wo = sb("wo", [P, 2, D])
        bg = sb("bg", [P, 256])
        bo = sb("bo", [P, D])
        yt = sb("yt3", [P, 2, P])
        v = sb("v", [P, 2, 2, 256])
        gz = sb("gz", [P, 2, 2, 256])
        og = sb("og", [P, 2, 2, 256])
        ogt = sb("ogt", [P, 2, 2, 2, P])
        res = sb("res3", [P, 4, D])
        ps_vg = kit.ps(c, "ps_vg", [P, 2, 2, 2, 256])
        ps_o = kit.ps(c, "ps_o", [P, 2, 8, 2, 32])
        ps_t = kit.ps(c, "ps_t3", [P, 2, 2, P])
        ps_h = kit.ps(c, "ps_h", [P, 4, D])
        w_in, yt_ready, vg_done, v_out, gz_out, sig = (sem(n) for n in ("w_in3", "yt_ready3", "vg_done", "v_out", "gz_out", "sig"))
        o_done, og_out, t_done, ogt_out, h_done, h_out, stored = (sem(n) for n in ("o_done", "og_out", "t_done3", "ogt_out", "h_done", "h_out", "stored3"))
        block = kit.block(c)

        @block.sync
        def _(sp):
            for dst, src in ((ident[:], a["ident"]), (wvg[:], a["attn_wvg"]), (wo[:], a["attn_wo"]),
                             (bg[:], a["attn_bg"].to_broadcast([P, 256])), (bo[:], a["attn_bo"].to_broadcast([P, D]))):
                sp.dma_start(dst, src).then_inc(w_in, 16)
            with sp.Fori(0, N // 2) as i:
                kit.hold(sp, h_out, i * 2 + 2)
                for l2 in range(2):
                    sp.dma_start(h1.rearrange("s (lp l2) d -> l2 s lp d", l2=2)[l2][:, bass.ds(i * 4, 4), :],
                                 H[64 * l2:64 * l2 + 64, bass.ds(i * 4, 4), :]).then_inc(stored, 16)
            sp.wait_ge(stored, 16 * N)

        @block.gpsimd
        def _(pool):
            with pool.Fori(0, N // 2) as i:
                for b in range(2):
                    kit.hold(pool, vg_done, i * 2 + b + 1)
                    pool.tensor_copy(yt[:, b, :], YT[:, bass.ds(i * 2 + b, 1), :].rearrange("p a t -> p (a t)")).then_inc(yt_ready, 1)

        @block.scalar
        def _(act):
            def values(i, b):
                kit.hold(act, vg_done, i * 2 + b + 3)
                act.activation(v[:, b], ps_vg[:, b, 0], ACT.Copy).then_inc(v_out, 1)

            def gates(i, b):
                kit.hold(act, gz_out, i * 2 + b + 1)
                act.activation(gz[:, b], gz[:, b], ACT.Sigmoid).then_inc(sig, 1)

            def turned(i, b):
                kit.hold(act, t_done, i * 2 + b + 1)
                act.activation(ogt[:, b].rearrange("p l k t -> p (l k t)"), ps_t[:].rearrange("p l k t -> p (l k t)"), ACT.Copy).then_inc(ogt_out, 1)

            values(0, 0)
            gates(0, 0)
            values(0, 1)
            with act.Fori(0, N // 2 - 1) as i:
                gates(i, 1)
                values(i + 1, 0)
                gates(i + 1, 0)
                values(i + 1, 1)
                turned(i, 0)
                turned(i, 1)
            gates(N // 2 - 1, 1)
            turned(N // 2 - 1, 0)
            turned(N // 2 - 1, 1)

        @block.vector
        def _(dve):
            dve.sem_inc(vg_done, 2)
            dve.wait_ge(w_in, 80)

            def gates(i, b):
                kit.hold(dve, vg_done, i * 2 + b + 3)
                dve.tensor_tensor(gz[:, b], ps_vg[:, b, 1], bg[:].unsqueeze(1).to_broadcast([P, 2, 256]), ALU.add).then_inc(gz_out, 1)

            def gated(i, b):
                kit.hold(dve, sig, i * 2 + b + 1)
                kit.hold(dve, o_done, i * 2 + b + 1)
                dve.tensor_tensor(og[:, b].rearrange("p l (h c) -> p h l c", h=8), ps_o[:, b], gz[:, b].rearrange("p l (h c) -> p h l c", h=8), ALU.mult).then_inc(og_out, 1)
                dve.drain()

            def residual(i):
                kit.hold(dve, h_done, i * 2 + 2)
                dve.tensor_tensor(res[:], ps_h[:], bo[:].unsqueeze(1).to_broadcast([P, 4, D]), ALU.add)
                dve.drain()
                hh = H[:, bass.ds(i * 4, 4), :]
                dve.tensor_tensor(hh, hh, res[:], ALU.add).then_inc(h_out, 2)

            gates(0, 0)
            gates(0, 1)
            with dve.Fori(0, N // 2 - 1) as i:
                for b in range(2):
                    gated(i, b)
                    gates(i + 1, b)
                residual(i)
            gated(N // 2 - 1, 0)
            gated(N // 2 - 1, 1)
            residual(N // 2 - 1)

        @block.tensor
        def _(pe):
            pe.wait_ge(w_in, 80)

            def project(i, b):
                kit.hold(pe, yt_ready, i * 2 + b + 1)
                for j in range(2):
                    for k in range(2):
                        mm = pe.matmul(ps_vg[:, b, k, j, :], yt[:, b, :], wvg[:, j, 256 * k:256 * k + 256], start=True, stop=True)
                mm.then_inc(vg_done, 1)

            def attend(i, b):
                kit.hold(pe, v_out, i * 2 + b + 1)
                for h in range(8):
                    mm = pe.matmul(ps_o[:, b, h], MIX[:, h, :], v[:, b, :, 32 * h:32 * h + 32], start=True, stop=True)
                mm.then_inc(o_done, 1)

            def turn(i, b):
                kit.hold(pe, og_out, i * 2 + b + 1)
                if b == 1:
                    kit.hold(pe, ogt_out, i * 2 + 1)
                for l in range(2):
                    for k in range(2):
                        mm = pe.transpose(ps_t[:, l, k, :], og[:, b, l, 128 * k:128 * k + 128], ident[:])
                mm.then_inc(t_done, 1)

            def out_rows(i, b):
                kit.hold(pe, ogt_out, i * 2 + b + 1)
                for l in range(2):
                    for k in range(2):
                        mm = pe.matmul(ps_h[:, 2 * b + l, :], ogt[:, b, l, k, :], wo[:, k, :], start=(k == 0), stop=(k == 1))
                mm.then_inc(h_done, 1)

            project(0, 0)
            project(0, 1)
            with pe.Fori(0, N // 2 - 1) as i:
                for b in range(2):
                    attend(i, b)
                    kit.hold(pe, gz_out, i * 2 + b + 1)
                    project(i + 1, b)
                turn(i, 0)
                turn(i, 1)
                out_rows(i, 0)
                out_rows(i, 1)
            last = N // 2 - 1
            attend(last, 0)
            attend(last, 1)
            turn(last, 0)
            turn(last, 1)
            out_rows(last, 0)
            out_rows(last, 1)


NEG = -1e30


def norm_statistics(dve, src, cen, sq, st):
    dve.tensor_reduce(st[:, 0], src, AX_X, ALU.add)
    dve.drain()
    dve.tensor_scalar(st[:, 1], st[:, 0], 1.0 / D, None, ALU.mult)
    dve.drain()
    dve.tensor_tensor(cen, src, bcast(st[:, 1], D), ALU.subtract)
    dve.drain()
    dve.tensor_tensor(sq, cen, cen, ALU.mult)
    dve.drain()
    dve.tensor_reduce(st[:, 2], sq, AX_X, ALU.add)
    dve.drain()


def causal_attention(nc, kit, a, h1, H, X2):
    with ExitStack() as c:
        sb = lambda n, s, d=F32: kit.sb(c, n, s, d)
        sem = lambda n: kit.sem(c, n)
        ident = sb("ident4", [P, P])
        identb = sb("identb4", [P, P], BF16)
        maskf = sb("maskf", [P, P])
        mask = sb("mask", [P, P], BF16)
        wqkv = sb("wqkv", [64, 4 * P + D])
        wo = sb("wo4", [64, D])
        ln1 = sb("ln1", [64, 1])
        rope = sb("rope", [P, 2, LEN])
        cen = sb("cen4", [P, 2, D])
        sq = sb("sq4", [P, 2, D])
        u = sb("u4", [P, 2, D])
        st = sb("st4", [P, 3, 2])
        var = sb("var4", [P, 2, 2])
        half = sb("half4", [P, 2, 2])
        rs = sb("rs4", [P, 2, 2])
        ht = sb("ht", [64, LEN])
        q = sb("q4", [P, LEN])
        k = sb("k4", [P, LEN])
        t1 = sb("t14", [P, LEN])
        t2 = sb("t24", [P, LEN])
        v = sb("v4", [P, 2, 2, 4 * 80])
        mx = sb("mx4", [P, 2, 4])
        nm = sb("nm4", [P, 2, 4])
        sums = sb("sums4", [P, 2, 2, 4])
        rsum = sb("rsum4", [P, 2, 4])
        E = sb("E4", [P, 2, 4, 3 * P])
        ET = sb("ET4", [P, 3, 4, P])
        rwide = sb("rwide4", [P, 2, D])
        rwt = sb("rwt4", [D, LEN])
        yt = sb("yt4", [64, LEN])
        ps_s = kit.ps(c, "ps_s", [P, 4, 512])
        ps_t = kit.ps(c, "ps_t4", [P, 2, 4, P])
        ps_a = kit.ps(c, "ps_a4", [P, 512])
        ps_b = kit.ps(c, "ps_b4", [P, 512])
        names = ("w_in rows_in var_ready u_ready ht_done ht_out proj q_out k_out v_done v_out scores nm_ready "
                 "exps t_done t_outa t_outd y_done rw_ready rwt_done rwt_out zeroed yt_out o_done o_out mask_ready").split()
        s = {n: sem(n + "_4") for n in names}
        block = kit.block(c)
        SCALE = 16 ** -0.5

        def steps(eng, step):
            step(-2, 0, tail=False, middle=False)
            step(-1, 1, tail=False)
            with eng.Fori(0, SEQ // 2 - 1) as i:
                step(i * 2, 0)
                step(i * 2 + 1, 1)
            step(SEQ - 2, 0, head=False)
            step(SEQ - 1, 1, head=False, middle=False)

        @block.sync
        def _(sp):
            for dst, src in ((ident[:], a["ident"]), (maskf[:], a["causal"]), (wqkv[:], a["ffn_wqkv"]), (wo[:], a["ffn_wo"]),
                             (ln1[:], a["ffn_ln1"]), (rope[:], a["rope"])):
                sp.dma_start(dst, src).then_inc(s["w_in"], 16)
            with sp.Fori(0, SEQ) as n:
                kit.hold(sp, s["rows_in"], n * 16 + 16)
                sp.dma_start(H[:, bass.ds(n * 2, 2), :], h1.rearrange("s (two p) d -> p (s two) d", p=P)[:, bass.ds(n * 2, 2), :]).then_inc(s["rows_in"], 16)
            sp.wait_ge(s["rows_in"], 16 * SEQ + 16)

        @block.gpsimd
        def _(pool):
            pool.memset(half[:], -0.5)
            pool.drain()

            def step(b, par, tail=True, middle=True, head=True):
                if head:
                    n = b + 2
                    kit.hold(pool, s["var_ready"], n + 1)
                    pool.tensor_tensor(rs[:], var[:], half[:], ALU.pow)
                    pool.drain()
                    pool.tensor_tensor(X2[:, bass.ds(n * 2, 2), :], cen[:], bcast(rs[:, 0], D), ALU.mult)
                    pool.tensor_tensor(u[:], cen[:], bcast(rs[:, 1], D), ALU.mult).then_inc(s["u_ready"], 1)

            steps(pool, step)

        @block.vector
        def _(dve):
            dve.sem_inc(s["rows_in"], 16)
            dve.wait_ge(s["w_in"], 96)
            dve.tensor_copy(identb[:], ident[:])
            dve.tensor_copy(mask[:], maskf[:]).then_inc(s["mask_ready"], 1)

            dve.memset(v[:], 0.0).then_inc(s["zeroed"], 1)
            dve.sem_inc(s["v_out"], 1)
            dve.sem_inc(s["exps"], 1)

            def rotate(dst, out, count):
                kit.hold(dve, s["proj"], count)
                dve.tensor_tensor(t1[:], ps_a[:, 0:LEN], rope[:, 0], ALU.mult)
                dve.tensor_tensor(t2[:], ps_a[:, LEN:2 * LEN], rope[:, 1], ALU.mult)
                dve.drain()
                dve.tensor_tensor(dst[:], t1[:], t2[:], ALU.add).then_inc(out, 1)

            def step(b, par, tail=True, middle=True, head=True):
                n = b + 2
                if tail:
                    kit.hold(dve, s["exps"], b + 2)
                    dve.reciprocal(rsum[:], sums[:, par])
                    dve.drain()
                    dve.tensor_copy(rwide[:].rearrange("p t (h c) -> p t h c", h=4),
                                    rsum[:].unsqueeze(3).to_broadcast([P, 2, 4, 16])).then_inc(s["rw_ready"], 1)
                if head:
                    kit.hold(dve, s["rows_in"], n * 16 + 32)
                    norm_statistics(dve, H[:, bass.ds(n * 2, 2), :], cen[:], sq[:], st)
                    dve.tensor_scalar(var[:, 0], st[:, 2], 1.0 / D, LN_EPS, ALU.mult, ALU.add)
                    dve.tensor_scalar(var[:, 1], st[:, 2], (1 + RMS_EPS) / D, RMS_EPS * LN_EPS, ALU.mult, ALU.add).then_inc(s["var_ready"], 1)
                if tail:
                    kit.hold(dve, s["t_done"], b * 3 + 2)
                    dve.tensor_copy(ET[:, 1], ps_t[:, 1]).then_inc(s["t_outd"], 1)
                if middle:
                    kit.hold(dve, s["scores"], b + 2)
                    dve.tensor_reduce(mx[:, 0], ps_s[:, :, 0:P], AX_X, ALU.max)
                    dve.tensor_reduce(mx[:, 1], ps_s[:, :, LEN:2 * LEN], AX_X, ALU.max)
                    dve.drain()
                    dve.tensor_scalar(nm[:], mx[:], -SCALE, None, ALU.mult).then_inc(s["nm_ready"], 1)
                if head:
                    rotate(q, s["q_out"], n * 2 + 1)
                if tail:
                    kit.hold(dve, s["y_done"], b + 1)
                    kit.hold(dve, s["rwt_out"], b + 1)
                    dve.tensor_tensor(yt[:], ps_b[0:64, 0:LEN], rwt[:], ALU.mult).then_inc(s["yt_out"], 1)
                if head:
                    rotate(k, s["k_out"], n * 2 + 2)
                if tail:
                    kit.hold(dve, s["o_done"], b + 1)
                    xx = X2[:, bass.ds(b * 2, 2), :]
                    dve.tensor_tensor(xx, xx, ps_b[:, 384:512].rearrange("p (t d) -> p t d", t=2), ALU.add).then_inc(s["o_out"], 1)

            steps(dve, step)

        @block.scalar
        def _(act):
            act.wait_ge(s["w_in"], 96)
            act.wait_ge(s["zeroed"], 1)

            def step(b, par, tail=True, middle=True, head=True):
                n = b + 2
                if tail:
                    kit.hold(act, s["t_done"], b * 3 + 1)
                    act.activation(ET[:, 0], ps_t[:, 0], ACT.Copy).then_inc(s["t_outa"], 1)
                if middle:
                    kit.hold(act, s["v_done"], b + 2)
                    act.activation(v[:, 1 - par].rearrange("p t (h w) -> p t h w", h=4)[:, :, :, 0:16],
                                   ps_a[:, 0:2 * D].rearrange("p (t h c) -> p t h c", t=2, h=4), ACT.Copy).then_inc(s["v_out"], 1)
                if tail:
                    kit.hold(act, s["rwt_done"], b + 1)
                    act.activation(rwt[:], ps_b[0:64, LEN:2 * LEN], ACT.Copy).then_inc(s["rwt_out"], 1)
                if head:
                    kit.hold(act, s["ht_done"], n + 1)
                    act.activation(ht[:], ps_a[0:64, 0:LEN], ACT.Copy, scale=ln1[:]).then_inc(s["ht_out"], 1)
                if tail:
                    kit.hold(act, s["t_done"], b * 3 + 3)
                    act.activation(ET[:, 2], ps_t[:, 0], ACT.Copy).then_inc(s["t_outa"], 1)
                if middle:
                    kit.hold(act, s["nm_ready"], b + 2)
                    other = 1 - par
                    for h in range(4):
                        act.activation(E[:, other, h, 0:P], ps_s[:, h, 0:P], ACT.Exp, bias=nm[:, 0, h:h + 1], scale=SCALE,
                                       accum_out=sums[:, other, 0, h:h + 1])
                        e = act.activation(E[:, other, h, P:3 * P], ps_s[:, h, LEN:2 * LEN], ACT.Exp, bias=nm[:, 1, h:h + 1], scale=SCALE,
                                           accum_out=sums[:, other, 1, h:h + 1])
                    e.then_inc(s["exps"], 1)

            steps(act, step)

        @block.tensor
        def _(pe):
            pe.wait_ge(s["w_in"], 96)
            pe.wait_ge(s["mask_ready"], 1)

            skip = dict(skip_group_check=True)

            def scores(n):
                kit.hold(pe, s["k_out"], n + 1)
                kit.hold(pe, s["exps"], n + 1)
                for h in range(4):
                    pe.matmul(ps_s[:, h, 0:P], identb[:], mask[:], start=True, stop=False, **skip)
                    pe.matmul(ps_s[:, h, 3 * P:4 * P], identb[:], mask[:], start=False, stop=False, **skip)
                for h in range(4):
                    r = slice(32 * h, 32 * h + 32)
                    pe.matmul(ps_s[:, h, 0:P], q[r, 0:P], k[r, 0:P], start=False, stop=False, tile_position=(32 * h, 0), **skip)
                    mm = pe.matmul(ps_s[:, h, LEN:2 * LEN], q[r, P:LEN], k[r, :], start=False, stop=True, tile_position=(32 * h, 0), **skip)
                mm.then_inc(s["scores"], 1)

            def project(which):
                for j in range(2):
                    mm = pe.matmul(ps_a[:, LEN * j:LEN * j + LEN], wqkv[:, P * (2 * which + j):P * (2 * which + j) + P], ht[:], start=True, stop=True)
                mm.then_inc(s["proj"], 1)

            def turn(par, g):
                for h in range(4):
                    mm = pe.transpose(ps_t[:, g % 2, h, :], E[:, par, h, P * g:P * g + P], ident[:])
                mm.then_inc(s["t_done"], 1)

            def values(n):
                kit.hold(pe, s["k_out"], n + 1)
                for t in range(2):
                    mm = pe.matmul(ps_a[:, D * t:D * t + D], ht[:, P * t:P * t + P], wqkv[:, 4 * P:4 * P + D], start=True, stop=True)
                mm.then_inc(s["v_done"], 1)

            def step(b, par, tail=True, middle=True, head=True):
                n = b + 2
                if tail:
                    kit.hold(pe, s["exps"], b + 2)
                    turn(par, 0)
                    turn(par, 1)
                if middle:
                    values(b + 1)
                if tail:
                    kit.hold(pe, s["rw_ready"], b + 1)
                    for t in range(2):
                        mm = pe.transpose(ps_b[0:64, LEN + P * t:LEN + P * t + P], rwide[:, t, :], ident[:])
                    mm.then_inc(s["rwt_done"], 1)
                if middle:
                    scores(b + 1)
                if head:
                    kit.hold(pe, s["v_out"], n + 1)
                    kit.hold(pe, s["u_ready"], n + 1)
                    for t in range(2):
                        mm = pe.transpose(ps_a[0:64, P * t:P * t + P], u[:, t, :], ident[:])
                    mm.then_inc(s["ht_done"], 1)
                if tail:
                    kit.hold(pe, s["t_outa"], b * 2 + 1)
                    turn(par, 2)
                if head:
                    kit.hold(pe, s["ht_out"], n + 1)
                    project(0)
                if tail:
                    kit.hold(pe, s["t_outa"], b * 2 + 2)
                    kit.hold(pe, s["t_outd"], b + 1)
                    kit.hold(pe, s["v_out"], b + 2)
                    kit.hold(pe, s["rwt_out"], b + 1)
                    for t, g, keys in ((0, 0, 0), (1, 1, 0), (1, 2, 1)):
                        for h in range(4):
                            mm = pe.matmul(ps_b[0:64, P * t:P * t + P], v[:, par, keys, 64 * h:64 * h + 64], ET[:, g, h, :],
                                           start=(g < 2 and h == 0), stop=(g != 1 and h == 3), **skip)
                    mm.then_inc(s["y_done"], 1)
                if head:
                    kit.hold(pe, s["q_out"], n + 1)
                    project(1)
                if tail:
                    kit.hold(pe, s["yt_out"], b + 1)
                    for t in range(2):
                        mm = pe.matmul(ps_b[:, 384 + 64 * t:448 + 64 * t], yt[:, P * t:P * t + P], wo[:], start=True, stop=True)
                    mm.then_inc(s["o_done"], 1)

            steps(pe, step)


def dense_experts(nc, kit, a, H, X2):
    NE, HID = 8, 170
    ROWS = NE * HID
    CH = -(-ROWS // P)
    T = 4
    BLOCKS = TILES // T
    W = T * P
    size = [min(P, ROWS - P * j) for j in range(CH)]
    with ExitStack() as c:
        sb = lambda n, s, d=F32: kit.sb(c, n, s, d)
        sem = lambda n: kit.sem(c, n)
        ident = sb("ident5", [P, P])
        identb = sb("identb5", [P, P], BF16)
        wide_w = sb("wide_w5", [P, ROWS])
        w_split = sb("w_split5", [P, 2, 3, ROWS], BF16)
        w2 = sb("w2_5", [P, CH, D])
        wr = sb("wr_5", [64, NE])
        ln2 = sb("ln2", [P, 1])
        spreadf = sb("spreadf", [24, ROWS])
        spread = sb("spread", [24, ROWS], BF16)
        iota = sb("iota5", [P, T, NE])
        iotai = sb("iotai5", [P, T, NE], I32)
        sq = sb("sq5", [P, T, D])
        st = sb("st5", [P, T])
        var = sb("var5", [P, T])
        half = sb("half5", [P, T])
        euler = sb("euler5", [P, T, NE])
        rs = sb("rs5", [P, T])
        fl = sb("fl5", [P, T, 2, D])
        flt = sb("flt", [P, W])
        xa = sb("xa5", [P, 2, W], BF16)
        xb = sb("xb5", [P, 2, W], BF16)
        lg = sb("lg5", [P, T, NE])
        pr = sb("pr5", [P, T, NE])
        m = sb("m5", [P, 4, T])
        top = sb("top5", [P, T, 8])
        topi = sb("topi5", [P, T, 8], U32)
        topf = sb("topf5", [P, T, 8])
        hot = sb("hot5", [P, 2, T, NE])
        wt = sb("wt5", [P, T, NE])
        rest = sb("rest5", [P, 2, T, NE])
        w3b = sb("w3b", [P, T, 3, NE], BF16)
        wtt = sb("wtt", [24, 2, W], BF16)
        gate = sb("gate5", [P, 2, W])
        up = sb("up5", [P, 2, W])
        hid = sb("hid5", [P, 2, W])
        acc = sb("acc5", [P, T, D])
        ps_u = kit.ps(c, "ps_u", [P, 2, 2, W])
        ps_w = kit.ps(c, "ps_w", [P, W])
        ps_d = kit.ps(c, "ps_d", [P, 512])
        ps_r = kit.ps(c, "ps_r", [P, W])
        ps_x = kit.ps(c, "ps_x", [P, 1024], BF16)
        names = ("w_in ready sq_ready var_ready fl_ready flt_done flt_out router lg_ready exp_done w_ready wtt_done wtt_out "
                 "ups split acc_ready x0_out half_ready wide gated hidden down out").split()
        s = {n: sem(n + "_5") for n in names}
        block = kit.block(c)

        @block.sync
        def _(sp):
            for dst, src in ((ident[:], a["ident"]), (w2[:], a["moe0_w2"]), (wr[:], a["moe0_wr"]), (ln2[:], a["ffn_ln2"]), (spreadf[:], a["moe0_spread"])):
                sp.dma_start(dst, src).then_inc(s["w_in"], 16)
            for j, name in enumerate(("moe0_w1", "moe0_w3")):
                if j:
                    sp.wait_ge(s["half_ready"], 1)
                sp.dma_start(wide_w[:], a[name]).then_inc(s["w_in"], 16)

        @block.gpsimd
        def _(pool):
            pool.memset(half[:], -0.5)
            pool.memset(euler[:], math.e)
            pool.iota(iotai[:], pattern=[[0, T], [1, NE]], base=0, channel_multiplier=0).then_inc(s["ready"], 1)
            pool.drain()

            def squares(n):
                x = X2[:, bass.ds(n * T, T), :]
                pool.tensor_tensor(sq[:], x, x, ALU.mult).then_inc(s["sq_ready"], 1)

            def addends(i):
                kit.hold(pool, s["out"], i + 1)
                rows = bass.ds(i * T, T)
                pool.tensor_tensor(acc[:], X2[:, rows, :], H[:, rows, :], ALU.add).then_inc(s["acc_ready"], 1)

            def split(n, b):
                kit.hold(pool, s["x0_out"], n + 1)
                pool.drain()
                pool.tensor_tensor(flt[64:P], flt[64:P], xa[64:P, b], ALU.subtract)
                pool.drain()
                pool.tensor_copy(xa[64:P, b], flt[64:P])
                pool.drain()
                pool.tensor_tensor(xb[64:P, b], flt[64:P], xa[64:P, b], ALU.subtract).then_inc(s["split"], 1)
                pool.drain()

            def flat_rows(n):
                kit.hold(pool, s["var_ready"], n + 1)
                pool.tensor_tensor(rs[:], var[:], half[:], ALU.pow)
                pool.drain()
                x = X2[:, bass.ds(n * T, T), :]
                pool.tensor_tensor(fl[:, :, 0], x, bcast(rs[:], D), ALU.mult)
                pool.tensor_tensor(fl[:, :, 1], x, bcast(rs[:], D), ALU.mult).then_inc(s["fl_ready"], 1)

            def exps(n):
                kit.hold(pool, s["lg_ready"], n + 1)
                pool.tensor_tensor(pr[:], euler[:], lg[:], ALU.pow).then_inc(s["exp_done"], 1)

            def block_of(i, b):
                flat_rows(i + 1)
                exps(i + 1)
                split(i + 1, 1 - b)
                addends(i)

            squares(0)
            flat_rows(0)
            exps(0)
            split(0, 0)
            squares(1)
            with pool.Fori(0, BLOCKS // 2 - 1) as i:
                for b in range(2):
                    block_of(i * 2 + b, b)
                    squares(i * 2 + b + 2)
            block_of(BLOCKS - 2, 0)
            addends(BLOCKS - 1)

        @block.vector
        def _(dve):
            dve.wait_ge(s["w_in"], 96)
            dve.wait_ge(s["ready"], 1)
            dve.sem_inc(s["out"], 1)
            dve.tensor_copy(identb[:], ident[:])
            dve.tensor_copy(spread[:], spreadf[:])
            dve.tensor_copy(iota[:], iotai[:]).then_inc(s["ready"], 1)
            dve.drain()
            for j in range(2):
                if j:
                    dve.wait_ge(s["w_in"], 112)
                w0, w1, w2_ = w_split[:, j, 0], w_split[:, j, 1], w_split[:, j, 2]
                dve.tensor_copy(w0, wide_w[:])
                dve.drain()
                dve.tensor_tensor(wide_w[:], wide_w[:], w0, ALU.subtract)
                dve.drain()
                dve.tensor_copy(w1, wide_w[:])
                dve.drain()
                dve.tensor_tensor(w2_[0:64], wide_w[0:64], w1[0:64], ALU.subtract)
                dve.tensor_copy(w2_[64:P], w0[64:P])
                dve.drain()
                dve.sem_inc(s["half_ready"], 1)

            def variance(n):
                kit.hold(dve, s["sq_ready"], n + 1)
                dve.tensor_reduce(st[:], sq[:], AX_X, ALU.add)
                dve.drain()
                dve.tensor_scalar(var[:], st[:], 1.0 / D, RMS_EPS, ALU.mult, ALU.add).then_inc(s["var_ready"], 1)

            def shifted(n):
                kit.hold(dve, s["router"], n + 1)
                dve.tensor_copy(lg[:], ps_r[:, 0:T * NE].rearrange("p (t e) -> p t e", e=NE))
                dve.drain()
                dve.tensor_reduce(m[:, 0], lg[:], AX_X, ALU.max)
                dve.drain()
                dve.tensor_tensor(lg[:], lg[:], bcast(m[:, 0], NE), ALU.subtract).then_inc(s["lg_ready"], 1)

            def shares(n):
                kit.hold(dve, s["exp_done"], n + 1)
                dve.tensor_reduce(m[:, 1], pr[:], AX_X, ALU.add)
                dve.drain()
                dve.reciprocal(m[:, 2], m[:, 1])
                dve.drain()
                dve.tensor_tensor(pr[:], pr[:], bcast(m[:, 2], NE), ALU.mult)
                dve.drain()

            def best(n):
                for t in range(T):
                    dve.max(top[:, t], pr[:, t])
                dve.drain()
                for t in range(T):
                    dve.max_index(topi[:, t], top[:, t], pr[:, t])
                dve.tensor_tensor(m[:, 1], top[:, :, 0], top[:, :, 1], ALU.add)
                dve.drain()

            def chosen(n):
                dve.tensor_scalar(m[:, 2], m[:, 1], 1e-9, None, ALU.add)
                dve.tensor_copy(topf[:], topi[:])
                dve.drain()
                dve.reciprocal(m[:, 3], m[:, 2])
                for j in range(2):
                    dve.tensor_tensor(hot[:, j], iota[:], topf[:, :, j:j + 1].to_broadcast([P, T, NE]), ALU.is_equal)
                dve.drain()

            def weights(n):
                dve.tensor_tensor(hot[:, 0], hot[:, 0], hot[:, 1], ALU.add)
                dve.tensor_tensor(wt[:], pr[:], bcast(m[:, 3], NE), ALU.mult)
                dve.drain()
                dve.tensor_tensor(wt[:], wt[:], hot[:, 0], ALU.mult)
                dve.drain()

            def parts(n):
                dve.tensor_copy(w3b[:, :, 0], wt[:])
                dve.drain()
                dve.tensor_tensor(rest[:, 0], wt[:], w3b[:, :, 0], ALU.subtract)
                dve.drain()
                dve.tensor_copy(w3b[:, :, 1], rest[:, 0])
                dve.drain()
                dve.tensor_tensor(rest[:, 1], rest[:, 0], w3b[:, :, 1], ALU.subtract)
                dve.drain()
                dve.tensor_copy(w3b[:, :, 2], rest[:, 1]).then_inc(s["w_ready"], 1)

            def hidden(n, j, b):
                r, buf = slice(0, size[j]), (j + b) % 2
                kit.hold(dve, s["gated"], n * CH + j + 1)
                dve.tensor_tensor(up[r, buf], ps_u[r, buf, 1], gate[r, buf], ALU.mult)
                dve.drain()
                kit.hold(dve, s["wide"], n * CH + j + 1)
                dve.tensor_tensor(hid[r, buf], ps_w[r], up[r, buf], ALU.mult).then_inc(s["hidden"], 1)

            def output(i):
                rows = H[:, bass.ds(i * T, T), :]
                kit.hold(dve, s["acc_ready"], i + 1)
                kit.hold(dve, s["down"], i + 1)
                dve.tensor_tensor(rows, acc[:], ps_d[:, 0:T * D].rearrange("p (t d) -> p t d", t=T), ALU.add).then_inc(s["out"], 1)

            def block_of(i, b, before=True, after=True):
                for j in range(CH):
                    hidden(i, j, b)
                    if j == 0 and before:
                        output(i - 1)
                    if after:
                        {0: variance, 3: shifted, 4: shares, 5: best, 6: chosen, 7: weights, 8: parts}.get(j, lambda n: None)(i + 1)

            variance(0)
            shifted(0)
            for piece in (shares, best, chosen, weights, parts):
                piece(0)
            block_of(0, 0, before=False)
            with dve.Fori(0, BLOCKS // 2 - 1) as i:
                block_of(i * 2 + 1, 1)
                block_of(i * 2 + 2, 0)
            block_of(BLOCKS - 1, 1, after=False)
            output(BLOCKS - 1)

        @block.scalar
        def _(act):
            act.wait_ge(s["w_in"], 112)

            def flat_at(n):
                kit.hold(act, s["flt_done"], n + 1)
                act.activation(flt[:], ps_r[:], ACT.Copy, scale=ln2[:]).then_inc(s["flt_out"], 1)
                act.drain()

            def whole(b):
                act.activation(xa[:, b], flt[:], ACT.Copy)

            def lower(b):
                act.activation(xb[0:64, b], flt[0:64], ACT.Copy).then_inc(s["x0_out"], 1)

            def turned(n, b):
                kit.hold(act, s["wtt_done"], n + 1)
                act.activation(wtt[:, b], ps_x[0:24, 0:W], ACT.Copy).then_inc(s["wtt_out"], 1)

            def block_of(i, n, b):
                for j in range(CH):
                    r, buf = slice(0, size[j]), (j + b) % 2
                    kit.hold(act, s["ups"], i * CH + j + 1)
                    act.activation(gate[r, buf], ps_u[r, buf, 0], ACT.Silu).then_inc(s["gated"], 1)
                    if n is not None:
                        if j == 2:
                            flat_at(n)
                        if j == 3:
                            whole(1 - b)
                        if j == 4:
                            lower(1 - b)
                        if j == 10:
                            turned(n, 1 - b)

            flat_at(0)
            whole(0)
            lower(0)
            turned(0, 0)
            with act.Fori(0, BLOCKS // 2 - 1) as i:
                block_of(i * 2, i * 2 + 1, 0)
                block_of(i * 2 + 1, i * 2 + 2, 1)
            block_of(BLOCKS - 2, BLOCKS - 1, 0)
            block_of(BLOCKS - 1, None, 1)

        @block.tensor
        def _(pe):
            pe.wait_ge(s["w_in"], 112)
            pe.wait_ge(s["ready"], 2)
            pe.wait_ge(s["half_ready"], 2)
            skip = dict(skip_group_check=True)

            def turn_rows(n):
                kit.hold(pe, s["fl_ready"], n + 1)
                for t in range(T):
                    mm = pe.transpose(ps_r[:, P * t:P * t + P], fl[:, t].rearrange("p k d -> p (k d)"), ident[:])
                mm.then_inc(s["flt_done"], 1)

            def router(n, b):
                kit.hold(pe, s["flt_out"], n + 1)
                for t in range(T):
                    mm = pe.matmul(ps_r[:, NE * t:NE * t + NE], flt[0:64, P * t:P * t + P], wr[:], start=True, stop=True)
                mm.then_inc(s["router"], 1)

            def turn_weights(n):
                kit.hold(pe, s["w_ready"], n + 1)
                for t in range(T):
                    mm = pe.transpose(ps_x[0:24, P * t:P * t + P], w3b[:, t].rearrange("p k e -> p (k e)"), identb[:])
                mm.then_inc(s["wtt_done"], 1)

            def ups(i, j, b):
                r = slice(0, size[j])
                cols = slice(P * j, P * j + size[j])
                for which in range(2):
                    for part, x in ((0, xa), (1, xa), (2, xb)):
                        mm = pe.matmul(ps_u[r, (j + b) % 2, which], w_split[:, which, part, cols], x[:, b], start=(part == 0), stop=(part == 2))
                mm.then_inc(s["ups"], 1)

            def wide(i, j, b):
                r = slice(0, size[j])
                pe.matmul(ps_w[r], spread[:, P * j:P * j + size[j]], wtt[:, b], start=True, stop=True).then_inc(s["wide"], 1)

            def block_of(i, n, b):
                for j in range(CH):
                    if j + 1 < CH:
                        ups(i, j + 1, b)
                    elif n is not None:
                        kit.hold(pe, s["split"], n + 1)
                        ups(n, 0, 1 - b)
                    kit.hold(pe, s["hidden"], i * CH + j + 1)
                    if j + 1 < CH:
                        wide(i, j + 1, b)
                    elif n is not None:
                        kit.hold(pe, s["wtt_out"], n + 1)
                        wide(n, 0, 1 - b)
                    if j == 0:
                        kit.hold(pe, s["out"], i + 1)
                    r = slice(0, size[j])
                    for t in range(T):
                        mm = pe.matmul(ps_d[:, D * t:D * t + D], hid[r, (j + b) % 2, P * t:P * t + P], w2[r, j, :],
                                       start=(j == 0 and t == 0), stop=(j == CH - 1 and t == T - 1), **skip)
                    if n is not None:
                        if j == 1:
                            turn_rows(n)
                        if j == 2:
                            router(n, 1 - b)
                        if j == 9:
                            turn_weights(n)
                mm.then_inc(s["down"], 1)

            turn_rows(0)
            router(0, 0)
            turn_weights(0)
            pe.wait_ge(s["split"], 1)
            ups(0, 0, 0)
            pe.wait_ge(s["wtt_out"], 1)
            wide(0, 0, 0)
            with pe.Fori(0, BLOCKS // 2 - 1) as i:
                block_of(i * 2, i * 2 + 1, 0)
                block_of(i * 2 + 1, i * 2 + 2, 1)
            block_of(BLOCKS - 2, BLOCKS - 1, 0)
            block_of(BLOCKS - 1, None, 1)


UNDERFLOW = -104.0


def mamba(nc, kit, a, H, bc_dram):
    CHUNKS, SC = 8, 8
    PIECES = SC // 2
    TC = SC * LEN // P
    W = 2 * LEN
    CW = SC * LEN
    NS, DI, RANK = 64, 128, 16
    GROUP = 4
    with ExitStack() as c:
        sb = lambda n, s, d=F32: kit.sb(c, n, s, d)
        sem = lambda n: kit.sem(c, n)
        ident = sb("ident6", [P, P])
        w_in = sb("w_in6w", [D, 2 * DI])
        w_x = sb("w_x6", [DI, RANK + 2 * NS])
        w_dt = sb("w_dt6", [RANK, DI])
        w_out = sb("w_out6", [DI, D])
        chan = sb("chan6", [DI, 7])
        A = sb("A6", [DI, NS])
        before = sb("before6", [NS, NS])
        slots = sb("slots6", [NS, NS])
        slots_i = sb("slots_i6", [NS, NS], I32)
        index = sb("index6", [NS, 1])
        index_i = sb("index_i6", [NS, 1], I32)
        half = sb("half6", [P, TC])
        keep = sb("keep6", [P, SC, LEN])
        cen = sb("cen6", [P, TC, D])
        sq = sb("sq6", [P, TC, D])
        st = sb("st6", [P, 3, TC])
        var = sb("var6", [P, TC])
        rs = sb("rs6", [P, TC])
        x = sb("x6", [P, TC, D])
        xt = sb("xt6", [D, PIECES, W])
        xpad = sb("xpad6", [DI, SC, LEN + 3])
        u = sb("u6", [DI, SC, LEN])
        dl = sb("dl6", [RANK, 2, W])
        bc = sb("bc6", [2 * NS, SC, LEN])
        delta = sb("delta6", [DI, SC, LEN])
        S = sb("S6", [DI, SC, LEN])
        DU = sb("DU6", [DI, SC, LEN])
        Y = sb("Y6", [DI, SC, LEN])
        Gt = sb("G6", [DI, SC, LEN])
        last_c = sb("last_c6", [NS, SC])
        least = sb("least6", [DI, 1])
        cand = sb("cand6", [DI, NS])
        flag = sb("flag6", [NS, 4])
        place = sb("place6", [NS, NS])
        dead = sb("dead6", [NS, DI])
        lastbc = sb("lastbc6", [NS, SC])
        tail = sb("tail6", [DI, SC])
        todo = sb("todo6", [1, NS + 2])
        todo_i = sb("todo_i6", [1, NS + 2], I32)
        acol = sb("acol6", [DI, 1])
        tiny = sb("tiny6", [DI, 1])
        Bb = sb("Bb6", [DI, SC, LEN])
        Cb = sb("Cb6", [DI, SC, LEN])
        e = sb("e6", [DI, SC, LEN])
        r = sb("r6", [DI, SC, LEN])
        t = sb("t6", [DI, SC, LEN])
        conv, az, rl, ey, lw, yg = t, e, r, Bb, Cb, e
        ps_x = [kit.ps(c, f"ps_x6{b}", [P, W]) for b in range(2)]
        ps_i = [kit.ps(c, f"ps_i6{b}", [P, W]) for b in range(2)]
        ps_g = kit.ps(c, "ps_g6", [P, W])
        ps_b = kit.ps(c, "ps_b6", [P, W])
        ps_f = kit.ps(c, "ps_f6", [P, W])
        ps_o = [kit.ps(c, "ps_o6", [P, W]), ps_b]
        names = ("w_in consts var_ready rs_ready x_ready xt_done xt_out in_done xi_out conv_ready u_ready y_ready dl_done dl_out dt_done z_out "
                 "bc_done bc_out bc_stored ey_ready lw_ready cand_ready cand_done flag_ready rank_done place_ready list_done "
                 "todo_ready acol_ready e_free r_free e_ready r_ready b_in c_in b_free c_free yg_ready o_done h_out g_ready").split()
        s = {n: sem(n + "_6") for n in names}
        block = kit.block(c)

        def flat(ap):
            return ap.rearrange("p a l -> p (a l)")

        def pair(ps):
            return ps[:].rearrange("p (a l) -> p a l", a=2)

        @block.sync
        def _(sp):
            for dst, src in ((ident[:], a["ident"]), (w_in[:], a["mb_win"]), (w_x[:], a["mb_wx"]), (w_dt[:], a["mb_wdt"]),
                             (w_out[:], a["mb_wout"]), (chan[:], a["mb_chan"]), (A[:], a["mb_alog"]), (before[:], a["before"])):
                sp.dma_start(dst, src).then_inc(s["w_in"], 16)
            with sp.Fori(0, CHUNKS) as ch:
                kit.hold(sp, s["bc_out"], (ch + 1) * PIECES)
                sp.dma_start(bc_dram.rearrange("j n (g w) -> g (j n) w", w=CW)[bass.ds(ch, 1), :, :].rearrange("g n w -> (g n) w"),
                             flat(bc[:])).then_inc(s["bc_stored"], 16)
                kit.hold(sp, s["bc_stored"], ch * 16 + 32)
                kit.hold(sp, s["todo_ready"], ch + 1)
                count = sp.value_load(todo_i[0:1, NS:NS + 1], min_val=0, max_val=NS)
                done = sp.value_load(todo_i[0:1, NS + 1:NS + 2], min_val=0, max_val=NS * CHUNKS)
                with sp.Fori(0, NS // GROUP ** 2) as far:
                    with sp.If(far * GROUP ** 2 < count):
                        with sp.Fori(0, GROUP) as mid:
                            with sp.If((far * GROUP + mid) * GROUP < count):
                                with sp.Fori(0, GROUP) as near:
                                    k = (far * GROUP + mid) * GROUP + near
                                    with sp.If(k < count):
                                        state = sp.value_load(todo_i[0:1, bass.ds(k, 1)], min_val=0, max_val=NS - 1)
                                        for j, dst, name in ((0, Bb, "b"), (1, Cb, "c")):
                                            kit.hold(sp, s[name + "_free"], done + k + 1)
                                            row = bc_dram[j, bass.ds(state, 1), bass.ds(ch * CW, CW)]
                                            sp.dma_start(flat(dst[:]), row.to_broadcast([DI, CW])).then_inc(s[name + "_in"], 16)

        @block.gpsimd
        def _(pool):
            pool.memset(half[:], -0.5)
            pool.iota(slots_i[:], pattern=[[1, NS]], base=0, channel_multiplier=0)
            pool.iota(index_i[:], pattern=[[0, 1]], base=0, channel_multiplier=1).then_inc(s["consts"], 1)
            pool.drain()

            def roots(ch):
                kit.hold(pool, s["var_ready"], ch + 1)
                pool.tensor_tensor(rs[:], var[:], half[:], ALU.pow).then_inc(s["rs_ready"], 1)

            roots(0)
            with pool.Fori(0, CHUNKS) as ch:
                roots(ch + 1)
                kit.hold(pool, s["todo_ready"], ch + 1)
                count = pool.value_load(todo_i[0:1, NS:NS + 1], min_val=0, max_val=NS)
                done = pool.value_load(todo_i[0:1, NS + 1:NS + 2], min_val=0, max_val=NS * CHUNKS)
                with pool.Fori(0, NS // GROUP ** 2) as far:
                    with pool.If(far * GROUP ** 2 < count):
                        with pool.Fori(0, GROUP) as mid:
                            with pool.If((far * GROUP + mid) * GROUP < count):
                                with pool.Fori(0, GROUP) as near:
                                    k = (far * GROUP + mid) * GROUP + near
                                    with pool.If(k < count):
                                        state = pool.value_load(todo_i[0:1, bass.ds(k, 1)], min_val=0, max_val=NS - 1)
                                        kit.hold(pool, s["e_ready"], done + k + 1)
                                        pool.tensor_copy(acol[:], A[:, bass.ds(state, 1)]).then_inc(s["acol_ready"], 1)

        @block.scalar
        def _(act):
            act.wait_ge(s["w_in"], 128)
            act.wait_ge(s["consts"], 2)
            act.activation(A[:], A[:], ACT.Exp).then_inc(s["consts"], 1)
            with act.Fori(0, CHUNKS) as ch:
                def count(p):
                    return ch * PIECES + p + 1

                def two(p):
                    return slice(2 * p, 2 * p + 2)

                def tokens(p):
                    kit.hold(act, s["xt_done"], count(p))
                    act.activation(xt[:, p], ps_x[p % 2][0:D, :], ACT.Copy).then_inc(s["xt_out"], 1)

                def halves(p):
                    kit.hold(act, s["in_done"], count(p))
                    act.activation(xpad[:, two(p), 3:LEN + 3], pair(ps_i[p % 2]), ACT.Copy).then_inc(s["xi_out"], 1)
                    act.activation(Gt[:, two(p), :], pair(ps_g), ACT.Silu).then_inc(s["g_ready"], 1)

                def convolved(p):
                    kit.hold(act, s["conv_ready"], count(p))
                    act.activation(u[:, two(p)], conv[:, two(p)], ACT.Silu, bias=chan[:, 4:5]).then_inc(s["u_ready"], 1)

                def projected(p):
                    kit.hold(act, s["dl_done"], count(p))
                    act.activation(dl[:, p % 2], ps_x[p % 2][0:RANK, :], ACT.Copy).then_inc(s["dl_out"], 1)
                    if p == 0:
                        kit.hold(act, s["bc_stored"], ch * 16 + 16)
                    kit.hold(act, s["bc_done"], count(p))
                    act.activation(bc[:, two(p)], pair(ps_b), ACT.Copy).then_inc(s["bc_out"], 1)

                def sizes(p):
                    kit.hold(act, s["dt_done"], count(p))
                    act.activation(az[:, two(p)], pair(ps_i[p % 2]), ACT.Abs, bias=chan[:, 5:6])
                    act.activation(rl[:, two(p)], pair(ps_i[p % 2]), ACT.Relu, bias=chan[:, 5:6]).then_inc(s["z_out"], 1)

                tokens(0)
                tokens(1)
                halves(0)
                tokens(2)
                halves(1)
                tokens(3)
                halves(2)
                convolved(0)
                projected(0)
                halves(3)
                convolved(1)
                sizes(0)
                projected(1)
                convolved(2)
                sizes(1)
                projected(2)
                convolved(3)
                sizes(2)
                projected(3)
                sizes(3)
                act.activation(Y[:], u[:], ACT.Copy, scale=chan[:, 6:7]).then_inc(s["y_ready"], 1)
                act.drain()
                act.activation(ey[:], az[:], ACT.Exp, scale=-1.0).then_inc(s["ey_ready"], 1)
                act.drain()
                act.activation(lw[:], ey[:], ACT.Ln, bias=1.0).then_inc(s["lw_ready"], 1)
                kit.hold(act, s["todo_ready"], ch + 1)
                count = act.value_load(todo_i[0:1, NS:NS + 1], min_val=0, max_val=NS)
                done = act.value_load(todo_i[0:1, NS + 1:NS + 2], min_val=0, max_val=NS * CHUNKS)
                with act.Fori(0, NS // GROUP ** 2) as far:
                    with act.If(far * GROUP ** 2 < count):
                        with act.Fori(0, GROUP) as mid:
                            with act.If((far * GROUP + mid) * GROUP < count):
                                with act.Fori(0, GROUP) as near:
                                    k = (far * GROUP + mid) * GROUP + near
                                    with act.If(k < count):
                                        kit.hold(act, s["acol_ready"], done + k + 1)
                                        kit.hold(act, s["e_free"], done + k + 1)
                                        act.activation(e[:], S[:], ACT.Exp, scale=acol[:]).then_inc(s["e_ready"], 1)
                                        act.drain()
                                        kit.hold(act, s["r_free"], done + k + 1)
                                        act.activation(r[:], e[:], ACT.Ln, bias=tiny[:])
                                        act.drain()
                                        act.activation(r[:], r[:], ACT.Exp, scale=-1.0).then_inc(s["r_ready"], 1)

        @block.vector
        def _(dve):
            dve.sem_inc(s["bc_stored"], 16)
            dve.sem_inc(s["b_free"], 1)
            dve.sem_inc(s["c_free"], 1)
            dve.sem_inc(s["e_free"], 1)
            dve.sem_inc(s["e_ready"], 1)
            dve.sem_inc(s["r_free"], 1)
            dve.memset(xpad[:], 0.0)
            dve.memset(S[:], 0.0)
            dve.memset(tiny[:], 1e-12)
            dve.memset(todo[:], 0.0)
            dve.memset(keep[:], 1.0)
            dve.drain()
            dve.memset(keep[:, :, 0:1], 0.0).then_inc(s["consts"], 1)
            dve.wait_ge(s["w_in"], 128)
            dve.wait_ge(s["consts"], 3)
            dve.tensor_scalar(A[:], A[:], -1.0, None, ALU.mult)
            dve.tensor_copy(slots[:], slots_i[:])
            dve.tensor_copy(index[:], index_i[:])
            dve.drain()

            def norm(ch):
                norm_statistics(dve, H[:, bass.ds(ch % CHUNKS * TC, TC), :], cen[:], sq[:], st)
                dve.tensor_scalar(var[:], st[:, 2], 1.0 / D, LN_EPS, ALU.mult, ALU.add).then_inc(s["var_ready"], 1)
                kit.hold(dve, s["rs_ready"], ch + 1)
                dve.tensor_tensor(x[:], cen[:], bcast(rs[:], D), ALU.mult).then_inc(s["x_ready"], 1)

            norm(0)
            with dve.Fori(0, CHUNKS) as ch:
                for p in range(PIECES):
                    two = slice(2 * p, 2 * p + 2)
                    kit.hold(dve, s["xi_out"], ch * PIECES + p + 1)
                    dve.tensor_scalar(conv[:, two], xpad[:, two, 0:LEN], chan[:, 0:1], None, ALU.mult)
                    for tap in range(1, 4):
                        dve.drain()
                        w = dve.scalar_tensor_tensor(conv[:, two], xpad[:, two, tap:tap + LEN], chan[:, tap:tap + 1], conv[:, two], ALU.mult, ALU.add)
                    w.then_inc(s["conv_ready"], 1)
                norm(ch + 1)
                kit.hold(dve, s["ey_ready"], ch + 1)
                dve.tensor_scalar(az[:], ey[:], 1.0, -1.0, ALU.add, ALU.add)
                dve.drain()
                dve.tensor_tensor(az[:], ey[:], az[:], ALU.subtract)
                dve.drain()
                dve.tensor_tensor(az[:], az[:], rl[:], ALU.add)
                dve.drain()
                kit.hold(dve, s["lw_ready"], ch + 1)
                dve.tensor_tensor(delta[:], az[:], lw[:], ALU.add)
                dve.drain()
                dve.tensor_tensor(DU[:], delta[:], u[:], ALU.mult)
                for j in range(SC):
                    dve.tensor_tensor_scan(S[:, j, LEN - 2::-1], keep[:, 0, 1:LEN], delta[:, j, :0:-1], 0.0, ALU.mult, ALU.add)
                dve.tensor_copy(last_c[:], bc[NS:2 * NS, :, LEN - 1])
                dve.drain()
                dve.tensor_reduce(least[:], S[:, :, LEN - 2], AX_X, ALU.min)
                dve.drain()
                dve.tensor_scalar(cand[:], A[:], least[:], None, ALU.mult).then_inc(s["cand_ready"], 1)
                kit.hold(dve, s["cand_done"], ch + 1)
                dve.tensor_reduce(flag[:, 0:1], ps_f[0:NS, 0:DI], AX_X, ALU.max)
                dve.drain()
                dve.tensor_scalar(flag[:, 2:3], flag[:, 0:1], UNDERFLOW, None, ALU.is_lt)
                dve.drain()
                dve.tensor_scalar(flag[:, 1:2], flag[:, 2:3], -1.0, 1.0, ALU.mult, ALU.add)
                dve.tensor_tensor(lastbc[:], bc[0:NS, :, LEN - 1], last_c[:], ALU.mult)
                dve.tensor_copy(dead[:], flag[:, 2:3].to_broadcast([NS, DI])).then_inc(s["flag_ready"], 1)
                kit.hold(dve, s["rank_done"], ch + 1)
                dve.tensor_copy(flag[:, 3:4], ps_f[0:NS, 128:129])
                dve.tensor_tensor(tail[:], ps_f[:, 192:192 + SC], DU[:, :, LEN - 1], ALU.mult)
                dve.drain()
                dve.tensor_scalar(place[:], slots[:], flag[:, 3:4], flag[:, 1:2], ALU.is_equal, ALU.mult).then_inc(s["place_ready"], 1)
                kit.hold(dve, s["y_ready"], ch + 1)
                dve.tensor_tensor(Y[:, :, LEN - 1], Y[:, :, LEN - 1], tail[:], ALU.add)
                dve.tensor_tensor(todo[:, NS + 1:NS + 2], todo[:, NS + 1:NS + 2], todo[:, NS:NS + 1], ALU.add)
                dve.drain()
                kit.hold(dve, s["list_done"], ch + 1)
                dve.tensor_copy(todo[:, 0:NS + 1], ps_f[0:1, 256:256 + NS + 1])
                dve.drain()
                dve.tensor_copy(todo_i[:], todo[:]).then_inc(s["todo_ready"], 1)
                kit.hold(dve, s["todo_ready"], ch + 1)
                count = dve.value_load(todo_i[0:1, NS:NS + 1], min_val=0, max_val=NS)
                done = dve.value_load(todo_i[0:1, NS + 1:NS + 2], min_val=0, max_val=NS * CHUNKS)
                with dve.Fori(0, NS // GROUP ** 2) as far:
                    with dve.If(far * GROUP ** 2 < count):
                        with dve.Fori(0, GROUP) as mid:
                            with dve.If((far * GROUP + mid) * GROUP < count):
                                with dve.Fori(0, GROUP) as near:
                                    k = (far * GROUP + mid) * GROUP + near
                                    with dve.If(k < count):
                                        kit.hold(dve, s["b_in"], (done + k + 1) * 16)
                                        dve.tensor_tensor(t[:], DU[:], Bb[:], ALU.mult).then_inc(s["b_free"], 1)
                                        dve.drain()
                                        kit.hold(dve, s["e_ready"], done + k + 2)
                                        dve.tensor_tensor(t[:], t[:], e[:], ALU.mult).then_inc(s["e_free"], 1)
                                        dve.drain()
                                        dve.tensor_tensor_scan(flat(t[:]), flat(keep[:]), flat(t[:]), 0.0, ALU.mult, ALU.add)
                                        dve.drain()
                                        kit.hold(dve, s["r_ready"], done + k + 1)
                                        dve.tensor_tensor(t[:], t[:], r[:], ALU.mult).then_inc(s["r_free"], 1)
                                        dve.drain()
                                        kit.hold(dve, s["c_in"], (done + k + 1) * 16)
                                        dve.tensor_tensor(t[:], t[:], Cb[:], ALU.mult).then_inc(s["c_free"], 1)
                                        dve.drain()
                                        dve.tensor_tensor(Y[:], Y[:], t[:], ALU.add)
                                        dve.drain()
                kit.hold(dve, s["g_ready"], (ch + 1) * PIECES)
                for p in range(PIECES):
                    two = slice(2 * p, 2 * p + 2)
                    dve.tensor_tensor(yg[:, two], Y[:, two], Gt[:, two], ALU.mult).then_inc(s["yg_ready"], 1)
                for g in range(2):
                    kit.hold(dve, s["o_done"], ch * 2 + g + 1)
                    rows = H[:, bass.ds(ch * TC + g * (TC // 2), TC // 2), :]
                    dve.tensor_tensor(rows, rows, ps_o[g][:].rearrange("p (t d) -> p t d", d=D), ALU.add).then_inc(s["h_out"], 1)
                dve.drain()

        @block.tensor
        def _(pe):
            pe.wait_ge(s["w_in"], 128)
            pe.wait_ge(s["consts"], 3)
            with pe.Fori(0, CHUNKS) as ch:
                def count(p):
                    return ch * PIECES + p + 1

                def turn(p):
                    if p > 1:
                        kit.hold(pe, s["xt_out"], count(p - 2))
                    for t4 in range(4):
                        mm = pe.transpose(ps_x[p % 2][0:D, P * t4:P * t4 + P], x[:, 4 * p + t4, :], ident[:])
                    mm.then_inc(s["xt_done"], 1)

                def inner(p):
                    kit.hold(pe, s["xt_out"], count(p))
                    if p > 0:
                        kit.hold(pe, s["g_ready"], count(p - 1))
                    pe.matmul(ps_i[p % 2][:], w_in[:, 0:DI], xt[:, p], start=True, stop=True)
                    pe.matmul(ps_g[:], w_in[:, DI:2 * DI], xt[:, p], start=True, stop=True).then_inc(s["in_done"], 1)

                def project(p):
                    kit.hold(pe, s["u_ready"], count(p))
                    if p > 0:
                        kit.hold(pe, s["bc_out"], count(p - 1))
                    pe.matmul(ps_x[p % 2][0:RANK, :], w_x[:, 0:RANK], u[:, 2 * p:2 * p + 2], start=True, stop=True).then_inc(s["dl_done"], 1)
                    pe.matmul(ps_b[:], w_x[:, RANK:RANK + 2 * NS], u[:, 2 * p:2 * p + 2], start=True, stop=True).then_inc(s["bc_done"], 1)

                def sizes(p):
                    kit.hold(pe, s["dl_out"], count(p))
                    if p > 1:
                        kit.hold(pe, s["z_out"], count(p - 2))
                    else:
                        kit.hold(pe, s["xi_out"], count(p + 2))
                    pe.matmul(ps_i[p % 2][:], w_dt[:], dl[:, p % 2], start=True, stop=True).then_inc(s["dt_done"], 1)

                kit.hold(pe, s["x_ready"], ch + 1)
                turn(0)
                turn(1)
                inner(0)
                turn(2)
                inner(1)
                turn(3)
                inner(2)
                project(0)
                inner(3)
                sizes(0)
                project(1)
                sizes(1)
                project(2)
                sizes(2)
                project(3)
                sizes(3)
                kit.hold(pe, s["cand_ready"], ch + 1)
                pe.transpose(ps_f[0:NS, 0:DI], cand[:], ident[:]).then_inc(s["cand_done"], 1)
                kit.hold(pe, s["flag_ready"], ch + 1)
                pe.matmul(ps_f[0:NS, 128:129], before[:], flag[:, 1:2], start=True, stop=True)
                pe.matmul(ps_f[:, 192:192 + SC], dead[:], lastbc[:], start=True, stop=True).then_inc(s["rank_done"], 1)
                kit.hold(pe, s["place_ready"], ch + 1)
                pe.matmul(ps_f[0:1, 256:256 + NS], index[:], place[:], start=True, stop=True)
                pe.matmul(ps_f[0:1, 256 + NS:257 + NS], flag[:, 1:2], flag[:, 1:2], start=True, stop=True).then_inc(s["list_done"], 1)
                for p in range(PIECES):
                    kit.hold(pe, s["yg_ready"], ch * PIECES + p + 1)
                    for t4 in range(4):
                        at = D * (4 * (p % 2) + t4)
                        mm = pe.matmul(ps_o[p // 2][:, at:at + D], flat(yg[:])[:, P * (4 * p + t4):P * (4 * p + t4) + P], w_out[:], start=True, stop=True)
                    if p % 2:
                        mm.then_inc(s["o_done"], 1)

def sparse_experts(nc, kit, a, H, out):
    NE, HID = 64, 128
    SLOTS = 2 * TILES + NE
    with ExitStack() as top:
        GATE = kit.sb(top, "GATE", [P, 2, TILES])
        SLOT = kit.sb(top, "SLOT", [P, 2, TILES], U32)
        OWNER = kit.sb(top, "OWNER", [1, SLOTS], I32)
        xs = nc.dram_tensor("xs_dram", (SLOTS * P, D), F32).ap()
        ys = nc.dram_tensor("ys_dram", (SLOTS * P, D), F32).ap()
        route_and_scatter(nc, kit, a, H, GATE, SLOT, OWNER, xs, SLOTS)
        run_experts(nc, kit, a, OWNER, xs, ys, SLOTS)
        combine(nc, kit, H, GATE, SLOT, ys, out)


def route_and_scatter(nc, kit, a, H, GATE, SLOT, OWNER, xs, SLOTS):
    NE, T = 64, 8
    STEPS = TILES // T
    G = 8
    Z = 2048
    with ExitStack() as c:
        sb = lambda n, s, d=F32: kit.sb(c, n, s, d)
        sem = lambda n: kit.sem(c, n)
        X = sb("X9", [P, TILES, D])
        ident = sb("ident9", [P, P])
        wr = sb("wr9", [D + 1, NE])
        prior_f = sb("prior_f9", [P, P])
        prior = sb("prior9", [P, P], BF16)
        ones = sb("ones9", [P, P], BF16)
        onesf = sb("onesf9", [P, P])
        zero = sb("zero9", [P, Z])
        iota_i = sb("iota_i9", [P, G, NE], I32)
        iota = sb("iota9", [P, G, NE])
        thr_i = sb("thr_i9", [P, 1], I32)
        thr = sb("thr9", [P, 1])
        kth_i = sb("kth_i9", [NE, SLOTS], I32)
        kth = sb("kth9", [NE, SLOTS])
        half = sb("half9", [P, T])
        cen = sb("cen9", [P, T, D])
        sq = sb("sq9", [P, T, D])
        st = sb("st9", [P, 3, T])
        var = sb("var9", [P, T])
        rs = sb("rs9", [P, T])
        x = sb("x9", [P, T, D])
        xt = sb("xt9", [D + 1, T * P])
        lg = sb("lg9", [P, 2, T, NE])
        top = sb("top9", [P, T, 8])
        topi = sb("topi9", [P, T, 8], U32)
        hot = sb("hot9", [P, 2, T, NE])
        both = sb("both9", [P, T, NE], BF16)
        mt = sb("mt9", [P, 2, T, NE])
        seen = sb("seen9", [P, NE])
        seen_add = sb("seen_add9", [P, NE])
        seen_b = sb("seen_b9", [P, NE], BF16)
        L1 = sb("L1_9", [P, 2, TILES])
        IDX = sb("IDX9", [P, 2, TILES])
        RANK = sb("RANK9", [P, 2, TILES])
        total = sb("total9", [P, NE])
        full = sb("full9", [P, NE])
        tiles = sb("tiles9", [P, NE])
        end = sb("end9", [P, NE])
        base = sb("base9", [P, NE])
        endc = sb("endc9", [NE, 1])
        past = sb("past9", [NE, SLOTS])
        own = sb("own9", [1, SLOTS])
        big = sb("big9", [P, G, NE])
        off = sb("off9", [P, G])
        rows = sb("rows9", [P, 2, G, D])
        slot_now = sb("slot_now9", [P, 2, 2, G], U32)
        ps_x = kit.ps(c, "ps_x9", [P, T * P])
        ps_l = kit.ps(c, "ps_l9", [P, 512])
        ps_r = kit.ps(c, "ps_r9", [P, 512])
        ps_m = kit.ps(c, "ps_m9", [P, 512])
        names = ("w_in consts ready var_ready x_ready xt_done xt_out l_done lg_out both_ready r_done seen_ready cleared "
                 "total_done full_ready tiles_done end_ready endc_done past_ready own_done diff_ready exp_done rows_ready "
                 ).split()
        s = {n: sem(n + "_9") for n in names}
        s["scattered"] = kit.indirect["scattered"]
        block = kit.block(c)

        @block.sync
        def _(sp):
            for dst, src in ((ident[:], a["ident"]), (wr[:], a["moe1_wr"]), (prior_f[:], a["prior"])):
                sp.dma_start(dst, src).then_inc(s["w_in"], 16)
            sp.wait_ge(s["ready"], 1)
            per = P * Z // D
            for j in range(SLOTS * P // per):
                sp.dma_start(xs[j * per:(j + 1) * per, :].rearrange("(p r) d -> p (r d)", p=P), zero[:]).then_inc(s["cleared"], 16)

        @block.gpsimd
        def _(pool):
            pool.memset(half[:], -0.5)
            pool.iota(iota_i[:], pattern=[[0, G], [1, NE]], base=0, channel_multiplier=0)
            pool.iota(thr_i[:], pattern=[[0, 1]], base=0, channel_multiplier=P)
            pool.iota(kth_i[:], pattern=[[1, SLOTS]], base=0, channel_multiplier=0).then_inc(s["consts"], 1)
            pool.drain()

            def normed(n, later=True):
                kit.hold(pool, s["var_ready"], n + 1)
                pool.tensor_tensor(rs[:], var[:], half[:], ALU.pow)
                pool.drain()
                if later:
                    kit.hold(pool, s["xt_done"], n)
                pool.tensor_tensor(x[:], cen[:], bcast(rs[:], D), ALU.mult)
                pool.tensor_tensor(X[:, bass.ds(n * T, T), :], cen[:], bcast(rs[:], D), ALU.mult).then_inc(s["x_ready"], 1)

            normed(0, later=False)
            with pool.Fori(1, STEPS) as n:
                normed(n)
            pool.wait_ge(s["cleared"], 16 * (SLOTS * D // Z))
            with pool.Fori(0, TILES // G // 2) as i:
                for b in range(2):
                    n = i * 2 + b
                    kit.hold(pool, s["rows_ready"], n + 1)
                    pool.tensor_copy(slot_now[:, b], SLOT[:, :, bass.ds(n * G, G)])
                    pool.drain()
                    for t in range(G):
                        for j in range(2):
                            pool.indirect_dma_start(xs, bass.IndirectOffsetOnAxis(ap=slot_now[:, b, j, t:t + 1], axis=0),
                                                    rows[:, b, t, :], None).then_inc(s["scattered"][b], 16)
            for b in range(2):
                pool.wait_ge(s["scattered"][b], 16 * TILES)

        @block.scalar
        def _(act):
            act.wait_ge(s["ready"], 1)

            def step(n, b):
                kit.hold(act, s["xt_done"], n + 1)
                for half_ in range(2):
                    cols = slice(half_ * (T * P // 2), (half_ + 1) * (T * P // 2))
                    w = act.activation(xt[0:D, cols], ps_x[0:D, cols], ACT.Copy)
                w.then_inc(s["xt_out"], 1)
                kit.hold(act, s["l_done"], n + 1)
                act.activation(lg[:, b], ps_l[:, 0:T * NE].rearrange("p (t e) -> p t e", e=NE), ACT.Copy).then_inc(s["lg_out"], 1)

            with act.Fori(0, STEPS // 2) as i:
                step(i * 2, 0)
                step(i * 2 + 1, 1)
            act.wait_ge(s["diff_ready"], 1)
            act.activation(GATE[:, 1], GATE[:, 1], ACT.Exp).then_inc(s["exp_done"], 1)

        @block.vector
        def _(dve):
            dve.memset(zero[:], 0.0)
            dve.memset(xt[D:D + 1, :], 1.0)
            dve.memset(seen[:], 0.0)
            dve.memset(ones[:], 1.0)
            dve.memset(onesf[:], 1.0)
            dve.memset(seen_b[:], 0.0)
            dve.drain().then_inc(s["ready"], 1)
            dve.wait_ge(s["w_in"], 48)
            dve.wait_ge(s["consts"], 1)
            dve.tensor_copy(prior[:], prior_f[:])
            dve.tensor_copy(iota[:], iota_i[:])
            dve.tensor_copy(thr[:], thr_i[:])
            dve.tensor_copy(kth[:], kth_i[:])
            dve.drain().then_inc(s["ready"], 1)

            def norm(n, later=True):
                if later:
                    kit.hold(dve, s["x_ready"], n)
                norm_statistics(dve, H[:, bass.ds(n * T, T), :], cen[:], sq[:], st)
                dve.tensor_scalar(var[:], st[:, 2], 1.0 / D, LN_EPS, ALU.mult, ALU.add).then_inc(s["var_ready"], 1)

            def route(n, b, following):
                here = bass.ds(n * T, T)
                kit.hold(dve, s["lg_out"], n + 1)
                for t in range(T):
                    dve.max(top[:, t], lg[:, b, t])
                dve.drain()
                for t in range(T):
                    dve.max_index(topi[:, t], top[:, t], lg[:, b, t])
                dve.tensor_copy(L1[:, :, here].rearrange("p j t -> p t j"), top[:, :, 0:2])
                dve.drain()
                dve.tensor_copy(IDX[:, :, here].rearrange("p j t -> p t j"), topi[:, :, 0:2])
                dve.drain()
                for j in range(2):
                    dve.tensor_tensor(hot[:, j], iota[:, 0:T], bcast(IDX[:, j, here], NE), ALU.is_equal)
                dve.drain()
                dve.tensor_tensor(both[:], hot[:, 0], hot[:, 1], ALU.add).then_inc(s["both_ready"], 1)
                dve.drain()
                dve.tensor_reduce(seen_add[:], both[:].rearrange("p t e -> p e t"), AX_X, ALU.add)
                following()
                kit.hold(dve, s["r_done"], n + 1)
                for j in range(2):
                    dve.tensor_tensor(mt[:, j], ps_r[:, 0:T * NE].rearrange("p (t e) -> p t e", e=NE), hot[:, j], ALU.mult)
                dve.drain()
                for j in range(2):
                    dve.tensor_reduce(RANK[:, j, here], mt[:, j], AX_X, ALU.add)
                dve.tensor_tensor(seen[:], seen[:], seen_add[:], ALU.add)
                dve.drain()
                dve.tensor_copy(seen_b[:], seen[:]).then_inc(s["seen_ready"], 1)

            norm(0, later=False)
            norm(1)
            with dve.Fori(0, STEPS // 2 - 1) as i:
                for b in range(2):
                    route(i * 2 + b, b, lambda: norm(i * 2 + b + 2))
            route(STEPS - 2, 0, lambda: None)
            route(STEPS - 1, 1, lambda: None)
            dve.drain()
            dve.tensor_tensor(GATE[:, 1], L1[:, 1], L1[:, 0], ALU.subtract).then_inc(s["diff_ready"], 1)
            dve.wait_ge(s["total_done"], 1)
            dve.tensor_copy(total[:], ps_m[:, 0:NE])
            dve.drain()
            dve.tensor_scalar(full[:], total[:], thr[:], None, ALU.is_gt).then_inc(s["full_ready"], 1)
            dve.wait_ge(s["tiles_done"], 1)
            dve.tensor_copy(tiles[:], ps_m[:, NE:2 * NE])
            dve.drain()
            dve.tensor_tensor_scan(end[:], onesf[:, 0:NE], tiles[:], 0.0, ALU.mult, ALU.add).then_inc(s["end_ready"], 1)
            dve.drain()
            dve.tensor_tensor(base[:], end[:], tiles[:], ALU.subtract)
            dve.drain()
            dve.tensor_scalar(base[:], base[:], float(P), None, ALU.mult)
            dve.wait_ge(s["endc_done"], 1)
            dve.tensor_copy(endc[:], ps_m[0:NE, 128:129])
            dve.drain()
            dve.tensor_scalar(past[:], kth[:], endc[:], None, ALU.is_ge).then_inc(s["past_ready"], 1)
            dve.wait_ge(s["own_done"], 1)
            dve.tensor_scalar(own[:], ps_l[0:1, 0:SLOTS], float(NE - 1), None, ALU.min)
            dve.drain()
            dve.tensor_copy(OWNER[:], own[:])
            dve.wait_ge(s["exp_done"], 1)
            dve.tensor_scalar(L1[:, 0], GATE[:, 1], 1.0, None, ALU.add)
            dve.drain()
            dve.reciprocal(GATE[:, 0], L1[:, 0])
            dve.drain()
            dve.tensor_tensor(GATE[:, 1], GATE[:, 1], GATE[:, 0], ALU.mult)

            def place_rows(i, b, later=True):
                n = i * 2 + b
                here = bass.ds(n * G, G)
                for j in range(2):
                    dve.tensor_tensor(big[:], iota[:], bcast(IDX[:, j, here], NE), ALU.is_equal)
                    dve.drain()
                    dve.tensor_tensor(big[:], big[:], base[:].unsqueeze(1).to_broadcast([P, G, NE]), ALU.mult)
                    dve.drain()
                    dve.tensor_reduce(off[:], big[:], AX_X, ALU.add)
                    dve.drain()
                    dve.tensor_tensor(off[:], off[:], RANK[:, j, here], ALU.add)
                    dve.drain()
                    dve.tensor_copy(SLOT[:, j, here], off[:])
                if later:
                    kit.hold(dve, s["scattered"][b], i * (16 * 2 * G))
                dve.tensor_copy(rows[:, b], X[:, here, :])
                dve.drain().then_inc(s["rows_ready"], 1)

            place_rows(0, 0, later=False)
            place_rows(0, 1, later=False)
            with dve.Fori(1, TILES // G // 2) as i:
                for b in range(2):
                    place_rows(i, b)

        @block.tensor
        def _(pe):
            pe.wait_ge(s["w_in"], 48)
            pe.wait_ge(s["ready"], 2)
            skip = dict(skip_group_check=True)

            def logits(n, later=True):
                kit.hold(pe, s["x_ready"], n + 1)
                for t in range(T):
                    mm = pe.transpose(ps_x[0:D, P * t:P * t + P], x[:, t, :], ident[:])
                mm.then_inc(s["xt_done"], 1)
                kit.hold(pe, s["xt_out"], n + 1)
                if later:
                    kit.hold(pe, s["lg_out"], n)
                for t in range(T):
                    mm = pe.matmul(ps_l[:, NE * t:NE * t + NE], xt[:, P * t:P * t + P], wr[:], start=True, stop=True)
                mm.then_inc(s["l_done"], 1)

            def ranks(n, later=True):
                kit.hold(pe, s["both_ready"], n + 1)
                if later:
                    kit.hold(pe, s["seen_ready"], n)
                pe.matmul(ps_r[:, 0:T * NE], prior[:], both[:].rearrange("p t e -> p (t e)"), start=True, stop=False, **skip)
                for t in range(T):
                    src, to = (seen_b[:], T) if t == 0 else (both[:, t - 1], T - t)
                    mm = pe.matmul(ps_r[:, NE * (T - to):NE * T].rearrange("p (t e) -> p t e", e=NE), ones[:], src.unsqueeze(1).to_broadcast([P, to, NE]),
                                   start=False, stop=(t == T - 1), **skip)
                mm.then_inc(s["r_done"], 1)

            logits(0, later=False)
            logits(1)
            ranks(0, later=False)
            with pe.Fori(2, STEPS) as n:
                logits(n)
                ranks(n - 1)
            ranks(STEPS - 1)
            pe.wait_ge(s["seen_ready"], STEPS)
            pe.matmul(ps_m[:, 0:NE], ones[:], seen_b[:], start=True, stop=True).then_inc(s["total_done"], 1)
            pe.wait_ge(s["full_ready"], 1)
            pe.matmul(ps_m[:, NE:2 * NE], onesf[:], full[:], start=True, stop=True).then_inc(s["tiles_done"], 1)
            pe.wait_ge(s["end_ready"], 1)
            pe.matmul(ps_m[0:NE, 128:129], end[0:1, :], onesf[0:1, 0:1], start=True, stop=True).then_inc(s["endc_done"], 1)
            pe.wait_ge(s["past_ready"], 1)
            pe.matmul(ps_l[0:1, 0:SLOTS], onesf[0:NE, 0:1], past[:], start=True, stop=True).then_inc(s["own_done"], 1)


def run_experts(nc, kit, a, OWNER, xs, ys, SLOTS):
    NE, HID, T, BUF = 64, 128, 4, 4
    GROUPS = SLOTS // T
    with ExitStack() as c:
        sb = lambda n, s, d=F32: kit.sb(c, n, s, d)
        sem = lambda n: kit.sem(c, n)
        ident = sb("ident10", [P, P])
        x = sb("x10", [P, BUF, T, D])
        xt = sb("xt10", [D + 1, 2, T * P])
        w = sb("w_10", [P, BUF, T, HID + D])
        bias = sb("bias10", [P, P])
        h = sb("h10", [HID, 2, T * P])
        y = sb("y10", [P, 2, T, D])
        ps_x = kit.ps(c, "ps_x10", [P, 2, T * P])
        ps_h = kit.ps(c, "ps_h10", [P, 2, T * P])
        ps_y = kit.ps(c, "ps_y10", [P, 2, 512])
        names = "w_in ready t_done xt_out h_done h_out y_done y_out".split()
        s = {n: sem(n + "_10") for n in names}
        s.update({n: [sem(f"{n}{b}_10") for b in range(BUF)] for n in ("x_in", "w_got")})
        s["stored"] = [sem("stored0_10"), sem("stored1_10")]
        block = kit.block(c)

        @block.sync
        def _(sp):
            sp.dma_start(ident[:], a["ident"]).then_inc(s["w_in"], 16)
            with sp.Fori(0, GROUPS // BUF) as i:
                for b in range(BUF):
                    g = i * BUF + b
                    kit.hold(sp, s["t_done"], g + 1)
                    sp.dma_start(x[:, b], xs.rearrange("(g t p) d -> g p t d", t=T, p=P)[bass.ds(g, 1), :, :, :].rearrange("g p t d -> (g p) t d")).then_inc(s["x_in"][b], 16)
                    kit.hold(sp, s["y_done"], g + 1)
                    for t in range(T):
                        e = sp.value_load(OWNER[0:1, bass.ds(g * T + t, 1)], min_val=0, max_val=NE - 1)
                        sp.dma_start(w[:, b, t], a["moe1_w"][bass.ds(e, 1), :, :].rearrange("e k n -> (e k) n")).then_inc(s["w_got"][b], 16)

        @block.scalar
        def _(act):
            def rows(g, b):
                kit.hold(act, s["t_done"], g + BUF + 1)
                act.activation(xt[0:D, b], ps_x[0:D, b, :], ACT.Copy).then_inc(s["xt_out"], 1)

            def hidden(g, b):
                kit.hold(act, s["h_done"], g + 1)
                act.activation(h[:, b], ps_h[:, b], ACT.Relu).then_inc(s["h_out"], 1)

            def store(g, b):
                kit.hold(act, s["y_out"], g + 3)
                act.dma_start(ys.rearrange("(g t p) d -> g p t d", t=T, p=P)[bass.ds(g, 1), :, :, :].rearrange("g p t d -> (g p) t d"), y[:, b]).then_inc(s["stored"][b], 16)

            rows(0, 0)
            rows(1, 1)
            hidden(0, 0)
            rows(2, 0)
            store(0, 0)
            hidden(1, 1)
            with act.Fori(1, GROUPS // 2 - 1) as i:
                for b in range(2):
                    rows(i * 2 + b + 1, 1 - b)
                    store(i * 2 + b - 1, 1 - b)
                    hidden(i * 2 + b, b)
            rows(GROUPS - 1, 1)
            store(GROUPS - 3, 1)
            hidden(GROUPS - 2, 0)
            store(GROUPS - 2, 0)
            hidden(GROUPS - 1, 1)
            store(GROUPS - 1, 1)
            for b in range(2):
                act.wait_ge(s["stored"][b], 16 * (GROUPS // 2))

        @block.vector
        def _(dve):
            dve.memset(xt[D:D + 1, :, :], 1.0)
            dve.wait_ge(s["w_in"], 16)
            dve.tensor_copy(bias[:], ident[:, D + 1:D + 2].to_broadcast([P, P]))
            dve.drain().then_inc(s["ready"], 1)
            dve.sem_inc(s["t_done"], BUF)
            dve.sem_inc(s["y_done"], BUF)
            dve.sem_inc(s["y_out"], 2)

            def out_rows(g, b):
                kit.hold(dve, s["y_done"], g + BUF + 1)
                dve.tensor_copy(y[:, b], ps_y[:, b, 0:T * D].rearrange("p (t d) -> p t d", t=T)).then_inc(s["y_out"], 1)

            out_rows(0, 0)
            out_rows(1, 1)
            with dve.Fori(1, GROUPS // 2) as i:
                for b in range(2):
                    kit.hold(dve, s["stored"][b], i * 16)
                    out_rows(i * 2 + b, b)

        @block.tensor
        def _(pe):
            pe.wait_ge(s["w_in"], 16)
            pe.wait_ge(s["ready"], 1)
            skip = dict(skip_group_check=True)

            def turn(use, b):
                kit.hold(pe, s["x_in"][b], use * 16 + 16)
                for t in range(T):
                    mm = pe.transpose(ps_x[0:D, b % 2, P * t:P * t + P], x[:, b, t, :], ident[:])
                mm.then_inc(s["t_done"], 1)

            def hidden(g, use, b):
                kit.hold(pe, s["xt_out"], g + 1)
                kit.hold(pe, s["w_got"][b], use * (16 * T) + 16 * T)
                for t in range(T):
                    mm = pe.matmul(ps_h[:, b % 2, P * t:P * t + P], w[0:D + 1, b, t, 0:HID], xt[:, b % 2, P * t:P * t + P], start=True, stop=True)
                mm.then_inc(s["h_done"], 1)

            def down(g, b):
                kit.hold(pe, s["h_out"], g + 1)
                kit.hold(pe, s["y_out"], g + 1)
                pe.matmul(ps_y[:, b % 2, 0:T * D].rearrange("p (t d) -> p t d", t=T), bias[:], w[:, b, :, 0:D], start=True, stop=False, **skip)
                for t in range(T):
                    mm = pe.matmul(ps_y[:, b % 2, D * t:D * t + D], h[:, b % 2, P * t:P * t + P], w[:, b, t, HID:HID + D], start=False, stop=True, **skip)
                mm.then_inc(s["y_done"], 1)

            turn(0, 0)
            turn(0, 1)
            hidden(0, 0, 0)
            with pe.Fori(0, GROUPS // BUF - 1) as i:
                for b in range(BUF):
                    g = i * BUF + b
                    turn(i + (b + 2) // BUF, (b + 2) % BUF)
                    hidden(g + 1, i + (b + 1) // BUF, (b + 1) % BUF)
                    down(g, b)
            last = GROUPS // BUF - 1
            for b in range(BUF):
                g = last * BUF + b
                if b + 2 < BUF:
                    turn(last, b + 2)
                if b + 1 < BUF:
                    hidden(g + 1, last, b + 1)
                down(g, b)


def combine(nc, kit, H, GATE, SLOT, ys, out):
    T = 8
    STEPS = TILES // T
    with ExitStack() as c:
        sb = lambda n, s, d=F32: kit.sb(c, n, s, d)
        sem = lambda n: kit.sem(c, n)
        now = sb("now11", [P, 2, 2, T], U32)
        got = sb("got11", [P, 2, 2, T, D])
        acc = sb("acc11", [P, 2, 2, T, D])
        picked = kit.indirect["fetched"]
        free, ready = sem("free11"), sem("ready11")
        stored = [sem("stored11_0"), sem("stored11_1")]
        block = kit.block(c, last=True)

        @block.gpsimd
        def _(pool):
            with pool.Fori(0, STEPS // 2) as i:
                for b in range(2):
                    kit.hold(pool, free, i * 2 + b + 1)
                    pool.tensor_copy(now[:, b], SLOT[:, :, bass.ds((i * 2 + b) * T, T)])
                    pool.drain()
                    for t in range(T):
                        for j in range(2):
                            pool.indirect_dma_start(got[:, b, j, t, :], None, ys,
                                                    bass.IndirectOffsetOnAxis(ap=now[:, b, j, t:t + 1], axis=0)).then_inc(picked[b], 16)

        @block.vector
        def _(dve):
            dve.sem_inc(free, 2)
            dve.sem_inc(stored[0], 16)
            dve.sem_inc(stored[1], 16)
            with dve.Fori(0, STEPS // 2) as i:
                for b in range(2):
                    n = i * 2 + b
                    here = bass.ds(n * T, T)
                    kit.hold(dve, picked[b], (i + 1) * (32 * T))
                    kit.hold(dve, stored[b], i * 16 + 16)
                    dve.tensor_tensor(acc[:, b, 0], got[:, b, 0], bcast(GATE[:, 0, here], D), ALU.mult)
                    dve.tensor_tensor(acc[:, b, 1], got[:, b, 1], bcast(GATE[:, 1, here], D), ALU.mult).then_inc(free, 1)
                    dve.drain()
                    dve.tensor_tensor(acc[:, b, 0], acc[:, b, 0], acc[:, b, 1], ALU.add)
                    dve.drain()
                    dve.tensor_tensor(acc[:, b, 0], acc[:, b, 0], H[:, here, :], ALU.add).then_inc(ready, 1)

        @block.sync
        def _(sp):
            o = out.rearrange("s (two p) d -> p (s two) d", p=P)
            with sp.Fori(0, STEPS // 2) as i:
                for b in range(2):
                    n = i * 2 + b
                    kit.hold(sp, ready, n + 1)
                    sp.dma_start(o[:, bass.ds(n * T, T), :], acc[:, b, 0]).then_inc(stored[b], 16)
            for b in range(2):
                sp.wait_ge(stored[b], 16 * (STEPS // 2 + 1))


def build(nc, a, out):
    h1 = nc.dram_tensor("h1", (SEQ, LEN, D), F32).ap()
    with ExitStack() as top:
        kit = Kit(nc, top)
        with ExitStack() as c:
            H = kit.sb(c, "H_rows", [P, TILES, D])
            YT = kit.sb(c, "YT", [P, TILES // 2, P])
            LOGITS = kit.sb(c, "LOGITS", [P, 4, SEQ])
            MIX = kit.sb(c, "MIX", [P, 8, P])
            embed_and_logits(nc, kit, a, H, YT, LOGITS)
            row_softmax(nc, kit, a, LOGITS, MIX)
            row_attention_out(nc, kit, a, H, YT, MIX, h1)
        H = kit.sb(top, "H", [P, TILES, D])
        with ExitStack() as c:
            X2 = kit.sb(c, "X2", [P, TILES, D])
            causal_attention(nc, kit, a, h1, H, X2)
            dense_experts(nc, kit, a, H, X2)
        bc_dram = nc.dram_tensor("bc_dram", (2, 64, SEQ * LEN), F32).ap()
        mamba(nc, kit, a, H, bc_dram)
        sparse_experts(nc, kit, a, H, out)


def kernel(**inputs):
    import numpy as np
    import concourse.bacc as _bacc
    from concourse.bass_utils import run_bass_kernel_spmd as _run

    w = {k: np.ascontiguousarray(v) for k, v in inputs.items()}
    f32 = np.float32
    feed = {"x": w["x"], "emb2": w["L0_tok_emb_2"], "emb3": w["L0_tok_emb_3"], "emb4": w["L0_tok_emb_4"],
            "ident": np.eye(128, dtype=f32)}
    wqk = np.zeros((2, 64, 2, 4, 2, 2, 32), f32)
    for k, name in enumerate(("Wq", "Wk")):
        wh = w["L0_attn_" + name].reshape(64, 4, 2, 32)
        for j in range(2):
            wqk[j, :, k, :, :, j, :] = wh
    feed["attn_wqk"] = wqk.reshape(128, 8, 128)
    feed["attn_gb"] = np.tile(np.stack([w["L0_attn_gamma"], w["L0_attn_beta"]], 1), (2, 1))
    wvg = np.zeros((2, 64, 2, 512), f32)
    for j in range(2):
        wvg[j, :, j] = np.concatenate([w["L0_attn_Wv"], w["L0_attn_Wg"]], 1)
    feed["attn_wvg"] = wvg.reshape(128, 2, 512)
    feed["attn_wo"] = w["L0_attn_Wo"].reshape(2, 128, 64).transpose(1, 0, 2)
    feed["attn_bg"] = w["L0_attn_bg"].reshape(1, 256)
    feed["attn_bo"] = w["L0_attn_bo"].reshape(1, 64)
    def heads(wt, kv):
        o = np.zeros((2, 64, 4, 32), f32)
        for h in range(4):
            rows = wt[(h // 2 if kv else h) * 16:][:16]
            o[0, :, h, :16] = rows.T
            o[1, :, h, :8], o[1, :, h, 8:16] = rows[8:].T, rows[:8].T
        return o.reshape(2, 64, 128)
    wq, wk = heads(w["L0_ffn_wq"], False), heads(w["L0_ffn_wk"], True)
    wv = np.repeat(w["L0_ffn_wv"].reshape(2, 16, 64), 2, axis=0).reshape(64, 64).T
    feed["ffn_wqkv"] = np.concatenate([wq[0], wq[1], wk[0], wk[1], wv], 1)
    feed["ffn_wo"] = w["L0_ffn_wo"].T
    feed["ffn_ln1"] = w["L0_ffn_ln1_w"].reshape(64, 1)
    feed["ffn_ln2"] = np.tile(w["L0_ffn_ln2_w"].reshape(64, 1), (2, 1))
    freq = 1.0 / 10000.0 ** (np.arange(0, 16, 2, dtype=f32) / 16)
    ang = np.outer(np.arange(256, dtype=f32), freq).astype(f32)
    rope = np.zeros((4, 32, 2, 256), f32)
    rope[:, :8, 0] = rope[:, 8:16, 0] = np.cos(ang).T
    rope[:, :8, 1], rope[:, 8:16, 1] = -np.sin(ang).T, np.sin(ang).T
    feed["rope"] = rope.reshape(128, 2, 256)
    feed["causal"] = np.where(np.tril(np.ones((128, 128), bool)), 0.0, NEG).astype(f32)
    feed["moe0_w1"] = np.tile(w["L0_ffn_w1"].reshape(1360, 64).T, (2, 1))
    feed["moe0_w3"] = np.tile(w["L0_ffn_w3"].reshape(1360, 64).T, (2, 1))
    w2 = np.zeros((11 * 128, 64), f32)
    w2[:1360] = w["L0_ffn_w2"].transpose(0, 2, 1).reshape(1360, 64)
    feed["moe0_w2"] = w2.reshape(11, 128, 64).transpose(1, 0, 2)
    feed["moe0_wr"] = w["L0_ffn_router_w"].T
    feed["moe0_spread"] = np.tile(np.repeat(np.eye(8, dtype=f32), 170, axis=1), (3, 1))
    feed["mb_win"], feed["mb_wx"] = w["L1_attn_W_in"], w["L1_attn_W_x"]
    feed["mb_wdt"], feed["mb_wout"] = w["L1_attn_W_dt"], w["L1_attn_W_out"]
    feed["mb_chan"] = np.concatenate([w["L1_attn_conv_k"].T, np.stack([w["L1_attn_conv_b"], w["L1_attn_b_dt"], w["L1_attn_D_param"]], 1)], 1)
    feed["mb_alog"] = w["L1_attn_A_log"]
    feed["before"] = np.triu(np.ones((64, 64), f32), 1)
    feed["moe1_wr"] = np.concatenate([w["L1_ffn_Wr"], w["L1_ffn_br"][None]], 0)
    moe1 = np.zeros((64, 128, 192), f32)
    moe1[:, :64, :128], moe1[:, 64, :128] = w["L1_ffn_W1"], w["L1_ffn_b1"]
    moe1[:, 65, :64], moe1[:, :, 128:] = w["L1_ffn_b2"], w["L1_ffn_W2"]
    feed["moe1_w"] = moe1
    feed["prior"] = np.triu(np.ones((128, 128), f32), 1)

    nc = _bacc.Bacc("TRN2", target_bir_lowering=False, num_devices=1)
    arrays, aps = {}, {}
    for name, v in feed.items():
        v = np.ascontiguousarray(v)
        arrays["in_" + name] = v
        aps[name] = nc.dram_tensor("in_" + name, v.shape, mybir.dt.from_np(v.dtype), kind="ExternalInput").ap()
    out = nc.dram_tensor("out_0", (SEQ, LEN, D), F32, kind="ExternalOutput").ap()
    build(nc, aps, out)
    r = _run(nc, [arrays], core_ids=[0])
    return r.results[0]["out_0"]
```
